# Optimizing a Trainium2 kernel written in Bass

```python
import numpy as np
import jax
import jax.numpy as jnp

def _softmax(x, axis=-1):
    return jax.nn.softmax(x, axis=axis)

def _gelu(x):
    return jax.nn.gelu(x, approximate=True)

def _silu(x):
    return jax.nn.silu(x)

def _sigmoid(x):
    return jax.nn.sigmoid(x)

def _layernorm(x, axis=-1, eps=1e-05):
    m = jnp.mean(x, axis=axis, keepdims=True)
    v = jnp.var(x, axis=axis, keepdims=True)
    return (x - m) / jnp.sqrt(v + eps)

def _scatter_add(tgt, idx, src, axis=0):
    return tgt.at[idx].add(src)

def _segment_sum(src, seg, n):
    return jax.ops.segment_sum(src, seg, n)
kernel_name = 'mk_gnn_preln_d2_gnn_r8_50b163'

def setup_inputs(seed: int=0):
    np.random.seed(seed)
    _w = jnp.asarray

    def _rec_inputs():
        import jax
        import jax.numpy as jnp
        _gk = jax.random.key(seed)
        x = -0.0001006 + 1 * jax.random.normal(jax.random.fold_in(_gk, 1), (12500, 96), jnp.float32)
        _s = jax.random.randint(jax.random.fold_in(_gk, 2), (200000,), 0, 12500, jnp.int32)
        _d = jax.random.randint(jax.random.fold_in(_gk, 3), (200000,), 0, 12500, jnp.int32)
        _loop = jnp.arange(12500, dtype=jnp.int32)
        src = jnp.concatenate([_s, _d, _loop])
        dst = jnp.concatenate([_d, _s, _loop])
        _o = jnp.argsort(dst, stable=True)
        src = src[_o]
        dst = dst[_o]
        edge_attr_4 = 0.000714719 + 1.00021 * jax.random.normal(jax.random.fold_in(_gk, 11), (412500, 4), jnp.float32)
        return (x, src, dst, edge_attr_4)
    x, src, dst, edge_attr_4 = _rec_inputs()

    def _L0_gnn_setup():
        import jax, jax.numpy as jnp
        import numpy as np
        EPS = 1e-05

        def _mlp(h, W, b, gamma, beta):
            h = jax.nn.relu(h @ W + b)
            mu = jnp.mean(h, axis=0)
            var = jnp.mean(jnp.square(h - mu), axis=0)
            return gamma * (h - mu) * jax.lax.rsqrt(var + EPS) + beta
        key = jax.random.key(seed)
        ks = jax.random.split(key, 10)
        N, E, C_in, C_out, E_dim = (6250, 100000, 96, 96, 4)
        x = jax.random.normal(ks[0], (N, C_in), dtype=jnp.float32)
        edge_index = jax.random.randint(ks[1], (2, E), 0, N, dtype=jnp.int64)
        edge_attr = jax.random.normal(ks[2], (E, E_dim), dtype=jnp.float32)
        s = lambda fan_in: 1.0 / np.sqrt(fan_in)
        W_node = jax.random.uniform(ks[3], (C_in, C_out), jnp.float32, -s(C_in), s(C_in))
        b_node = jnp.zeros((C_out,), jnp.float32)
        g_node = jnp.ones((C_out,), jnp.float32)
        beta_node = jnp.zeros((C_out,), jnp.float32)
        W_edge = jax.random.uniform(ks[4], (E_dim, C_out), jnp.float32, -s(E_dim), s(E_dim))
        b_edge = jnp.zeros((C_out,), jnp.float32)
        g_edge = jnp.ones((C_out,), jnp.float32)
        beta_edge = jnp.zeros((C_out,), jnp.float32)
        M_in = 2 * C_in + C_out
        W_msg = jax.random.uniform(ks[5], (M_in, C_out), jnp.float32, -s(M_in), s(M_in))
        b_msg = jnp.zeros((C_out,), jnp.float32)
        g_msg = jnp.ones((C_out,), jnp.float32)
        beta_msg = jnp.zeros((C_out,), jnp.float32)
        return dict(x=x, edge_index=edge_index, edge_attr=edge_attr, W_node=W_node, b_node=b_node, g_node=g_node, beta_node=beta_node, W_edge=W_edge, b_edge=b_edge, g_edge=g_edge, beta_edge=beta_edge, W_msg=W_msg, b_msg=b_msg, g_msg=g_msg, beta_msg=beta_msg)
    _L0_gnn_all = _L0_gnn_setup()
    _L0_gnn_in = {k: v for k, v in _L0_gnn_all.items() if k in ('W_node', 'b_node', 'g_node', 'beta_node', 'W_edge', 'b_edge', 'g_edge', 'beta_edge', 'W_msg', 'b_msg', 'g_msg', 'beta_msg')}
    del _L0_gnn_all

    def _L1_gnn_setup():
        import jax, jax.numpy as jnp
        import numpy as np
        N_NODES = 6250
        N_EDGES = 100000
        C = 96
        HID = 32

        def _gcn_conv(x, W, edge_index, n_nodes):
            src, dst = (edge_index[0], edge_index[1])
            loop = jnp.arange(n_nodes, dtype=src.dtype)
            src = jnp.concatenate([src, loop])
            dst = jnp.concatenate([dst, loop])
            deg = jax.ops.segment_sum(jnp.ones_like(dst, dtype=x.dtype), dst, num_segments=n_nodes)
            dinv = jnp.where(deg > 0, jax.lax.rsqrt(deg), 0.0)
            norm = dinv[src] * dinv[dst]
            h = x @ W
            msg = h[src] * norm[:, None]
            return jax.ops.segment_sum(msg, dst, num_segments=n_nodes)
        key = jax.random.key(seed)
        ks = jax.random.split(key, 7)
        x = jax.random.normal(ks[0], (N_NODES, C), dtype=jnp.float32)
        edge_index = jax.random.randint(ks[1], (2, N_EDGES), 0, N_NODES, dtype=jnp.int64)
        W_gcn = jax.random.normal(ks[2], (C, 3 * C), dtype=jnp.float32) / np.sqrt(C)
        W1 = jax.random.normal(ks[3], (3 * C, HID), dtype=jnp.float32) / np.sqrt(3 * C)
        b1 = jnp.zeros((HID,), dtype=jnp.float32)
        W2 = jax.random.normal(ks[4], (HID, C), dtype=jnp.float32) / np.sqrt(HID)
        b2 = jnp.zeros((C,), dtype=jnp.float32)
        return {'x': x, 'W_gcn': W_gcn, 'W1': W1, 'b1': b1, 'W2': W2, 'b2': b2, 'edge_index': edge_index}
    _L1_gnn_all = _L1_gnn_setup()
    _L1_gnn_in = {k: v for k, v in _L1_gnn_all.items() if k in ('W_gcn', 'W1', 'b1', 'W2', 'b2')}
    del _L1_gnn_all
    return {'x': x, 'src': src, 'dst': dst, 'edge_attr_4': edge_attr_4, 'L0_gnn_W_node': _L0_gnn_in['W_node'], 'L0_gnn_b_node': _L0_gnn_in['b_node'], 'L0_gnn_g_node': _L0_gnn_in['g_node'], 'L0_gnn_beta_node': _L0_gnn_in['beta_node'], 'L0_gnn_W_edge': _L0_gnn_in['W_edge'], 'L0_gnn_b_edge': _L0_gnn_in['b_edge'], 'L0_gnn_g_edge': _L0_gnn_in['g_edge'], 'L0_gnn_beta_edge': _L0_gnn_in['beta_edge'], 'L0_gnn_W_msg': _L0_gnn_in['W_msg'], 'L0_gnn_b_msg': _L0_gnn_in['b_msg'], 'L0_gnn_g_msg': _L0_gnn_in['g_msg'], 'L0_gnn_beta_msg': _L0_gnn_in['beta_msg'], 'L1_gnn_W_gcn': _L1_gnn_in['W_gcn'], 'L1_gnn_W1': _L1_gnn_in['W1'], 'L1_gnn_b1': _L1_gnn_in['b1'], 'L1_gnn_W2': _L1_gnn_in['W2'], 'L1_gnn_b2': _L1_gnn_in['b2']}

def reference(x, src, dst, edge_attr_4, L0_gnn_W_node, L0_gnn_b_node, L0_gnn_g_node, L0_gnn_beta_node, L0_gnn_W_edge, L0_gnn_b_edge, L0_gnn_g_edge, L0_gnn_beta_edge, L0_gnn_W_msg, L0_gnn_b_msg, L0_gnn_g_msg, L0_gnn_beta_msg, L1_gnn_W_gcn, L1_gnn_W1, L1_gnn_b1, L1_gnn_W2, L1_gnn_b2):
    import jax
    import jax.numpy as jnp

    def _L0_gnn_ref(x, edge_index, edge_attr, W_node, b_node, g_node, beta_node, W_edge, b_edge, g_edge, beta_edge, W_msg, b_msg, g_msg, beta_msg):
        import jax, jax.numpy as jnp
        import numpy as np
        EPS = 1e-05

        def _mlp(h, W, b, gamma, beta):
            h = jax.nn.relu(h @ W + b)
            mu = jnp.mean(h, axis=0)
            var = jnp.mean(jnp.square(h - mu), axis=0)
            return gamma * (h - mu) * jax.lax.rsqrt(var + EPS) + beta
        node_feat = _mlp(x, W_node, b_node, g_node, beta_node)
        edge_feat = _mlp(edge_attr, W_edge, b_edge, g_edge, beta_edge)
        row, col = (edge_index[0], edge_index[1])
        message = jnp.concatenate([x[row], x[col], edge_feat], axis=1)
        message = _mlp(message, W_msg, b_msg, g_msg, beta_msg)
        agg = jax.ops.segment_sum(message, col, num_segments=node_feat.shape[0])
        return agg + node_feat

    def _L1_gnn_ref(x, W_gcn, W1, b1, W2, b2, edge_index):
        import jax, jax.numpy as jnp
        import numpy as np
        N_NODES = 6250
        N_EDGES = 100000
        C = 96
        HID = 32

        def _gcn_conv(x, W, edge_index, n_nodes):
            src, dst = (edge_index[0], edge_index[1])
            loop = jnp.arange(n_nodes, dtype=src.dtype)
            src = jnp.concatenate([src, loop])
            dst = jnp.concatenate([dst, loop])
            deg = jax.ops.segment_sum(jnp.ones_like(dst, dtype=x.dtype), dst, num_segments=n_nodes)
            dinv = jnp.where(deg > 0, jax.lax.rsqrt(deg), 0.0)
            norm = dinv[src] * dinv[dst]
            h = x @ W
            msg = h[src] * norm[:, None]
            return jax.ops.segment_sum(msg, dst, num_segments=n_nodes)
        n_nodes = x.shape[0]
        features = _gcn_conv(x, W_gcn, edge_index, n_nodes)
        update = jax.nn.relu(features @ W1 + b1) @ W2 + b2
        return x + update
    edge_index = jnp.stack([src, dst])
    h = jnp.maximum(_layernorm(x, axis=-1), 0.0)
    x = x + _L0_gnn_ref(h, edge_index, edge_attr_4, L0_gnn_W_node, L0_gnn_b_node, L0_gnn_g_node, L0_gnn_beta_node, L0_gnn_W_edge, L0_gnn_b_edge, L0_gnn_g_edge, L0_gnn_beta_edge, L0_gnn_W_msg, L0_gnn_b_msg, L0_gnn_g_msg, L0_gnn_beta_msg)
    h = jnp.maximum(_layernorm(x, axis=-1), 0.0)
    x = x + _L1_gnn_ref(h, L1_gnn_W_gcn, L1_gnn_W1, L1_gnn_b1, L1_gnn_W2, L1_gnn_b2, edge_index)
    return x

_drawn_inputs = setup_inputs


def setup_inputs(seed=0):
    import zlib

    import numpy as np

    out = dict(_drawn_inputs(seed))
    spreads = {'L0_gnn_b_node': (0.0, 0.711),
     'L0_gnn_g_node': (1.0, 0.6),
     'L0_gnn_beta_node': (0.0, 0.8),
     'L0_gnn_b_edge': (0.0, 0.1),
     'L0_gnn_g_edge': (1.0, 0.2),
     'L0_gnn_beta_edge': (0.0, 0.274),
     'L0_gnn_b_msg': (0.0, 0.1),
     'L0_gnn_g_msg': (1.0, 0.2),
     'L0_gnn_beta_msg': (0.0, 0.1),
     'L1_gnn_b1': (0.0, 0.8),
     'L1_gnn_b2': (0.0, 0.8)}
    factors = {'L1_gnn_W_gcn': 3.392, 'L1_gnn_W1': 4.523, 'L1_gnn_W2': 2.795}
    for name, (base, spread) in spreads.items():
        noise = np.random.default_rng([zlib.crc32(name.encode()), seed]).standard_normal(out[name].shape)
        drawn = base * np.exp(spread * noise) if base else spread * noise
        out[name] = jnp.asarray(drawn.astype(out[name].dtype))
    for name, factor in factors.items():
        out[name] = (out[name] * factor).astype(out[name].dtype)
    return out
```

```python
import concourse.bass as bass
from concourse import mybir
from contextlib import ExitStack

FP32 = mybir.dt.float32
BF16 = mybir.dt.bfloat16
I32 = mybir.dt.int32
ALU = mybir.AluOpType
ACT = mybir.ActivationFunctionType
AX = mybir.AxisListType.X
RMAX = bass.bass_isa.ReduceOp.max
RADD = bass.bass_isa.ReduceOp.add

C = 96
KE = 4
H = 32
P = 128
TILE = 128
SUP = 4
ES = TILE * SUP
W = P - C
CH = 512
CT = CH // P
PARTS = 3
KR = PARTS * PARTS * KE
EPS = 1e-5
GROUP = 8
NEG = -1e30


class Dims:

    def __init__(self, n, e):
        self.N, self.E = n, e
        self.NCH = -(-(n + W) // CH)
        self.NP = self.NCH * CH
        self.NT = self.NP // P
        self.S = -(-e // (ES * GROUP)) * GROUP
        self.EP = self.S * ES
        self.T = self.S * SUP


class Signal:

    def __init__(self, handle, ahead):
        self.sem, self.ahead = handle, ahead

    def start(self, engine):
        engine.sem_inc(self.sem, self.ahead)

    def at(self, item):
        return item + (1 + self.ahead)


def gnn_kernel(nc, d, a, out):
    N, E, NP, NT, NCH, S, EP, T = d.N, d.E, d.NP, d.NT, d.NCH, d.S, d.EP, d.T
    ctx = ExitStack()
    with ctx:
        ctx.enter_context(nc.allow_non_contiguous_dma(reason="short rows of node tables and parameters"))

        def sb(name, shape, dt=FP32):
            return ctx.enter_context(nc.sbuf_tensor(name, shape, dt))

        def sem(name):
            return ctx.enter_context(nc.semaphore(name))

        def signal(name, ahead):
            return Signal(ctx.enter_context(nc.semaphore(name)), ahead)

        pool_turn = sem("pool_turn")
        sp_turn = sem("sp_turn")

        def dram(name, shape, dt=FP32):
            return nc.dram_tensor(name, shape, dt, kind="Internal").ap()

        attr_parts = dram("attr_parts", (PARTS, KE, EP), BF16)
        w_parts = dram("w_parts", (PARTS, KE, C), BF16)
        a_tab = dram("a_tab", (NP, C))
        b_tab = dram("b_tab", (NP, C))
        t_tab = dram("t_tab", (NP, C))
        cnt_row = dram("cnt_row", (1, NP))
        s_tab = dram("s_tab", (NP + P, C + 1))

        x_all = sb("x_all", [P, NT, C])
        sT = sb("sT", [P, max(NP, (NT + 1) * (C + 1), 6 * KE * EP // P // 8, 6 * S)])
        nf = sb("nf", [P, max(NP, T + NT * C, GROUP * ES)])
        src_i = sb("src_i", [P, T], I32)
        dstrel = sb("dstrel", [P, S, SUP])
        winid = sb("winid", [P, S])
        base_i = sb("base_i", [1, S], I32)
        ident = sb("ident", [P, P])
        iota_w = sb("iota_w", [P, W])
        pcol = sb("pcol", [P, 1])
        ones = sb("ones", [P, P])
        flag_f = sb("flag_f", [P, 4])
        flag_i = sb("flag_i", [1, 1], I32)
        negrow = sb("negrow", [1, C])
        zrow = sb("zrow", [1, C])
        w36 = sb("w36", [KR, C], BF16)
        wnode = sb("wnode", [C, C])
        wab = sb("wab", [C, 2 * C])
        w3 = sb("w3", [C, C])
        bm_row = sb("bm_row", [1, C])
        par = sb("par", [C, 8])
        B_NODE, G_NODE, T_NODE, B_EDGE, G_EDGE, T_EDGE, G_MSG, T_MSG = range(8)
        eps = sb("eps", [P, 1])
        cstb = sb("cstb", [P, C])
        aff = sb("aff", [C, 16])
        S_E, T_E, S_N, T_N, S_M, T_M, TMP0, TMP1, TMP2, TMP3 = range(10)
        rstd = sb("rstd", [P, NT])
        mean = sb("mean", [P, NT])
        nstat = sb("nstat", [C, NCH, 6])
        agg2 = sb("agg2", [C, 4])
        dinv = sb("dinv", [P, NT])
        smc = sb("smc", [C + 1, 1])
        wgT = sb("wgT", [C, 3, C])
        w1 = sb("w1", [C, 3, H])
        w2 = sb("w2", [H + 1, C])
        wc = sb("wc", [C, H])
        b1c = sb("b1c", [H, 1])
        trep = sb("trep", [C, P])
        gbuf = sb("gbuf", [P, 4, SUP, C])
        idxb = sb("idxb", [P, 4, SUP], I32)
        lhs = sb("lhs", [P, 2, ES])
        rhs = sb("rhs", [P, 2, C])
        pre = sb("pre", [P, 2, SUP, C])
        msg = sb("msg", [P, 2, SUP, C + 1])
        sq = sb("sq", [P, 2, SUP, C])
        acc = sb("acc", [P, SUP, C])
        oh = sb("oh", [P, 4, SUP, W])
        psum = ctx.enter_context(nc.psum_tensor("psum", [P, 8 * 512], FP32))
        bank = [psum[:, i * 512:(i + 1) * 512] for i in range(8)]

        x_flat = x_all[:, :, :].rearrange("p t c -> p (t c)")
        rk = x_flat[0:KR, 0:2 * ES].bitcast(BF16).rearrange("p (b s e) -> p b s e", b=2, e=ES)
        dstbc = x_flat[:, 2 * ES:6 * ES].bitcast(I32).rearrange("p (b s e) -> p b s e", b=2, e=ES)
        dst_i = nf[:, 0:T].bitcast(I32)
        sum_sq = nf[:, T:T + NT * C].rearrange("p (t c) -> p t c", c=C)
        NPC = 8
        AC = KE * EP // P // NPC
        araw = sT[:, 0:2 * AC].rearrange("p (b f) -> p b f", b=2)
        ares = sT[:, 2 * AC:3 * AC]
        apart = sT[:, 3 * AC:6 * AC].bitcast(BF16).rearrange("p (b i f) -> p b i f", b=2, i=PARTS)
        attr_in = a["attr"].rearrange("k e -> (k e)").rearrange("(p q f) -> q p f", p=P, q=NPC)
        attr_out = [attr_parts[j].rearrange("k e -> (k e)").rearrange("(p q f) -> q p f", p=P, q=NPC)
                    for j in range(PARTS)]

        l_par = sem("l_par")
        l_dst = sem("l_dst")
        l_src = sem("l_src")
        l_x = sem("l_x")
        l_attr = [sem("l_attr0"), sem("l_attr1")]
        l_we = sem("l_we")
        o_wp = sem("o_wp")
        l_w36 = sem("l_w36")
        o_attr = [sem("o_attr0"), sem("o_attr1")]
        split_done = sem("split_done")
        c_pool = sem("c_pool")
        v = sem("v")
        base_f_ok = sem("base_f_ok")
        base_mm = sem("base_mm")
        viol_ok = sem("viol_ok")
        viol_all = sem("viol_all")
        centred = sem("centred")
        squared = sem("squared")
        var_ok = sem("var_ok")
        std_ok = sem("std_ok")
        we_ok = sem("we_ok")

        base_f = lhs[0:1, :, :].rearrange("p a b -> p (a b)")[:, 0:S]
        we_f = trep[0:KE, 0:C]
        we_r = cstb[0:KE, 0:C]
        we_p = acc[0:KE, 0:2, :].rearrange("p a b -> p (a b)").bitcast(BF16)[:, 0:PARTS * C].rearrange("p (i c) -> p i c", i=PARTS)
        SH = S // 2

        with nc.Block() as block:
            @block.sync
            def _(sp):
                sp.dma_start(dst_i[:, :], a["dst"]).then_inc(l_dst, 16)
                sp.dma_start(we_f, a["W_edge"]).then_inc(l_we, 16)
                sp.dma_start(x_all[:, :, :], a["x"]).then_inc(l_x, 16)
                sp.dma_start(src_i[:, :], a["src"]).then_inc(l_src, 16)
                sp.dma_start(wnode[:, :], a["W_node"]).then_inc(l_par, 16)
                sp.dma_start(wab[:, 0:C], a["W_msg"][0:C, :]).then_inc(l_par, 16)
                sp.dma_start(wab[:, C:2 * C], a["W_msg"][C:2 * C, :]).then_inc(l_par, 16)
                sp.dma_start(w3[:, :], a["W_msg"][2 * C:3 * C, :]).then_inc(l_par, 16)
                sp.dma_start(bm_row[:, :], a["b_msg"]).then_inc(l_par, 16)
                for j, name in enumerate(("b_node", "g_node", "beta_node", "b_edge", "g_edge", "beta_edge", "g_msg", "beta_msg")):
                    sp.dma_start(par[:, j:j + 1], a[name].rearrange("a c -> c a")).then_inc(l_par, 16)
                sp.wait_ge(we_ok, 3)
                sp.dma_start(w_parts.rearrange("i k c -> k i c"), we_p).then_inc(o_wp, 16)
                sp.wait_ge(o_wp, 16)
                for j in range(PARTS):
                    for i in range(PARTS):
                        r = (j * PARTS + i) * KE
                        sp.dma_start(w36[r:r + KE, :], w_parts[j]).then_inc(l_w36, 16)
                sp.wait_ge(l_w36, 16 * PARTS * PARTS)
                sp.wait_ge(l_par, 16 * 13)
                sp.wait_ge(l_src, 16)

            @block.scalar
            def _(act):
                for i in range(2):
                    act.dma_start(araw[:, i, :], attr_in[i]).then_inc(l_attr[i], 16)
                for i in range(NPC):
                    act.wait_ge(split_done, i + 1)
                    for j in range(PARTS):
                        act.dma_start(attr_out[j][i], apart[:, i % 2, j, :]).then_inc(o_attr[i % 2], 16)
                    if i + 2 < NPC:
                        act.dma_start(araw[:, i % 2, :], attr_in[i + 2]).then_inc(l_attr[i % 2], 16)
                act.wait_ge(centred, 1)
                act.activation(sum_sq, x_all[:, :, :], ACT.Square).then_inc(squared, 1)
                act.wait_ge(var_ok, 1)
                act.activation(rstd[:, :], rstd[:, :], ACT.Sqrt, bias=eps[:, :], scale=1.0 / C).then_inc(std_ok, 1)
                for b in range(2):
                    act.wait_ge(o_attr[b], NPC // 2 * 16 * PARTS)

            @block.gpsimd
            def _(g):
                g.memset(ident[:, :], 0.0).then_inc(c_pool, 1)
                g.memset(ones[:, :], 1.0).then_inc(c_pool, 1)
                g.wait_ge(c_pool, 2)
                g.affine_select(out=ident[:, :], in_=ident[:, :], compare_op=ALU.not_equal, fill=1.0,
                                base=0, pattern=[[-1, P]], channel_multiplier=1).then_inc(c_pool, 1)
                g.iota(iota_w[:, :], [[1, W]], base=0, channel_multiplier=0,
                       allow_small_or_imprecise_dtypes=True).then_inc(c_pool, 1)
                g.iota(pcol[:, :], [[0, 1]], base=-C, channel_multiplier=1,
                       allow_small_or_imprecise_dtypes=True).then_inc(c_pool, 1)
                g.memset(negrow[:, :], NEG).then_inc(c_pool, 1)
                g.memset(zrow[:, :], 0.0).then_inc(c_pool, 1)
                g.memset(eps[:, :], EPS).then_inc(c_pool, 1)
                g.memset(msg[:, :, :, C:C + 1], 1.0).then_inc(c_pool, 1)
                g.memset(acc[:, 2:SUP, :], 0.0).then_inc(c_pool, 1)
                g.wait_ge(viol_ok, 2)
                g.partition_all_reduce(flag_f[:, 2:4], flag_f[:, 0:2], P, RMAX).then_inc(viol_all, 1)

            @block.tensor
            def _(pe):
                pe.wait_ge(c_pool, 10)
                pe.wait_ge(base_f_ok, 1)
                for h in range(2):
                    pe.matmul(bank[h][:, 0:SH], ones[0:1, :], base_f[:, h * SH:(h + 1) * SH],
                              start=True, stop=True).then_inc(base_mm, 1)

            @block.vector
            def _(dve):
                steps = [0]

                def link(ins):
                    steps[0] += 1
                    ins.then_inc(v, 1)
                    dve.wait_ge(v, steps[0])

                dve.wait_ge(l_we, 16)
                dve.wait_ge(c_pool, 10)
                dve.tensor_copy(we_p[:, 0, :], we_f).then_inc(we_ok, 1)
                dve.wait_ge(we_ok, 1)
                link(dve.tensor_tensor(we_r, we_f, we_p[:, 0, :], ALU.subtract))
                dve.tensor_copy(we_p[:, 1, :], we_r).then_inc(we_ok, 1)
                dve.wait_ge(we_ok, 2)
                link(dve.tensor_tensor(we_r, we_r, we_p[:, 1, :], ALU.subtract))
                dve.tensor_copy(we_p[:, 2, :], we_r).then_inc(we_ok, 1)
                dve.wait_ge(l_dst, 16)
                dst3 = dst_i.rearrange("p (s t) -> p s t", t=SUP)
                dve.tensor_copy(base_f, dst3[0:1, :, 0]).then_inc(base_f_ok, 1)
                link(dve.tensor_copy(base_i[:, :], dst3[0:1, :, 0]))
                for h in range(2):
                    dve.wait_ge(base_mm, h + 1)
                    s = slice(h * SH, (h + 1) * SH)
                    link(dve.tensor_scalar(winid[:, s], bank[h][:, 0:SH], pcol[:, :], None, ALU.add))
                    link(dve.tensor_tensor(dstrel[:, s, :], dst3[:, s, :],
                                           bank[h][:, 0:SH].unsqueeze(2).to_broadcast([P, SH, SUP]), ALU.subtract))
                dflat = dstrel[:, :, :].rearrange("p s t -> p (s t)")
                dve.tensor_reduce(flag_f[:, 0:1], dflat, AX, ALU.max).then_inc(viol_ok, 1)
                dve.tensor_reduce(flag_f[:, 1:2], dflat, AX, ALU.min, negate=True).then_inc(viol_ok, 1)
                dve.wait_ge(l_x, 16)
                link(dve.tensor_reduce(mean[:, :], x_all[:, :, :], AX, ALU.add))
                link(dve.tensor_scalar(mean[:, :], mean[:, :], 1.0 / C, None, ALU.mult))
                dve.tensor_tensor(x_all[:, :, :], x_all[:, :, :], mean[:, :].unsqueeze(2).to_broadcast([P, NT, C]),
                                  ALU.subtract).then_inc(centred, 1)
                dve.wait_ge(viol_all, 1)
                link(dve.tensor_scalar(flag_f[:, 2:3], flag_f[:, 2:3], float(W - 1), None, ALU.is_le))
                link(dve.tensor_scalar(flag_f[:, 3:4], flag_f[:, 3:4], 0.0, None, ALU.is_le))
                link(dve.tensor_tensor(flag_f[:, 0:1], flag_f[:, 2:3], flag_f[:, 3:4], ALU.mult))
                link(dve.tensor_copy(flag_i[:, :], flag_f[0:1, 0:1]))
                for i in range(NPC):
                    b = i % 2
                    dve.wait_ge(l_attr[b], 16 * (i // 2 + 1))
                    if i >= 2:
                        dve.wait_ge(o_attr[b], 16 * PARTS * (i // 2))
                    link(dve.tensor_copy(apart[:, b, 0, :], araw[:, b, :]))
                    link(dve.tensor_tensor(ares, araw[:, b, :], apart[:, b, 0, :], ALU.subtract))
                    link(dve.tensor_copy(apart[:, b, 1, :], ares))
                    link(dve.tensor_tensor(ares, ares, apart[:, b, 1, :], ALU.subtract))
                    dve.tensor_copy(apart[:, b, 2, :], ares).then_inc(split_done, 1)
                    dve.wait_ge(split_done, i + 1)
                dve.wait_ge(squared, 1)
                dve.tensor_reduce(rstd[:, :], sum_sq, AX, ALU.add).then_inc(var_ok, 1)
                dve.wait_ge(std_ok, 1)
                dve.reciprocal(rstd[:, :], rstd[:, :]).then_inc(v, 1)

        HG = GROUP // 2
        ek = nf[0:KR, 0:GROUP * ES // 2].bitcast(BF16).rearrange("p (b s e) -> p b s e", b=2, e=ES)
        er = nf[0:C, GROUP * ES // 2:GROUP * ES // 2 + 4 * ES].rearrange("p (b e) -> p b e", b=2)
        estat = sT[0:C, 0:S * 6].rearrange("p (s k) -> p s k", k=6)
        attr_rows = attr_parts.rearrange("i k e -> (i k) e")
        SV = -(-E // ES)
        ITER = (SV - 1) // GROUP
        e_land = [sem("e_land0"), sem("e_land1")]
        e_mm = signal("e_mm", GROUP)
        e_relu = signal("e_relu", 2)
        e_stat = signal("e_stat", 4)
        e_v = sem("e_v")
        e_std = sem("e_std")
        cst_mm = sem("cst_mm")
        SREST = SV - ITER * GROUP

        with nc.Block() as block:
            def load_rows(sp, i, b):
                sp.wait_ge(e_mm.sem, e_mm.at(i * GROUP + (b + 1) * HG - 1 - GROUP))
                sp.sem_inc(sp_turn, 1)
                for j in range(PARTS):
                    r = j * PARTS * KE
                    sp.dma_start(ek[r:r + PARTS * KE, b, :, :].rearrange("p s e -> p (s e)"),
                                 attr_rows[:, bass.ds((i * GROUP + b * HG) * ES, HG * ES)]).then_inc(e_land[b], 16)

            @block.sync
            def _(sp):
                with sp.Fori(0, ITER) as i:
                    for b in range(2):
                        load_rows(sp, i, b)
                for b in range(2):
                    if b * HG < SREST:
                        load_rows(sp, ITER, b)

            def product(pe, i, k):
                if k % HG == 0:
                    pe.wait_ge(e_land[k // HG], i * (16 * PARTS) + 16 * PARTS)
                if k % 2 == 0:
                    pe.wait_ge(e_relu.sem, e_relu.at(i * (GROUP // 2) + k // 2 - 2))
                pe.matmul(bank[k % 4][0:C, :], w36[:, :], ek[:, k // HG, k % HG, :],
                          start=True, stop=True).then_inc(e_mm.sem, 1)

            @block.tensor
            def _(pe):
                e_mm.start(pe)
                with pe.Fori(0, ITER) as i:
                    for k in range(GROUP):
                        product(pe, i, k)
                for k in range(SREST):
                    product(pe, ITER, k)
                pe.wait_ge(e_v, 6)
                pe.matmul(bank[7][:, 0:C], trep[0:C, :], w3[:, :], start=True, stop=False)
                pe.matmul(bank[7][:, 0:C], ones[0:1, :], bm_row[:, :], start=False, stop=True).then_inc(cst_mm, 1)

            def relu_pair(act, i, k, n):
                act.wait_ge(e_mm.sem, e_mm.at(i * GROUP + k + n - 1))
                act.wait_ge(e_stat.sem, e_stat.at(i * GROUP + k - 3))
                act.activation(er[:, (k // 2) % 2, 0:n * ES], psum[0:C, (k % 4) * ES:(k % 4 + n) * ES], ACT.Relu,
                               bias=par[:, B_EDGE:B_EDGE + 1]).then_inc(e_relu.sem, 1)

            @block.scalar
            def _(act):
                e_relu.start(act)
                with act.Fori(0, ITER) as i:
                    for k in range(0, GROUP, 2):
                        relu_pair(act, i, k, 2)
                for k in range(0, SREST, 2):
                    relu_pair(act, ITER, k, min(2, SREST - k))
                act.wait_ge(e_v, 1)
                act.activation(aff[:, TMP0:TMP0 + 1], agg2[:, 1:2], ACT.Sqrt, bias=eps[0:C, :]).then_inc(e_std, 1)

            def stats(dve, i, k, cols):
                if k % 2 == 0:
                    dve.wait_ge(e_relu.sem, e_relu.at(i * (GROUP // 2) + k // 2))
                dve.bn_stats(estat[:, i * GROUP + k, :],
                             er[:, (k // 2) % 2, (k % 2) * ES:(k % 2) * ES + cols]).then_inc(e_stat.sem, 1)

            @block.vector
            def _(dve):
                e_stat.start(dve)
                with dve.Fori(0, ITER) as i:
                    for k in range(GROUP):
                        stats(dve, i, k, ES)
                for k in range(SREST):
                    stats(dve, ITER, k, min(ES, E - (ITER * GROUP + k) * ES))
                dve.wait_ge(e_stat.sem, e_stat.at(SV - 1))
                dve.bn_aggr(agg2[:, 0:2], sT[0:C, 0:SV * 6]).then_inc(e_v, 1)
                dve.wait_ge(e_std, 1)
                n = [1]

                def link(ins):
                    n[0] += 1
                    ins.then_inc(e_v, 1)
                    dve.wait_ge(e_v, n[0])
                def col(c):
                    return aff[:, c:c + 1]
                link(dve.reciprocal(col(TMP1), col(TMP0)))
                link(dve.tensor_tensor(col(S_E), col(TMP1), par[:, G_EDGE:G_EDGE + 1], ALU.mult))
                link(dve.tensor_tensor(col(TMP2), agg2[:, 0:1], col(S_E), ALU.mult))
                link(dve.tensor_tensor(col(T_E), par[:, T_EDGE:T_EDGE + 1], col(TMP2), ALU.subtract))
                link(dve.tensor_scalar(trep[0:C, :], ones[0:C, :], col(T_E), None, ALU.mult))
                for b in range(2):
                    link(dve.tensor_scalar(rhs[0:C, b, :], w3[:, :], col(S_E), None, ALU.mult))
                dve.wait_ge(cst_mm, 1)
                link(dve.tensor_copy(cstb[:, :], bank[7][:, 0:C]))


        h_sb = pre[:, 0, :, :]
        hT = lhs[0:C, 0, :]
        abuf = sq[:, 0, :, :]
        bbuf = sq[:, 1, :, :]
        ps_a, ps_b = [bank[b][:, 0:CT * C].rearrange("p (k f) -> p k f", k=CT) for b in (4, 5)]
        n_h = signal("n_h", 0)
        n_tr = signal("n_tr", 1)
        n_hT = signal("n_hT", 1)
        n_mlp = signal("n_mlp", 0)
        n_nf = signal("n_nf", 1)
        n_ab = signal("n_ab", 1)
        n_a = signal("n_a", 1)
        n_b = signal("n_b", 1)
        n_out = signal("n_out", 1)
        n_stat = sem("n_stat")
        o_ab = sem("o_ab")
        o_pad = sem("o_pad")
        n_v = sem("n_v")
        n_std = sem("n_std")
        NFULL = N // CH
        a_rows = a_tab.rearrange("(c k p) f -> c p k f", k=CT, p=P)
        b_rows = b_tab.rearrange("(c k p) f -> c p k f", k=CT, p=P)

        with nc.Block() as block:
            def node_dve(dve, c):
                dve.wait_ge(n_tr.sem, n_tr.at(c - 1))
                dve.scalar_tensor_tensor(h_sb, x_all[:, bass.ds(c * CT, CT), :], 0.0,
                                         rstd[:, bass.ds(c * CT, CT)].unsqueeze(2).to_broadcast([P, CT, C]),
                                         ALU.max, ALU.mult).then_inc(n_h.sem, 1)
                dve.wait_ge(n_ab.sem, n_ab.at(c))
                dve.wait_ge(n_out.sem, n_out.at(c - 1))
                dve.tensor_tensor(bbuf, ps_b, cstb[:, :].unsqueeze(1).to_broadcast([P, CT, C]),
                                  ALU.add).then_inc(n_b.sem, 1)

            def node_stats(dve, c, cols):
                dve.wait_ge(n_nf.sem, n_nf.at(c))
                dve.bn_stats(nstat[:, c, :], nf[0:C, bass.ds(c * CH, cols)]).then_inc(n_stat, 1)

            def node_pe(pe, c):
                pe.wait_ge(n_h.sem, n_h.at(c))
                pe.wait_ge(n_hT.sem, n_hT.at(c - 1))
                for k in range(CT):
                    ins = pe.transpose(bank[0][0:C, k * P:(k + 1) * P], h_sb[:, k, :], ident[:, :])
                ins.then_inc(n_tr.sem, 1)
                pe.wait_ge(n_hT.sem, n_hT.at(c))
                pe.wait_ge(n_nf.sem, n_nf.at(c - 1))
                pe.matmul(bank[1][0:C, :], wnode[:, :], hT, start=True, stop=True).then_inc(n_mlp.sem, 1)
                pe.wait_ge(n_a.sem, n_a.at(c - 1))
                pe.wait_ge(n_b.sem, n_b.at(c - 1))
                for k in range(CT):
                    pe.matmul(ps_a[:, k, :], hT[:, k * P:(k + 1) * P], wab[:, 0:C], start=True, stop=True)
                    ins = pe.matmul(ps_b[:, k, :], hT[:, k * P:(k + 1) * P], wab[:, C:2 * C], start=True, stop=True)
                ins.then_inc(n_ab.sem, 1)

            def node_act(act, c):
                act.wait_ge(n_tr.sem, n_tr.at(c))
                act.wait_ge(n_ab.sem, n_ab.at(c - 1))
                act.activation(hT, bank[0][0:C, :], ACT.Copy).then_inc(n_hT.sem, 1)
                act.wait_ge(n_mlp.sem, n_mlp.at(c))
                act.activation(nf[0:C, bass.ds(c * CH, CH)], bank[1][0:C, :], ACT.Relu,
                               bias=par[:, B_NODE:B_NODE + 1]).then_inc(n_nf.sem, 1)
                act.wait_ge(n_ab.sem, n_ab.at(c))
                act.wait_ge(n_out.sem, n_out.at(c - 1))
                act.activation(abuf, ps_a, ACT.Copy).then_inc(n_a.sem, 1)

            @block.vector
            def _(dve):
                n_b.start(dve)
                with dve.Fori(0, NFULL) as c:
                    node_dve(dve, c)
                    node_stats(dve, c, CH)
                for c in range(NFULL, NCH):
                    node_dve(dve, c)
                    if N > c * CH:
                        node_stats(dve, c, min(CH, N - c * CH))
                NSTAT = -(-N // CH)
                dve.wait_ge(n_stat, NSTAT)
                dve.bn_aggr(agg2[:, 2:4], nstat[:, 0:NSTAT, :].rearrange("p c k -> p (c k)")).then_inc(n_v, 1)
                n = [1]

                def link(ins):
                    n[0] += 1
                    ins.then_inc(n_v, 1)
                    dve.wait_ge(n_v, n[0])

                def col(c):
                    return aff[:, c:c + 1]
                dve.wait_ge(n_std, 1)
                link(dve.reciprocal(col(TMP1), col(TMP0)))
                link(dve.tensor_tensor(col(S_N), col(TMP1), par[:, G_NODE:G_NODE + 1], ALU.mult))
                link(dve.tensor_tensor(col(TMP2), agg2[:, 2:3], col(S_N), ALU.mult))
                link(dve.tensor_tensor(col(T_N), par[:, T_NODE:T_NODE + 1], col(TMP2), ALU.subtract))

            @block.tensor
            def _(pe):
                n_tr.start(pe)
                n_ab.start(pe)
                with pe.Fori(0, NCH) as c:
                    node_pe(pe, c)

            @block.scalar
            def _(act):
                n_hT.start(act)
                n_nf.start(act)
                n_a.start(act)
                with act.Fori(0, NCH) as c:
                    node_act(act, c)
                act.wait_ge(n_v, 1)
                act.activation(aff[:, TMP0:TMP0 + 1], agg2[:, 3:4], ACT.Sqrt, bias=eps[0:C, :]).then_inc(n_std, 1)

            @block.sync
            def _(sp):
                n_out.start(sp)
                with sp.Fori(0, NCH) as c:
                    sp.wait_ge(n_a.sem, n_a.at(c))
                    sp.sem_inc(sp_turn, 1)
                    sp.dma_start(a_rows[c], abuf).then_inc(o_ab, 16)
                    sp.wait_ge(n_b.sem, n_b.at(c))
                    sp.sem_inc(sp_turn, 1)
                    sp.dma_start(b_rows[c], bbuf).then_inc(o_ab, 16)
                    sp.wait_ge(o_ab, c * 32 + 32)
                    sp.sem_inc(n_out.sem, 1)
                sp.dma_start(a_tab[N:N + 1, :], negrow[:, :]).then_inc(o_pad, 16)
                sp.wait_ge(o_pad, 16)

        HP = 2
        g_land = [sem(f"g_land{k}") for k in range(4)]
        r_land = [sem(f"r_land{k}") for k in range(2)]
        d_land = [sem(f"d_land{k}") for k in range(2)]
        w_land = [sem(f"w_land{k}") for k in range(2)]
        idx_ok = signal("idx_ok", 0)
        r_mm = signal("r_mm", 4)
        r_ok = signal("r_ok", 2)
        ohT_ok = signal("ohT_ok", 4)
        oh_ok = signal("oh_ok", 0)
        m_mm = signal("m_mm", 2)
        m_pre = signal("m_pre", 4)
        m_ok = signal("m_ok", 2)
        m_sq = signal("m_sq", 2)
        m_acc = signal("m_acc", 2)
        s_mm = signal("s_mm", 4)
        s_add = signal("s_add", 2)
        last_b = S - 1

        def ps_r(k):
            return bank[k % 2][0:C, :]

        def ps_m(k):
            return bank[2 + k % 2][:, 0:SUP * C].rearrange("p (t c) -> p t c", t=SUP)

        def ps_s(k):
            return bank[4 + k % 2][0:C + 1, 0:W]

        def earlier(i, k, n):
            return i + (k - n) // 4, (k - n) % 4

        def absent(i, k):
            return isinstance(i, int) and not 0 <= 4 * i + k < S

        def pipelined(engine, step, lag):
            for k in range(4):
                step(0, k)
            with engine.Fori(1, S // 4) as i:
                for k in range(4):
                    step(i, k)
            for k in range(lag):
                step(S // 4, k)

        def copy_indices(act, i, k):
            if absent(i, k):
                return
            act.wait_ge(m_pre.sem, m_pre.at(4 * i + k - 4))
            act.activation(idxb[:, k, :], src_i[:, bass.ds(16 * i + 4 * k, SUP)], ACT.Copy).then_inc(idx_ok.sem, 1)

        def gather(g, i, k):
            if absent(i, k):
                return
            g.wait_ge(idx_ok.sem, idx_ok.at(4 * i + k))
            g.wait_ge(m_pre.sem, m_pre.at(4 * i + k - 4))
            g.sem_inc(pool_turn, 1)
            for t in range(SUP):
                g.indirect_dma_start(gbuf[:, k, t, :], None, a_tab[:, :],
                                     bass.IndirectOffsetOnAxis(ap=idxb[:, k, t:t + 1], axis=0)).then_inc(g_land[k], 16)

        def load_pair(sp, i, k):
            if absent(i, k):
                return
            if k % HP:
                return
            b = k // HP
            e0 = (4 * i + k) * ES
            sp.wait_ge(r_mm.sem, r_mm.at(4 * i + k + 1 - 4))
            sp.sem_inc(sp_turn, 1)
            for j in range(PARTS):
                r = j * PARTS * KE
                sp.dma_start(rk[r:r + PARTS * KE, b, :, :].rearrange("p s e -> p (s e)"),
                             attr_rows[:, bass.ds(e0, HP * ES)]).then_inc(r_land[b], 16)
            sp.wait_ge(ohT_ok.sem, ohT_ok.at(4 * i + k + 1 - 4))
            sp.sem_inc(sp_turn, 1)
            sp.dma_start(dstbc[C:P, b, :, :].rearrange("p s e -> p (s e)"),
                         a["dst_row"][:, bass.ds(e0, HP * ES)].partition_broadcast(W)).then_inc(d_land[b], 16)

        def load_window(sp, i, k):
            if absent(i, k):
                return
            base = sp.value_load(base_i[:, bass.ds(4 * i + k, 1)], min_val=0, max_val=N - 1)
            sp.wait_ge(m_mm.sem, m_mm.at(4 * i + k - 2))
            sp.sem_inc(sp_turn, 1)
            sp.dma_start(rhs[C:P, k % 2, :], b_tab[bass.ds(base, W), :]).then_inc(w_land[k % 2], 16)

        def edge_product(pe, i, k):
            if absent(i, k):
                return
            if k % HP == 0:
                pe.wait_ge(r_land[k // HP], i * (16 * PARTS) + 16 * PARTS)
            pe.wait_ge(r_ok.sem, r_ok.at(4 * i + k - 2))
            pe.matmul(ps_r(k), w36[:, :], rk[:, k // HP, k % HP, :], start=True, stop=True).then_inc(r_mm.sem, 1)

        def edge_relu(act, i, k):
            if absent(i, k):
                return
            act.wait_ge(r_mm.sem, r_mm.at(4 * i + k))
            act.wait_ge(m_mm.sem, m_mm.at(4 * i + k - 2))
            act.activation(lhs[0:C, k % 2, :], ps_r(k), ACT.Relu, bias=par[:, B_EDGE:B_EDGE + 1]).then_inc(r_ok.sem, 1)

        def onehot_T(dve, i, k):
            if absent(i, k):
                return
            if k % HP == 0:
                dve.wait_ge(d_land[k // HP], i * 16 + 16)
            dve.wait_ge(m_mm.sem, m_mm.at(4 * i + k - 2))
            dve.tensor_scalar(lhs[C:P, k % 2, :], dstbc[C:P, k // HP, k % HP, :], winid[C:P, bass.ds(4 * i + k, 1)],
                              None, ALU.is_equal).then_inc(ohT_ok.sem, 1)

        def onehot(dve, i, k):
            if absent(i, k):
                return
            dve.wait_ge(s_mm.sem, s_mm.at(4 * i + k - 4))
            dve.tensor_tensor(oh[:, k, :, :], iota_w[:, :].unsqueeze(1).to_broadcast([P, SUP, W]),
                              dstrel[:, bass.ds(4 * i + k, 1), :].rearrange("p s t -> p (s t)").unsqueeze(2).to_broadcast([P, SUP, W]),
                              ALU.is_equal).then_inc(oh_ok.sem, 1)

        def message_product(pe, i, k):
            if absent(i, k):
                return
            pe.wait_ge(r_ok.sem, r_ok.at(4 * i + k))
            pe.wait_ge(ohT_ok.sem, ohT_ok.at(4 * i + k))
            pe.wait_ge(w_land[k % 2], i * 32 + 16 * (k // 2) + 16)
            pe.wait_ge(m_pre.sem, m_pre.at(4 * i + k - 2))
            for t in range(SUP):
                ins = pe.matmul(ps_m(k)[:, t, :], lhs[:, k % 2, t * TILE:(t + 1) * TILE], rhs[:, k % 2, :],
                                start=True, stop=True)
            ins.then_inc(m_mm.sem, 1)

        def add_gathered(dve, i, k):
            if absent(i, k):
                return
            dve.wait_ge(m_mm.sem, m_mm.at(4 * i + k))
            dve.wait_ge(g_land[k], i * (16 * SUP) + 16 * SUP)
            dve.wait_ge(m_ok.sem, m_ok.at(4 * i + k - 2))
            dve.tensor_tensor(pre[:, k % 2, :, :], ps_m(k), gbuf[:, k, :, :], ALU.add).then_inc(m_pre.sem, 1)

        def message_relu(act, i, k):
            if absent(i, k):
                return
            act.wait_ge(m_pre.sem, m_pre.at(4 * i + k))
            act.wait_ge(s_mm.sem, s_mm.at(4 * i + k - 2))
            act.wait_ge(m_sq.sem, m_sq.at(4 * i + k - 2))
            act.activation(msg[:, k % 2, :, 0:C], pre[:, k % 2, :, :], ACT.Relu).then_inc(m_ok.sem, 1)

        def square(act, i, k):
            if absent(i, k):
                return
            act.wait_ge(m_ok.sem, m_ok.at(4 * i + k))
            act.wait_ge(m_acc.sem, m_acc.at(4 * i + k - 2))
            act.activation(sq[:, k % 2, :, :], msg[:, k % 2, :, 0:C], ACT.Square).then_inc(m_sq.sem, 1)

        def accumulate(dve, i, k):
            if absent(i, k):
                return
            dve.wait_ge(m_sq.sem, m_sq.at(4 * i + k))
            dve.wait_ge(m_acc.sem, m_acc.at(4 * i + k - 1))
            dve.tensor_tensor(acc[:, :, :], acc[:, :, :], sq[:, k % 2, :, :], ALU.add).then_inc(m_acc.sem, 1)

        def sum_edges(pe, i, k):
            if absent(i, k):
                return
            pe.wait_ge(m_ok.sem, m_ok.at(4 * i + k))
            pe.wait_ge(oh_ok.sem, oh_ok.at(4 * i + k))
            pe.wait_ge(s_add.sem, s_add.at(4 * i + k - 2))
            for t in range(SUP):
                ins = pe.matmul(ps_s(k), msg[:, k % 2, t, :], oh[:, k, t, :], start=(t == 0), stop=(t == SUP - 1))
            ins.then_inc(s_mm.sem, 1)

        def add_window(dve, i, k):
            if absent(i, k):
                return
            base = dve.value_load(base_i[:, bass.ds(4 * i + k, 1)], min_val=0, max_val=N - 1)
            dve.wait_ge(s_mm.sem, s_mm.at(4 * i + k))
            dve.wait_ge(s_add.sem, s_add.at(4 * i + k - 1))
            cols = sT[0:C + 1, bass.ds(base, W)]
            dve.tensor_tensor(cols, cols, ps_s(k), ALU.add).then_inc(s_add.sem, 1)


        y = gbuf[:, :, :, :].rearrange("p k t c -> p (k t c)")
        y_drow = y[:, 0:P].bitcast(I32)
        y_eq = y[:, P:2 * P]
        y_low = y[:, 2 * P:3 * P]
        y_both = y[:, 3 * P:4 * P]
        y_ga = y[:, 4 * P:4 * P + C]
        y_gb = y[:, 4 * P + C:4 * P + 2 * C]
        y_gs = y[:, 4 * P + 2 * C:4 * P + 3 * C + 1]
        YS = 4 * P + 3 * C + 1
        y_is, y_id, y_iw = (y[:, YS + j:YS + j + 1].bitcast(I32) for j in range(3))
        y_dst, y_rank, y_trash, y_w = (y[:, YS + j:YS + j + 1] for j in range(3, 7))
        y_msg = msg[:, 0, 0, :]

        def general_pass(tag, messages):
            table = a_tab if messages else t_tab
            y_zero = sem("y_zero" + tag)
            y_init = sem("y_init" + tag)
            y_load = sem("y_load" + tag)
            y_gath = sem("y_gath" + tag)
            y_scat = sem("y_scat" + tag)
            y_v = sem("y_v" + tag)
            y_pe = sem("y_pe" + tag)
            y_act = sem("y_act" + tag)
            z_load = sem("z_load" + tag)
            z_tr = sem("z_tr" + tag)
            z_copy = sem("z_copy" + tag)
            nload = 3 + (PARTS if messages else 0)
            ngath = 3 if messages else 2
            VSTEPS = 11 if messages else 9
            PSTEPS = 3 if messages else 1
            ASTEPS = 3
            ninit = 5

            with nc.Block() as block:
                @block.sync
                def _(sp):
                    sp.wait_ge(y_init, ninit)
                    sp.dma_start(s_tab.rearrange("(t p) f -> p t f", p=P),
                                 sT[:, 0:(NT + 1) * (C + 1)].rearrange("p (t f) -> p t f", f=C + 1)).then_inc(y_zero, 16)
                    sp.wait_ge(y_zero, 16)
                    with sp.Fori(0, T) as t:
                        sp.dma_start(y_is, a["src"][:, bass.ds(t, 1)]).then_inc(y_load, 16)
                        sp.dma_start(y_id, a["dst"][:, bass.ds(t, 1)]).then_inc(y_load, 16)
                        sp.dma_start(y_drow, a["dst_row"][:, bass.ds(t * TILE, TILE)].partition_broadcast(P)).then_inc(y_load, 16)
                        if messages:
                            for j in range(PARTS):
                                r = j * PARTS * KE
                                sp.dma_start(rk[r:r + PARTS * KE, 0, 0, 0:TILE],
                                             attr_rows[:, bass.ds(t * TILE, TILE)]).then_inc(y_load, 16)
                        sp.wait_ge(y_scat, t * 16 + 16)
                        sp.sem_inc(sp_turn, 1)
                    with sp.Fori(0, NT) as t:
                        sp.dma_start(y_gs, s_tab[bass.ds(t * P, P), :]).then_inc(z_load, 16)
                        sp.wait_ge(z_copy, t + 1)
                        sp.sem_inc(sp_turn, 1)

                @block.gpsimd
                def _(g):
                    g.memset(y_low, 1.0).then_inc(y_init, 1)
                    g.memset(sT[:, 0:(NT + 1) * (C + 1)], 0.0).then_inc(y_init, 1)
                    g.wait_ge(y_init, 2)
                    g.affine_select(out=y_low, in_=y_low, compare_op=ALU.is_gt, fill=0.0, base=0,
                                    pattern=[[-1, P]], channel_multiplier=1).then_inc(y_init, 1)
                    g.iota(y_trash, [[0, 1]], base=NP, channel_multiplier=1,
                           allow_small_or_imprecise_dtypes=True).then_inc(y_init, 1)
                    g.memset(acc[:, :, :], 0.0).then_inc(y_init, 1)
                    with g.Fori(0, T) as t:
                        g.wait_ge(y_load, t * (16 * nload) + 16 * nload)
                        g.sem_inc(pool_turn, 1)

                        def gather_rows(to, tab, idx):
                            g.indirect_dma_start(to, None, tab[:, :], bass.IndirectOffsetOnAxis(ap=idx, axis=0)).then_inc(y_gath, 16)
                        gather_rows(y_ga, table, y_is)
                        if messages:
                            gather_rows(y_gb, b_tab, y_id)
                        gather_rows(y_gs, s_tab, y_id)
                        g.wait_ge(y_v, t * VSTEPS + VSTEPS)
                        g.sem_inc(pool_turn, 1)
                        g.indirect_dma_start(s_tab[:, :], bass.IndirectOffsetOnAxis(ap=y_iw, axis=0), y_gs, None).then_inc(y_scat, 16)

                @block.vector
                def _(dve):
                    dve.wait_ge(y_init, ninit)
                    with dve.Fori(0, T) as t:
                        n = [0]

                        def link(ins):
                            n[0] += 1
                            ins.then_inc(y_v, 1)
                            dve.wait_ge(y_v, t * VSTEPS + n[0])
                        dve.wait_ge(y_load, t * (16 * nload) + 16 * nload)
                        link(dve.tensor_copy(y_dst, y_id))
                        link(dve.tensor_scalar(y_eq, y_drow, y_dst, None, ALU.is_equal))
                        link(dve.tensor_tensor(y_both, y_eq, y_low, ALU.mult))
                        link(dve.tensor_reduce(y_rank, y_both, AX, ALU.max))
                        link(dve.tensor_tensor(y_w, y_trash, y_dst, ALU.subtract))
                        link(dve.tensor_tensor(y_w, y_w, y_rank, ALU.mult))
                        link(dve.tensor_tensor(y_iw, y_w, y_dst, ALU.add))
                        dve.wait_ge(y_gath, t * (16 * ngath) + 16 * ngath)
                        if messages:
                            dve.wait_ge(y_pe, t * PSTEPS + 2)
                            link(dve.tensor_tensor(pre[:, 0, 0, :], bank[1][:, 0:C], y_ga, ALU.add))
                            link(dve.tensor_tensor(pre[:, 0, 0, :], pre[:, 0, 0, :], y_gb, ALU.add))
                            dve.wait_ge(y_act, t * ASTEPS + 3)
                            link(dve.tensor_tensor(acc[:, 0, :], acc[:, 0, :], sq[:, 0, 0, :], ALU.add))
                        else:
                            link(dve.tensor_copy(y_msg[:, 0:C], y_ga))
                        dve.wait_ge(y_pe, t * PSTEPS + PSTEPS)
                        link(dve.tensor_tensor(y_gs, bank[2][:, 0:C + 1], y_gs, ALU.add))

                @block.tensor
                def _(pe):
                    with pe.Fori(0, T) as t:
                        if messages:
                            pe.wait_ge(y_load, t * (16 * nload) + 16 * nload)
                            pe.matmul(bank[0][0:C, 0:TILE], w36[:, :], rk[:, 0, 0, 0:TILE], start=True, stop=True).then_inc(y_pe, 1)
                            pe.wait_ge(y_act, t * ASTEPS + 1)
                            pe.matmul(bank[1][:, 0:C], lhs[0:C, 0, 0:TILE], rhs[0:C, 0, :], start=True, stop=True).then_inc(y_pe, 1)
                            pe.wait_ge(y_act, t * ASTEPS + 2)
                        else:
                            pe.wait_ge(y_v, t * VSTEPS + 8)
                        pe.matmul(bank[2][:, 0:C + 1], y_eq, y_msg, start=True, stop=True).then_inc(y_pe, 1)
                    with pe.Fori(0, NT) as t:
                        pe.wait_ge(z_load, t * 16 + 16)
                        pe.transpose(bank[0][0:C + 1, 0:P], y_gs, ident[:, :]).then_inc(z_tr, 1)

                @block.scalar
                def _(act):
                    if messages:
                        with act.Fori(0, T) as t:
                            act.wait_ge(y_pe, t * PSTEPS + 1)
                            act.activation(lhs[0:C, 0, 0:TILE], bank[0][0:C, 0:TILE], ACT.Relu,
                                           bias=par[:, B_EDGE:B_EDGE + 1]).then_inc(y_act, 1)
                            act.wait_ge(y_v, t * VSTEPS + 9)
                            act.activation(y_msg[:, 0:C], pre[:, 0, 0, :], ACT.Relu).then_inc(y_act, 1)
                            act.wait_ge(y_act, t * ASTEPS + 2)
                            act.activation(sq[:, 0, 0, :], y_msg[:, 0:C], ACT.Square).then_inc(y_act, 1)
                    with act.Fori(0, NT) as t:
                        act.wait_ge(z_tr, t + 1)
                        act.activation(sT[0:C + 1, bass.ds(t * P, P)], bank[0][0:C + 1, 0:P], ACT.Copy).then_inc(z_copy, 1)

        windowed = nc.values_load(flag_i[:, :], min_val=0, max_val=1)
        m0 = sem("m0")
        with nc.If(windowed):
            with nc.Block() as block:
                @block.gpsimd
                def _(g):
                    def step(i, k):
                        gather(g, i, k)
                    pipelined(g, step, 0)

                @block.sync
                def _(sp):
                    def step(i, k):
                        load_pair(sp, i, k)
                        load_window(sp, i, k)
                    pipelined(sp, step, 0)

                @block.tensor
                def _(pe):
                    for x in (r_mm, m_mm, s_mm):
                        x.start(pe)
                    def step(i, k):
                        edge_product(pe, i, k)
                        message_product(pe, *earlier(i, k, 1))
                        sum_edges(pe, *earlier(i, k, 2))
                    pipelined(pe, step, 2)

                @block.scalar
                def _(act):
                    for x in (r_ok, m_ok, m_sq):
                        x.start(act)
                    def step(i, k):
                        copy_indices(act, i, k)
                        edge_relu(act, i, k)
                        message_relu(act, *earlier(i, k, 1))
                        square(act, *earlier(i, k, 1))
                    pipelined(act, step, 1)

                @block.vector
                def _(dve):
                    dve.memset(sT[:, 0:NP], 0.0).then_inc(m0, 1)
                    dve.memset(acc[:, :, :], 0.0).then_inc(m0, 1)
                    dve.wait_ge(m0, 2)
                    for x in (ohT_ok, m_pre, m_acc, s_add):
                        x.start(dve)
                    def step(i, k):
                        onehot_T(dve, i, k)
                        onehot(dve, i, k)
                        add_gathered(dve, *earlier(i, k, 1))
                        accumulate(dve, *earlier(i, k, 2))
                        add_window(dve, *earlier(i, k, 2))
                    pipelined(dve, step, 2)
        with nc.Else():
            general_pass("_m", True)

        h2_all = nf[:, 0:NT * C].rearrange("p (t c) -> p t c", c=C)
        sq_all = sT[:, 0:NT * C].rearrange("p (t c) -> p t c", c=C)
        v_sb = lhs[0:C + 1, 0, :]
        v1_sb = lhs[0:C + 1, 1, :]
        tm_l = trep[0:C, 0:C + 1]
        mix = cstb[0:C + 1, :]
        m_row = bank[6][0:C + 1, 0:C]
        ps_x = bank[0][:, 0:CT * C].rearrange("p (k f) -> p k f", k=CT)
        ps_c = bank[1][:, 0:CT].unsqueeze(2)
        PADS = EP - E
        l_x2 = sem("l_x2")
        q_mm = sem("q_mm")
        q_v = sem("q_v")
        q_std = sem("q_std")
        q_row = sem("q_row")
        q_lhs = sem("q_lhs")
        p_v1 = signal("p_v1", 0)
        p_v = signal("p_v", 1)
        p_mm = signal("p_mm", 1)
        p_x1 = signal("p_x1", 1)
        p_row = sem("p_row")
        o_cnt = sem("o_cnt")
        p_c = sem("p_c")
        p_sq = sem("p_sq")
        p_var = sem("p_var")
        p_std = sem("p_std")
        p_h2 = sem("p_h2")
        p_xh = sem("p_xh")
        p_t2 = sem("p_t2")
        p_sum = sem("p_sum")
        o_t = sem("o_t")
        l_w5 = sem("l_w5")
        wc_mm = sem("wc_mm")
        wc_ok = sem("wc_ok")
        s_zero = sem("s_zero")
        t_rows = t_tab.rearrange("(t p) f -> p t f", p=P)

        with nc.Block() as block:
            @block.sync
            def _(sp):
                sp.dma_start(x_all[:, :, :], a["x"]).then_inc(l_x2, 16)
                sp.wait_ge(q_lhs, 3)
                sp.dma_start(cnt_row[:, :], sT[C:C + 1, 0:NP]).then_inc(o_cnt, 16)
                sp.wait_ge(p_t2, 1)
                sp.dma_start(t_rows, h2_all).then_inc(o_t, 16)
                sp.wait_ge(o_t, 16)
                sp.dma_start(t_tab[N:N + 1, :], zrow[:, :]).then_inc(o_t, 16)
                sp.wait_ge(o_t, 32)

            @block.vector
            def _(dve):
                n = [0]

                def link(ins):
                    n[0] += 1
                    ins.then_inc(q_v, 1)
                    dve.wait_ge(q_v, n[0])

                def col(c):
                    return aff[:, c:c + 1]
                link(dve.tensor_reduce(col(TMP0), sT[0:C, 0:N], AX, ALU.add))
                link(dve.tensor_scalar(col(TMP0), col(TMP0), 1.0 / E, None, ALU.mult))
                link(dve.tensor_tensor(col(TMP1), col(TMP0), col(TMP0), ALU.mult))
                dve.wait_ge(q_mm, 1)
                link(dve.scalar_tensor_tensor(col(TMP2), bank[7][0:C, 0:1], 1.0 / E, col(TMP1), ALU.mult, ALU.subtract))
                dve.tensor_scalar(col(TMP2), col(TMP2), 0.0, None, ALU.max).then_inc(q_row, 1)
                dve.wait_ge(q_std, 1)
                link(dve.reciprocal(col(TMP1), col(TMP3)))
                link(dve.memset(smc[:, :], 1.0))
                link(dve.tensor_tensor(smc[0:C, :], col(TMP1), par[:, G_MSG:G_MSG + 1], ALU.mult))
                link(dve.tensor_tensor(col(TMP2), col(TMP0), smc[0:C, :], ALU.mult))
                link(dve.memset(tm_l, 0.0))
                dve.tensor_tensor(tm_l[:, C:C + 1], par[:, T_MSG:T_MSG + 1], col(TMP2), ALU.subtract).then_inc(q_lhs, 1)
                link(dve.tensor_copy(mix[:, :], ident[0:C + 1, 0:C]))
                dve.wait_ge(q_lhs, 2)
                link(dve.tensor_copy(mix[C:C + 1, :], m_row[C:C + 1, :]))
                last = sT[C:C + 1, N - 1:N]
                link(dve.tensor_scalar(last, last, -float(PADS), None, ALU.add))
                dve.memset(v1_sb[C:C + 1, :], 0.0).then_inc(q_lhs, 1)
                dve.wait_ge(q_lhs, 3)
                dve.wait_ge(l_x2, 16)
                p_v.start(dve)
                p_x1.start(dve)
                with dve.Fori(0, NCH) as c:
                    dve.wait_ge(p_v1.sem, p_v1.at(c))
                    dve.wait_ge(p_mm.sem, p_mm.at(c - 1))
                    dve.scalar_tensor_tensor(v_sb, sT[0:C + 1, bass.ds(c * CH, CH)], smc[:, :], v1_sb,
                                             ALU.mult, ALU.add).then_inc(p_v.sem, 1)
                    dve.wait_ge(p_mm.sem, p_mm.at(c))
                    xs = x_all[:, bass.ds(c * CT, CT), :]
                    dve.tensor_tensor(xs, xs, ps_x, ALU.add)
                    dve.tensor_copy(dinv[:, bass.ds(c * CT, CT)], bank[1][:, 0:CT]).then_inc(p_x1.sem, 1)
                dve.wait_ge(p_x1.sem, p_x1.at(NCH - 1))
                dve.tensor_reduce(mean[:, :], x_all[:, :, :], AX, ALU.add).then_inc(p_sum, 1)
                dve.wait_ge(p_sum, 1)
                dve.tensor_scalar(mean[:, :], mean[:, :], 1.0 / C, None, ALU.mult).then_inc(p_sum, 1)
                dve.wait_ge(p_sum, 2)
                dve.tensor_tensor(h2_all, x_all[:, :, :], mean[:, :].unsqueeze(2).to_broadcast([P, NT, C]),
                                  ALU.subtract).then_inc(p_c, 1)
                dve.wait_ge(p_row, 1)
                dve.reciprocal(dinv[:, :], dinv[:, :]).then_inc(p_sum, 1)
                dve.wait_ge(p_sq, 1)
                dve.tensor_reduce(rstd[:, :], sq_all, AX, ALU.add).then_inc(p_var, 1)
                dve.wait_ge(p_std, 1)
                dve.reciprocal(rstd[:, :], rstd[:, :]).then_inc(p_sum, 1)
                dve.wait_ge(p_sum, 4)
                dve.wait_ge(p_c, 1)
                dve.scalar_tensor_tensor(h2_all, h2_all, 0.0, rstd[:, :].unsqueeze(2).to_broadcast([P, NT, C]),
                                         ALU.max, ALU.mult).then_inc(p_h2, 1)
                dve.wait_ge(p_h2, 1)
                dve.tensor_tensor(x_all[:, :, :], x_all[:, :, :], h2_all, ALU.add).then_inc(p_xh, 1)
                dve.wait_ge(p_xh, 1)
                dve.tensor_tensor(h2_all, h2_all, dinv[:, :].unsqueeze(2).to_broadcast([P, NT, C]),
                                  ALU.mult).then_inc(p_t2, 1)

            @block.tensor
            def _(pe):
                for t in range(SUP):
                    ins = pe.matmul(bank[7][0:C, 0:1], acc[:, t, :], ones[:, 0:1], start=(t == 0), stop=(t == SUP - 1))
                ins.then_inc(q_mm, 1)
                pe.wait_ge(q_lhs, 1)
                pe.matmul(m_row, tm_l, ident[0:C, 0:C], start=True, stop=True).then_inc(q_lhs, 1)
                pe.wait_ge(l_w5, 16 * 5)
                for j in range(3):
                    ins = pe.matmul(bank[5][0:C, 0:H], wgT[:, j, :], w1[:, j, :], start=(j == 0), stop=(j == 2))
                ins.then_inc(wc_mm, 1)
                p_mm.start(pe)
                with pe.Fori(0, NCH) as c:
                    pe.wait_ge(p_v.sem, p_v.at(c))
                    pe.wait_ge(p_x1.sem, p_x1.at(c - 1))
                    for k in range(CT):
                        pe.matmul(ps_x[:, k, :], v_sb[:, k * P:(k + 1) * P], mix[:, :], start=True, stop=True)
                        ins = pe.matmul(ps_c[:, k, :], v_sb[:, k * P:(k + 1) * P], ident[0:C + 1, C:C + 1], start=True, stop=True)
                    ins.then_inc(p_mm.sem, 1)

            @block.scalar
            def _(act):
                act.wait_ge(q_row, 1)
                act.activation(aff[:, TMP3:TMP3 + 1], aff[:, TMP2:TMP2 + 1], ACT.Sqrt, bias=eps[0:C, :]).then_inc(q_std, 1)
                act.wait_ge(wc_mm, 1)
                act.activation(wc[:, :], bank[5][0:C, 0:H], ACT.Copy).then_inc(wc_ok, 1)
                with act.Fori(0, NCH) as c:
                    act.wait_ge(p_v.sem, p_v.at(c - 1))
                    act.activation(v1_sb[0:C, :], nf[0:C, bass.ds(c * CH, CH)], ACT.Identity,
                                   bias=aff[:, T_N:T_N + 1], scale=aff[:, S_N:S_N + 1]).then_inc(p_v1.sem, 1)
                act.wait_ge(p_x1.sem, p_x1.at(NCH - 1))
                act.activation(dinv[:, :], dinv[:, :], ACT.Sqrt, bias=ones[:, 0:1]).then_inc(p_row, 1)
                act.wait_ge(p_c, 1)
                act.wait_ge(o_cnt, 16)
                act.activation(sq_all, h2_all, ACT.Square).then_inc(p_sq, 1)
                act.wait_ge(p_var, 1)
                act.activation(rstd[:, :], rstd[:, :], ACT.Sqrt, bias=eps[:, :], scale=1.0 / C).then_inc(p_std, 1)

            @block.gpsimd
            def _(g):
                g.dma_start(wgT[:, :, :], a["W_gcn_T"].rearrange("(j p) c -> p j c", p=C)).then_inc(l_w5, 16)
                g.dma_start(w1[:, :, :], a["W1"].rearrange("(j p) h -> p j h", p=C)).then_inc(l_w5, 16)
                g.dma_start(w2[0:H, :], a["W2"]).then_inc(l_w5, 16)
                g.dma_start(w2[H:H + 1, :], a["b2"]).then_inc(l_w5, 16)
                g.dma_start(b1c[:, :], a["b1"].rearrange("a h -> h a")).then_inc(l_w5, 16)
                g.wait_ge(l_w5, 16 * 5)
                g.wait_ge(p_var, 1)
                g.memset(sT[:, 0:NP], 0.0).then_inc(s_zero, 1)

        c_land = [sem(f"c_land{k}") for k in range(4)]
        c_idx = signal("c_idx", 0)
        c_oh = signal("c_oh", 0)
        c_mm = signal("c_mm", 4)
        c_add = signal("c_add", 2)

        def gcn_indices(act, i, k):
            if absent(i, k):
                return
            act.wait_ge(c_mm.sem, c_mm.at(4 * i + k - 4))
            act.activation(idxb[:, k, :], src_i[:, bass.ds(16 * i + 4 * k, SUP)], ACT.Copy).then_inc(c_idx.sem, 1)

        def gcn_gather(g, i, k):
            if absent(i, k):
                return
            g.wait_ge(c_idx.sem, c_idx.at(4 * i + k))
            g.wait_ge(c_mm.sem, c_mm.at(4 * i + k - 4))
            g.sem_inc(pool_turn, 1)
            for t in range(SUP):
                g.indirect_dma_start(gbuf[:, k, t, :], None, t_tab[:, :],
                                     bass.IndirectOffsetOnAxis(ap=idxb[:, k, t:t + 1], axis=0)).then_inc(c_land[k], 16)

        def gcn_onehot(dve, i, k):
            if absent(i, k):
                return
            dve.wait_ge(c_mm.sem, c_mm.at(4 * i + k - 4))
            dve.tensor_tensor(oh[:, k, :, :], iota_w[:, :].unsqueeze(1).to_broadcast([P, SUP, W]),
                              dstrel[:, bass.ds(4 * i + k, 1), :].rearrange("p s t -> p (s t)").unsqueeze(2).to_broadcast([P, SUP, W]),
                              ALU.is_equal).then_inc(c_oh.sem, 1)

        def gcn_sum(pe, i, k):
            if absent(i, k):
                return
            pe.wait_ge(c_land[k], i * (16 * SUP) + 16 * SUP)
            pe.wait_ge(c_oh.sem, c_oh.at(4 * i + k))
            pe.wait_ge(c_add.sem, c_add.at(4 * i + k - 2))
            for t in range(SUP):
                ins = pe.matmul(ps_s(k)[0:C, :], gbuf[:, k, t, :], oh[:, k, t, :], start=(t == 0), stop=(t == SUP - 1))
            ins.then_inc(c_mm.sem, 1)

        def gcn_add(dve, i, k):
            if absent(i, k):
                return
            base = dve.value_load(base_i[:, bass.ds(4 * i + k, 1)], min_val=0, max_val=N - 1)
            dve.wait_ge(c_mm.sem, c_mm.at(4 * i + k))
            dve.wait_ge(c_add.sem, c_add.at(4 * i + k - 1))
            cols = sT[0:C, bass.ds(base, W)]
            dve.tensor_tensor(cols, cols, ps_s(k)[0:C, :], ALU.add).then_inc(c_add.sem, 1)

        with nc.If(windowed):
            with nc.Block() as block:
                @block.gpsimd
                def _(g):
                    def step(i, k):
                        gcn_gather(g, i, k)
                    pipelined(g, step, 0)

                @block.scalar
                def _(act):
                    def step(i, k):
                        gcn_indices(act, i, k)
                    pipelined(act, step, 0)

                @block.tensor
                def _(pe):
                    c_mm.start(pe)
                    def step(i, k):
                        gcn_sum(pe, i, k)
                    pipelined(pe, step, 0)

                @block.vector
                def _(dve):
                    c_add.start(dve)
                    def step(i, k):
                        gcn_onehot(dve, i, k)
                        gcn_add(dve, *earlier(i, k, 1))
                    pipelined(dve, step, 1)
        with nc.Else():
            general_pass("_g", False)

        t2_sb = pre[:, 0, :, :]
        u_sb = lhs[0:C, 0, :]
        g_flat = gbuf[0:H, :, :, :].rearrange("p k t c -> p (k t c)")
        cnt_sb = g_flat[:, 0:CH]
        z1_sb = g_flat[:, CH:2 * CH]
        z_sb = lhs[0:H + 1, 1, :]
        o_sb = pre[:, 1, :, :]
        ps_o = bank[2][:, 0:CT * C].rearrange("p (k f) -> p k f", k=CT)
        f_cnt = sem("f_cnt")
        f_t2 = signal("f_t2", 0)
        f_tr = signal("f_tr", 1)
        f_u = signal("f_u", 1)
        f_z = signal("f_z", 1)
        f_sd = signal("f_sd", 0)
        f_di = signal("f_di", 0)
        f_z1 = signal("f_z1", 1)
        f_zr = signal("f_zr", 1)
        f_o = signal("f_o", 1)
        f_out = signal("f_out", 1)
        f_st = signal("f_st", 1)
        f_one = sem("f_one")
        o_out = sem("o_out")

        with nc.Block() as block:
            @block.sync
            def _(sp):
                f_st.start(sp)
                with sp.Fori(0, NCH) as c:
                    sp.wait_ge(f_z1.sem, f_z1.at(c - 1))
                    sp.sem_inc(sp_turn, 1)
                    sp.dma_start(cnt_sb, cnt_row[:, bass.ds(c * CH, CH)].partition_broadcast(H)).then_inc(f_cnt, 16)
                    sp.wait_ge(f_out.sem, f_out.at(c))
                    sp.sem_inc(sp_turn, 1)
                    sp.dma_start(out[:, bass.ds(c * CT, CT), :], o_sb).then_inc(o_out, 16)
                    sp.wait_ge(o_out, c * 16 + 16)
                    sp.sem_inc(f_st.sem, 1)

            @block.scalar
            def _(act):
                f_zr.start(act)
                with act.Fori(0, NCH) as c:
                    act.wait_ge(f_tr.sem, f_tr.at(c - 1))
                    act.activation(t2_sb, h2_all[:, bass.ds(c * CT, CT), :], ACT.Copy).then_inc(f_t2.sem, 1)
                    act.wait_ge(f_cnt, c * 16 + 16)
                    act.activation(cnt_sb, cnt_sb, ACT.Sqrt, bias=ones[0:H, 0:1]).then_inc(f_sd.sem, 1)
                    act.wait_ge(f_z1.sem, f_z1.at(c))
                    act.wait_ge(f_o.sem, f_o.at(c - 1))
                    act.activation(z_sb[0:H, :], z1_sb, ACT.Relu, bias=b1c[:, :]).then_inc(f_zr.sem, 1)

            @block.tensor
            def _(pe):
                f_tr.start(pe)
                f_z.start(pe)
                f_o.start(pe)
                pe.wait_ge(f_one, 1)
                with pe.Fori(0, NCH) as c:
                    pe.wait_ge(f_t2.sem, f_t2.at(c))
                    pe.wait_ge(f_u.sem, f_u.at(c - 1))
                    for k in range(CT):
                        ins = pe.transpose(bank[0][0:C, k * P:(k + 1) * P], t2_sb[:, k, :], ident[:, :])
                    ins.then_inc(f_tr.sem, 1)
                    pe.wait_ge(f_u.sem, f_u.at(c))
                    pe.wait_ge(f_z1.sem, f_z1.at(c - 1))
                    pe.matmul(bank[1][0:H, :], wc[:, :], u_sb, start=True, stop=True).then_inc(f_z.sem, 1)
                    pe.wait_ge(f_zr.sem, f_zr.at(c))
                    pe.wait_ge(f_out.sem, f_out.at(c - 1))
                    for k in range(CT):
                        ins = pe.matmul(ps_o[:, k, :], z_sb[:, k * P:(k + 1) * P], w2[:, :], start=True, stop=True)
                    ins.then_inc(f_o.sem, 1)

            @block.vector
            def _(dve):
                f_u.start(dve)
                f_z1.start(dve)
                f_out.start(dve)
                dve.memset(z_sb[H:H + 1, :], 1.0).then_inc(f_one, 1)
                with dve.Fori(0, NCH) as c:
                    dve.wait_ge(f_tr.sem, f_tr.at(c))
                    dve.wait_ge(f_z.sem, f_z.at(c - 1))
                    dve.tensor_tensor(u_sb, bank[0][0:C, :], sT[0:C, bass.ds(c * CH, CH)], ALU.add).then_inc(f_u.sem, 1)
                    dve.wait_ge(f_sd.sem, f_sd.at(c))
                    dve.reciprocal(cnt_sb, cnt_sb).then_inc(f_di.sem, 1)
                    dve.wait_ge(f_di.sem, f_di.at(c))
                    dve.wait_ge(f_z.sem, f_z.at(c))
                    dve.wait_ge(f_zr.sem, f_zr.at(c - 1))
                    dve.tensor_tensor(z1_sb, bank[1][0:H, :], cnt_sb, ALU.mult).then_inc(f_z1.sem, 1)
                    dve.wait_ge(f_o.sem, f_o.at(c))
                    dve.wait_ge(f_st.sem, f_st.at(c - 1))
                    dve.tensor_tensor(o_sb, ps_o, x_all[:, bass.ds(c * CT, CT), :], ALU.add).then_inc(f_out.sem, 1)

def lay_out(inputs):
    import numpy as np
    x = np.asarray(inputs["x"])
    src, dst = np.asarray(inputs["src"]), np.asarray(inputs["dst"])
    attr = np.asarray(inputs["edge_attr_4"])
    n, e = x.shape[0], src.shape[0]
    d = Dims(n, e)

    def nodes(v):
        pad = np.zeros((d.NP, v.shape[1]), v.dtype)
        pad[:n] = v
        return np.ascontiguousarray(pad.reshape(d.NT, P, -1).transpose(1, 0, 2))

    def edges(v, fill):
        pad = np.full(d.EP, fill, v.dtype)
        pad[:e] = v
        return pad

    attr_t = np.zeros((KE, d.EP), attr.dtype)
    attr_t[:, :e] = attr.T
    dst_p = edges(dst, n - 1)
    arrays = {
        "x": nodes(x),
        "src": np.ascontiguousarray(edges(src, n).reshape(d.T, P).T),
        "dst": np.ascontiguousarray(dst_p.reshape(d.T, P).T),
        "dst_row": dst_p.reshape(1, d.EP),
        "attr": attr_t,
    }
    for name, v in inputs.items():
        if name[:3] in ("L0_", "L1_"):
            v = np.asarray(v)
            arrays[name[7:]] = np.ascontiguousarray(v if v.ndim == 2 else v.reshape(1, -1))
    arrays["W_gcn_T"] = np.ascontiguousarray(arrays.pop("W_gcn").T)
    return d, arrays


def build(nc, d, arrays):
    a = {k: nc.dram_tensor(k, v.shape, mybir.dt.from_np(v.dtype), kind="ExternalInput").ap() for k, v in arrays.items()}
    out = nc.dram_tensor("out_0_dram", (P, d.NT, C), FP32, kind="ExternalOutput").ap()
    gnn_kernel(nc, d, a, out)


def unpack(o, n):
    import numpy as np
    return np.ascontiguousarray(np.asarray(o).transpose(1, 0, 2).reshape(-1, C)[:n])


def kernel(**inputs):
    import concourse.bacc as bacc
    from concourse.bass_utils import run_bass_kernel_spmd
    d, arrays = lay_out(inputs)
    nc = bacc.Bacc("TRN2", target_bir_lowering=False, num_devices=1)
    build(nc, d, arrays)
    r = run_bass_kernel_spmd(nc, [arrays], core_ids=[0])
    return unpack(r.results[0]["out_0_dram"], d.N)
```

```python
import concourse.bass as bass
from concourse import mybir
from contextlib import ExitStack

FP32 = mybir.dt.float32
BF16 = mybir.dt.bfloat16
I32 = mybir.dt.int32
ALU = mybir.AluOpType
ACT = mybir.ActivationFunctionType
AX = mybir.AxisListType.X
RMAX = bass.bass_isa.ReduceOp.max
RADD = bass.bass_isa.ReduceOp.add

C = 96
KE = 4
H = 32
P = 128
TILE = 128
SUP = 4
ES = TILE * SUP
W = P - C
CH = 512
CT = CH // P
PARTS = 3
KR = PARTS * PARTS * KE
EPS = 1e-5
SPILL = 8
NEG = -1e30


class Dims:

    def __init__(self, n, e):
        self.N, self.E = n, e
        self.NCH = -(-(n + W) // CH)
        self.NP = self.NCH * CH
        self.NT = self.NP // P
        self.S = -(-e // (ES * SPILL)) * SPILL
        self.EP = self.S * ES
        self.T = self.S * SUP


class Signal:

    def __init__(self, handle, ahead):
        self.sem, self.ahead = handle, ahead

    def start(self, engine):
        engine.sem_inc(self.sem, self.ahead)

    def at(self, item):
        return item + (1 + self.ahead)


class Turns:

    def __init__(self, count, unroll, plain=None):
        self.count, self.unroll = count, unroll
        self.loops = (count if plain is None else plain) // unroll

    def earlier(self, i, k, n):
        return i + (k - n) // self.unroll, (k - n) % self.unroll

    def absent(self, i, k):
        return isinstance(i, int) and not 0 <= self.unroll * i + k < self.count

    def run(self, engine, step, lag):
        for k in range(self.unroll):
            step(0, k)
        with engine.Fori(1, self.loops) as i:
            for k in range(self.unroll):
                step(i, k)
        for k in range(self.count - self.loops * self.unroll + lag):
            step(self.loops + k // self.unroll, k % self.unroll)


def gnn_kernel(nc, d, a, out):
    N, E, NP, NT, NCH, S, EP, T = d.N, d.E, d.NP, d.NT, d.NCH, d.S, d.EP, d.T
    ctx = ExitStack()
    with ctx:
        ctx.enter_context(nc.allow_non_contiguous_dma(reason="short rows of node tables and parameters"))

        def sb(name, shape, dt=FP32):
            return ctx.enter_context(nc.sbuf_tensor(name, shape, dt))

        def sem(name):
            return ctx.enter_context(nc.semaphore(name))

        def signal(name, ahead):
            return Signal(ctx.enter_context(nc.semaphore(name)), ahead)

        pool_turn = sem("pool_turn")
        sp_turn = sem("sp_turn")

        def dram(name, shape, dt=FP32):
            return nc.dram_tensor(name, shape, dt, kind="Internal").ap()

        attr_parts = dram("attr_parts", (PARTS, KE, EP), BF16)
        w_parts = dram("w_parts", (PARTS, KE, C), BF16)
        a_tab = dram("a_tab", (NP, C))
        b_tab = dram("b_tab", (NP, C))
        t_tab = dram("t_tab", (NP, C))
        cnt_row = dram("cnt_row", (1, NP))
        NSPILL = S // SPILL
        spilled = dram("spilled", (NSPILL, P, SUP * C))
        s_tab = dram("s_tab", (NP + P, C + 1))

        x_all = sb("x_all", [P, NT, C])
        sT = sb("sT", [P, max(NP, (NT + 1) * (C + 1), 8 * KE * EP // P // 8, 6 * S)])
        nf = sb("nf", [P, max(NP, T + NT * C)])
        src_i = sb("src_i", [P, T], I32)
        dstrel = sb("dstrel", [P, S, SUP])
        winid = sb("winid", [P, S])
        base_i = sb("base_i", [1, S], I32)
        ident = sb("ident", [P, P])
        iota_w = sb("iota_w", [P, W])
        pcol = sb("pcol", [P, 1])
        ones = sb("ones", [P, P])
        flag_f = sb("flag_f", [P, 4])
        flag_i = sb("flag_i", [1, 1], I32)
        negrow = sb("negrow", [1, C])
        zrow = sb("zrow", [1, C])
        w36 = sb("w36", [KR, C], BF16)
        wnode = sb("wnode", [C, C])
        wab = sb("wab", [C, 2 * C])
        w3 = sb("w3", [C, C])
        bm_row = sb("bm_row", [1, C])
        par = sb("par", [C, 8])
        B_NODE, G_NODE, T_NODE, B_EDGE, G_EDGE, T_EDGE, G_MSG, T_MSG = range(8)
        eps = sb("eps", [P, 1])
        cstb = sb("cstb", [P, C])
        aff = sb("aff", [C, 16])
        S_E, T_E, S_N, T_N, S_M, T_M, TMP0, TMP1, TMP2, TMP3 = range(10)
        rstd = sb("rstd", [P, NT])
        mean = sb("mean", [P, NT])
        nstat = sb("nstat", [C, NCH, 6])
        agg2 = sb("agg2", [C, 4])
        dinv = sb("dinv", [P, NT])
        smc = sb("smc", [C + 1, 1])
        wgT = sb("wgT", [C, 3, C])
        w1 = sb("w1", [C, 3, H])
        w2 = sb("w2", [H + 1, C])
        wc = sb("wc", [C, H])
        b1c = sb("b1c", [H, 1])
        trep = sb("trep", [C, P])
        gbuf = sb("gbuf", [P, 4, SUP, C])
        idxb = sb("idxb", [P, 4, SUP], I32)
        lhs = sb("lhs", [P, 2, ES])
        rhs = sb("rhs", [P, 2, C])
        pre = sb("pre", [P, 2, SUP, C])
        msg = sb("msg", [P, 2, SUP, C + 1])
        sq = sb("sq", [P, 2, SUP, C])
        acc = sb("acc", [P, SUP, C])
        oh = sb("oh", [P, 4, SUP, W])
        psum = ctx.enter_context(nc.psum_tensor("psum", [P, 8 * 512], FP32))
        bank = [psum[:, i * 512:(i + 1) * 512] for i in range(8)]

        x_flat = x_all[:, :, :].rearrange("p t c -> p (t c)")
        rk = x_flat[0:KR, 0:2 * ES].bitcast(BF16).rearrange("p (b s e) -> p b s e", b=2, e=ES)
        dstbc = x_flat[:, 2 * ES:6 * ES].bitcast(I32).rearrange("p (b s e) -> p b s e", b=2, e=ES)
        dst_i = nf[:, 0:T].bitcast(I32)
        sum_sq = nf[:, T:T + NT * C].rearrange("p (t c) -> p t c", c=C)
        NPC = 8
        AC = KE * EP // P // NPC
        araw = sT[:, 0:2 * AC].rearrange("p (b f) -> p b f", b=2)
        ares = sT[:, 2 * AC:4 * AC].rearrange("p (b f) -> p b f", b=2)
        part0 = sT[:, 4 * AC:4 * AC + 3 * AC // 2].bitcast(BF16).rearrange("p (b f) -> p b f", b=3)
        part12 = sT[:, 4 * AC + 3 * AC // 2:4 * AC + 7 * AC // 2].bitcast(BF16).rearrange("p (i b f) -> p i b f", i=2, b=2)
        attr_in = a["attr"].rearrange("k e -> (k e)").rearrange("(p q f) -> q p f", p=P, q=NPC)
        attr_out = [attr_parts[j].rearrange("k e -> (k e)").rearrange("(p q f) -> q p f", p=P, q=NPC)
                    for j in range(PARTS)]

        l_par = sem("l_par")
        l_dst = sem("l_dst")
        l_src = sem("l_src")
        l_x = [sem("l_x0"), sem("l_x1")]
        l_attr = [sem("l_attr0"), sem("l_attr1")]
        l_we = sem("l_we")
        o_wp = sem("o_wp")
        l_w36 = sem("l_w36")
        o_sp = [sem("o_sp0"), sem("o_sp1"), sem("o_sp2")]
        split_0 = sem("split_0")
        split_1 = sem("split_1")
        split_2 = sem("split_2")
        rest_1 = sem("rest_1")
        rest_2 = sem("rest_2")
        c_pool = sem("c_pool")
        v = sem("v")
        base_f_ok = sem("base_f_ok")
        base_mm = sem("base_mm")
        viol_ok = sem("viol_ok")
        viol_all = sem("viol_all")
        centred = sem("centred")
        squared = sem("squared")
        var_ok = sem("var_ok")
        std_ok = sem("std_ok")
        we_ok = sem("we_ok")

        base_f = lhs[0:1, :, :].rearrange("p a b -> p (a b)")[:, 0:S]
        we_f = trep[0:KE, 0:C]
        we_r = cstb[0:KE, 0:C]
        we_p = acc[0:KE, 0:2, :].rearrange("p a b -> p (a b)").bitcast(BF16)[:, 0:PARTS * C].rearrange("p (i c) -> p i c", i=PARTS)
        SH = S // 2
        NH = NT // 2

        with nc.Block() as block:
            @block.sync
            def _(sp):
                sp.dma_start(dst_i[:, :], a["dst"]).then_inc(l_dst, 16)
                sp.dma_start(we_f, a["W_edge"]).then_inc(l_we, 16)
                for h in range(2):
                    sp.dma_start(x_all[:, h * NH:(h + 1) * NH, :], a["x"][:, h * NH:(h + 1) * NH, :]).then_inc(l_x[h], 16)
                for i in range(2):
                    sp.dma_start(araw[:, i, :], attr_in[i]).then_inc(l_attr[i], 16)
                sp.dma_start(src_i[:, :], a["src"]).then_inc(l_src, 16)
                sp.dma_start(wnode[:, :], a["W_node"]).then_inc(l_par, 16)
                sp.dma_start(wab[:, 0:C], a["W_msg"][0:C, :]).then_inc(l_par, 16)
                sp.dma_start(wab[:, C:2 * C], a["W_msg"][C:2 * C, :]).then_inc(l_par, 16)
                sp.dma_start(w3[:, :], a["W_msg"][2 * C:3 * C, :]).then_inc(l_par, 16)
                sp.dma_start(bm_row[:, :], a["b_msg"]).then_inc(l_par, 16)
                for j, name in enumerate(("b_node", "g_node", "beta_node", "b_edge", "g_edge", "beta_edge", "g_msg", "beta_msg")):
                    sp.dma_start(par[:, j:j + 1], a[name].rearrange("a c -> c a")).then_inc(l_par, 16)
                sp.wait_ge(we_ok, 3)
                sp.dma_start(w_parts.rearrange("i k c -> k i c"), we_p).then_inc(o_wp, 16)
                sp.wait_ge(o_wp, 16)
                for j in range(PARTS):
                    for i in range(PARTS):
                        r = (j * PARTS + i) * KE
                        sp.dma_start(w36[r:r + KE, :], w_parts[j]).then_inc(l_w36, 16)
                for i in range(NPC):
                    if i + 2 < NPC:
                        sp.wait_ge(rest_1, i + 1)
                        sp.dma_start(araw[:, i % 2, :], attr_in[i + 2]).then_inc(l_attr[i % 2], 16)
                    sp.wait_ge(split_2, i + 1)
                    for j, part in enumerate((part0[:, i % 3, :], part12[:, 0, i % 2, :], part12[:, 1, i % 2, :])):
                        sp.dma_start(attr_out[j][i], part).then_inc(o_sp[i % 3], 16)
                for b in range(3):
                    sp.wait_ge(o_sp[b], 16 * PARTS * len(range(b, NPC, 3)))
                sp.wait_ge(l_w36, 16 * PARTS * PARTS)
                sp.wait_ge(l_par, 16 * 13)
                sp.wait_ge(l_src, 16)

            @block.scalar
            def _(act):
                def stored(i):
                    if i >= 0:
                        act.wait_ge(o_sp[i % 3], 16 * PARTS * (i // 3 + 1))

                def split0(i):
                    act.wait_ge(l_attr[i % 2], 16 * (i // 2 + 1))
                    stored(i - 3)
                    act.activation(part0[:, i % 3, :], araw[:, i % 2, :], ACT.Copy).then_inc(split_0, 1)
                split0(0)
                split0(1)
                for i in range(NPC):
                    act.wait_ge(rest_1, i + 1)
                    stored(i - 2)
                    act.activation(part12[:, 0, i % 2, :], ares[:, i % 2, :], ACT.Copy).then_inc(split_1, 1)
                    if i + 2 < NPC:
                        split0(i + 2)
                    act.wait_ge(rest_2, i + 1)
                    act.activation(part12[:, 1, i % 2, :], ares[:, i % 2, :], ACT.Copy).then_inc(split_2, 1)
                    if i in (2, 3):
                        h = i - 2
                        act.wait_ge(centred, h + 1)
                        act.activation(sum_sq[:, h * NH:(h + 1) * NH, :], x_all[:, h * NH:(h + 1) * NH, :],
                                       ACT.Square).then_inc(squared, 1)
                act.wait_ge(var_ok, 2)
                act.activation(rstd[:, :], rstd[:, :], ACT.Sqrt, bias=eps[:, :], scale=1.0 / C).then_inc(std_ok, 1)

            @block.gpsimd
            def _(g):
                g.memset(ident[:, :], 0.0).then_inc(c_pool, 1)
                g.memset(ones[:, :], 1.0).then_inc(c_pool, 1)
                g.wait_ge(c_pool, 2)
                g.affine_select(out=ident[:, :], in_=ident[:, :], compare_op=ALU.not_equal, fill=1.0,
                                base=0, pattern=[[-1, P]], channel_multiplier=1).then_inc(c_pool, 1)
                g.iota(iota_w[:, :], [[1, W]], base=0, channel_multiplier=0,
                       allow_small_or_imprecise_dtypes=True).then_inc(c_pool, 1)
                g.iota(pcol[:, :], [[0, 1]], base=-C, channel_multiplier=1,
                       allow_small_or_imprecise_dtypes=True).then_inc(c_pool, 1)
                g.memset(negrow[:, :], NEG).then_inc(c_pool, 1)
                g.memset(zrow[:, :], 0.0).then_inc(c_pool, 1)
                g.memset(eps[:, :], EPS).then_inc(c_pool, 1)
                g.memset(msg[:, :, :, C:C + 1], 1.0).then_inc(c_pool, 1)
                g.memset(acc[:, 2:SUP, :], 0.0).then_inc(c_pool, 1)
                def rest1(i):
                    g.wait_ge(split_0, i + 1)
                    if i >= 2:
                        g.wait_ge(split_2, i - 1)
                    g.tensor_tensor(ares[:, i % 2, :], araw[:, i % 2, :], part0[:, i % 3, :], ALU.subtract).then_inc(rest_1, 1)
                rest1(0)
                for i in range(NPC):
                    if i + 1 < NPC:
                        rest1(i + 1)
                    g.wait_ge(split_1, i + 1)
                    g.tensor_tensor(ares[:, i % 2, :], ares[:, i % 2, :], part12[:, 0, i % 2, :], ALU.subtract).then_inc(rest_2, 1)
                g.wait_ge(viol_ok, 2)
                g.partition_all_reduce(flag_f[:, 2:4], flag_f[:, 0:2], P, RMAX).then_inc(viol_all, 1)

            @block.tensor
            def _(pe):
                pe.wait_ge(c_pool, 10)
                pe.wait_ge(base_f_ok, 1)
                for h in range(2):
                    pe.matmul(bank[h][:, 0:SH], ones[0:1, :], base_f[:, h * SH:(h + 1) * SH],
                              start=True, stop=True).then_inc(base_mm, 1)

            @block.vector
            def _(dve):
                steps = [0]

                def link(ins):
                    steps[0] += 1
                    ins.then_inc(v, 1)
                    dve.wait_ge(v, steps[0])

                dve.wait_ge(l_we, 16)
                dve.wait_ge(c_pool, 10)
                dve.tensor_copy(we_p[:, 0, :], we_f).then_inc(we_ok, 1)
                dve.wait_ge(we_ok, 1)
                link(dve.tensor_tensor(we_r, we_f, we_p[:, 0, :], ALU.subtract))
                dve.tensor_copy(we_p[:, 1, :], we_r).then_inc(we_ok, 1)
                dve.wait_ge(we_ok, 2)
                link(dve.tensor_tensor(we_r, we_r, we_p[:, 1, :], ALU.subtract))
                dve.tensor_copy(we_p[:, 2, :], we_r).then_inc(we_ok, 1)
                for h in range(2):
                    t = slice(h * NH, (h + 1) * NH)
                    dve.wait_ge(l_x[h], 16)
                    link(dve.tensor_reduce(mean[:, t], x_all[:, t, :], AX, ALU.add))
                    link(dve.tensor_scalar(mean[:, t], mean[:, t], 1.0 / C, None, ALU.mult))
                    dve.tensor_tensor(x_all[:, t, :], x_all[:, t, :], mean[:, t].unsqueeze(2).to_broadcast([P, NH, C]),
                                      ALU.subtract).then_inc(centred, 1)
                dve.wait_ge(l_dst, 16)
                dst3 = dst_i.rearrange("p (s t) -> p s t", t=SUP)
                dve.tensor_copy(base_f, dst3[0:1, :, 0]).then_inc(base_f_ok, 1)
                link(dve.tensor_copy(base_i[:, :], dst3[0:1, :, 0]))
                for h in range(2):
                    dve.wait_ge(base_mm, h + 1)
                    s = slice(h * SH, (h + 1) * SH)
                    link(dve.tensor_scalar(winid[:, s], bank[h][:, 0:SH], pcol[:, :], None, ALU.add))
                    link(dve.tensor_tensor(dstrel[:, s, :], dst3[:, s, :],
                                           bank[h][:, 0:SH].unsqueeze(2).to_broadcast([P, SH, SUP]), ALU.subtract))
                dflat = dstrel[:, :, :].rearrange("p s t -> p (s t)")
                dve.tensor_reduce(flag_f[:, 0:1], dflat, AX, ALU.max).then_inc(viol_ok, 1)
                dve.tensor_reduce(flag_f[:, 1:2], dflat, AX, ALU.min, negate=True).then_inc(viol_ok, 1)
                for h in range(2):
                    t = slice(h * NH, (h + 1) * NH)
                    dve.wait_ge(squared, h + 1)
                    dve.tensor_reduce(rstd[:, t], sum_sq[:, t, :], AX, ALU.add).then_inc(var_ok, 1)
                dve.wait_ge(std_ok, 1)
                dve.reciprocal(rstd[:, :], rstd[:, :]).then_inc(v, 1)
                steps[0] += 1
                dve.wait_ge(viol_all, 1)
                link(dve.tensor_scalar(flag_f[:, 2:3], flag_f[:, 2:3], float(W - 1), None, ALU.is_le))
                link(dve.tensor_scalar(flag_f[:, 3:4], flag_f[:, 3:4], 0.0, None, ALU.is_le))
                link(dve.tensor_tensor(flag_f[:, 0:1], flag_f[:, 2:3], flag_f[:, 3:4], ALU.mult))
                link(dve.tensor_copy(flag_i[:, :], flag_f[0:1, 0:1]))

        nodes = Turns(NCH, 2, N // CH)
        h_sb = pre
        abuf = sq
        bbuf = gbuf[:, 0:2, :, :]

        def ps_chunk(b):
            return bank[b][:, 0:CT * C].rearrange("p (k f) -> p k f", k=CT)
        n_h = signal("n_h", 0)
        n_tr = signal("n_tr", 2)
        n_hT = signal("n_hT", 2)
        n_mlp = signal("n_mlp", 0)
        n_nf = signal("n_nf", 2)
        n_ab = signal("n_ab", 2)
        n_a = signal("n_a", 2)
        n_b = signal("n_b", 2)
        n_out = signal("n_out", 2)
        n_stat = sem("n_stat")
        o_ab = [sem("o_ab0"), sem("o_ab1")]
        o_pad = sem("o_pad")
        n_v = sem("n_v")
        n_std = sem("n_std")
        NSTAT = -(-N // CH)
        a_rows = a_tab.rearrange("(c k p) f -> c p k f", k=CT, p=P)
        b_rows = b_tab.rearrange("(c k p) f -> c p k f", k=CT, p=P)

        def node_h(dve, i, k):
            if nodes.absent(i, k):
                return
            c = 2 * i + k
            dve.wait_ge(n_tr.sem, n_tr.at(c - 2))
            dve.scalar_tensor_tensor(h_sb[:, k, :, :], x_all[:, bass.ds(c * CT, CT), :], 0.0,
                                     rstd[:, bass.ds(c * CT, CT)].unsqueeze(2).to_broadcast([P, CT, C]),
                                     ALU.max, ALU.mult).then_inc(n_h.sem, 1)

        def node_transpose(pe, i, k):
            if nodes.absent(i, k):
                return
            c = 2 * i + k
            pe.wait_ge(n_h.sem, n_h.at(c))
            pe.wait_ge(n_hT.sem, n_hT.at(c - 2))
            for t in range(CT):
                ins = pe.transpose(bank[k][0:C, t * P:(t + 1) * P], h_sb[:, k, t, :], ident[:, :])
            ins.then_inc(n_tr.sem, 1)

        def node_copy(act, i, k):
            if nodes.absent(i, k):
                return
            c = 2 * i + k
            act.wait_ge(n_tr.sem, n_tr.at(c))
            act.wait_ge(n_ab.sem, n_ab.at(c - 2))
            act.activation(lhs[0:C, k, :], bank[k][0:C, :], ACT.Copy).then_inc(n_hT.sem, 1)

        def node_products(pe, i, k):
            if nodes.absent(i, k):
                return
            c = 2 * i + k
            pe.wait_ge(n_hT.sem, n_hT.at(c))
            pe.wait_ge(n_nf.sem, n_nf.at(c - 2))
            pe.matmul(bank[2 + k][0:C, :], wnode[:, :], lhs[0:C, k, :], start=True, stop=True).then_inc(n_mlp.sem, 1)
            pe.wait_ge(n_a.sem, n_a.at(c - 2))
            pe.wait_ge(n_b.sem, n_b.at(c - 2))
            for t in range(CT):
                rows = lhs[0:C, k, t * P:(t + 1) * P]
                pe.matmul(ps_chunk(4 + k)[:, t, :], rows, wab[:, 0:C], start=True, stop=True)
                ins = pe.matmul(ps_chunk(6 + k)[:, t, :], rows, wab[:, C:2 * C], start=True, stop=True)
            ins.then_inc(n_ab.sem, 1)

        def node_relu(act, i, k):
            if nodes.absent(i, k):
                return
            c = 2 * i + k
            act.wait_ge(n_mlp.sem, n_mlp.at(c))
            act.activation(nf[0:C, bass.ds(c * CH, CH)], bank[2 + k][0:C, :], ACT.Relu,
                           bias=par[:, B_NODE:B_NODE + 1]).then_inc(n_nf.sem, 1)

        def node_src_rows(act, i, k):
            if nodes.absent(i, k):
                return
            c = 2 * i + k
            act.wait_ge(n_ab.sem, n_ab.at(c))
            act.wait_ge(n_out.sem, n_out.at(c - 2))
            act.activation(abuf[:, k, :, :], ps_chunk(4 + k), ACT.Copy).then_inc(n_a.sem, 1)

        def node_dst_rows(dve, i, k):
            if nodes.absent(i, k):
                return
            c = 2 * i + k
            dve.wait_ge(n_ab.sem, n_ab.at(c))
            dve.wait_ge(n_out.sem, n_out.at(c - 2))
            dve.tensor_copy(bbuf[:, k, :, :], ps_chunk(6 + k)).then_inc(n_b.sem, 1)

        def node_stats(dve, i, k):
            if nodes.absent(i, k):
                return
            c = 2 * i + k
            cols = min(CH, N - c * CH) if isinstance(i, int) else CH
            if cols > 0:
                dve.wait_ge(n_nf.sem, n_nf.at(c))
                dve.bn_stats(nstat[:, c, :], nf[0:C, bass.ds(c * CH, cols)]).then_inc(n_stat, 1)

        def node_store(sp, i, k):
            if nodes.absent(i, k):
                return
            c = 2 * i + k
            sp.wait_ge(n_a.sem, n_a.at(c))
            sp.wait_ge(n_b.sem, n_b.at(c))
            sp.sem_inc(sp_turn, 1)
            sp.dma_start(a_rows[c], abuf[:, k, :, :]).then_inc(o_ab[k], 16)
            sp.dma_start(b_rows[c], bbuf[:, k, :, :]).then_inc(o_ab[k], 16)

        def node_stored(sp, i, k):
            if nodes.absent(i, k):
                return
            sp.wait_ge(o_ab[k], i * 32 + 32)
            sp.sem_inc(n_out.sem, 1)

        with nc.Block() as block:
            @block.vector
            def _(dve):
                n_b.start(dve)

                def step(i, k):
                    node_h(dve, i, k)
                    node_dst_rows(dve, *nodes.earlier(i, k, 2))
                    node_stats(dve, *nodes.earlier(i, k, 2))
                nodes.run(dve, step, 2)
                dve.wait_ge(n_stat, NSTAT)
                dve.bn_aggr(agg2[:, 2:4], nstat[:, 0:NSTAT, :].rearrange("p c k -> p (c k)")).then_inc(n_v, 1)
                n = [1]

                def link(ins):
                    n[0] += 1
                    ins.then_inc(n_v, 1)
                    dve.wait_ge(n_v, n[0])

                def col(c):
                    return aff[:, c:c + 1]
                dve.wait_ge(n_std, 1)
                link(dve.reciprocal(col(TMP1), col(TMP0)))
                link(dve.tensor_tensor(col(S_N), col(TMP1), par[:, G_NODE:G_NODE + 1], ALU.mult))
                link(dve.tensor_tensor(col(TMP2), agg2[:, 2:3], col(S_N), ALU.mult))
                link(dve.tensor_tensor(col(T_N), par[:, T_NODE:T_NODE + 1], col(TMP2), ALU.subtract))

            @block.tensor
            def _(pe):
                n_tr.start(pe)
                n_ab.start(pe)

                def step(i, k):
                    node_transpose(pe, i, k)
                    node_products(pe, *nodes.earlier(i, k, 1))
                nodes.run(pe, step, 1)

            @block.scalar
            def _(act):
                n_hT.start(act)
                n_nf.start(act)
                n_a.start(act)

                def step(i, k):
                    node_copy(act, i, k)
                    node_relu(act, *nodes.earlier(i, k, 1))
                    node_src_rows(act, *nodes.earlier(i, k, 1))
                nodes.run(act, step, 1)
                act.wait_ge(n_v, 1)
                act.activation(aff[:, TMP0:TMP0 + 1], agg2[:, 3:4], ACT.Sqrt, bias=eps[0:C, :]).then_inc(n_std, 1)

            @block.sync
            def _(sp):
                n_out.start(sp)

                def step(i, k):
                    node_store(sp, i, k)
                    node_stored(sp, *nodes.earlier(i, k, 1))
                nodes.run(sp, step, 1)
                sp.dma_start(a_tab[N:N + 1, :], negrow[:, :]).then_inc(o_pad, 16)
                sp.wait_ge(o_pad, 16)

        HG = 4
        EG = 32
        NQ = EG // HG
        NX = EG // SPILL
        ek = x_flat[0:KR, 0:4 * ES].bitcast(BF16).rearrange("p (b s e) -> p b s e", b=2, e=ES)
        er = x_flat[0:C, 4 * ES:8 * ES].rearrange("p (b e) -> p b e", b=2)
        estat = sT[0:C, 0:S * 6].rearrange("p (s k) -> p s k", k=6)
        attr_rows = attr_parts.rearrange("i k e -> (i k) e")
        SV = -(-E // ES)
        ITER = (SV - 1) // EG
        e_land = [sem("e_land0"), sem("e_land1")]
        e_mm = signal("e_mm", 2 * HG)
        e_relu = signal("e_relu", 2)
        e_stat = signal("e_stat", 4)
        x_idx = signal("x_idx", 0)
        x_land = [sem(f"x_land{j}") for j in range(NX)]
        x_st = [sem("x_st0"), sem("x_st1")]
        x_out = signal("x_out", NX)
        e_v = sem("e_v")
        e_std = sem("e_std")
        cst_mm = sem("cst_mm")
        SREST = SV - ITER * EG

        with nc.Block() as block:
            def load_rows(sp, i, q):
                b = q % 2
                sp.wait_ge(e_mm.sem, e_mm.at(i * EG + (q - 1) * HG - 1))
                sp.sem_inc(sp_turn, 1)
                for j in range(PARTS):
                    r = j * PARTS * KE
                    sp.dma_start(ek[r:r + PARTS * KE, b, :, :].rearrange("p s e -> p (s e)"),
                                 attr_rows[:, bass.ds((i * EG + q * HG) * ES, HG * ES)]).then_inc(e_land[b], 16)

            def spill_indices(act, i, j):
                n = NX * i + j
                act.wait_ge(x_out.sem, x_out.at(n - NX))
                act.activation(idxb[:, j, :], src_i[:, bass.ds(n * (SPILL * SUP) + (SPILL - 1) * SUP, SUP)],
                               ACT.Copy).then_inc(x_idx.sem, 1)

            def spill_gather(g, i, j):
                n = NX * i + j
                g.wait_ge(x_idx.sem, x_idx.at(n))
                g.wait_ge(x_out.sem, x_out.at(n - NX))
                g.sem_inc(pool_turn, 1)
                for t in range(SUP):
                    g.indirect_dma_start(gbuf[:, j, t, :], None, a_tab[:, :],
                                         bass.IndirectOffsetOnAxis(ap=idxb[:, j, t:t + 1], axis=0)).then_inc(x_land[j], 16)

            def spill_store(sp, i, j):
                sp.wait_ge(x_land[j], i * (16 * SUP) + 16 * SUP)
                sp.sem_inc(sp_turn, 1)
                sp.dma_start(spilled[NX * i + j], gbuf[:, j, :, :].rearrange("p t c -> p (t c)")).then_inc(x_st[j % 2], 16)

            def spill_stored(sp, i, j):
                sp.wait_ge(x_st[j % 2], (i * (NX // 2) + j // 2 + 1) * 16)
                sp.sem_inc(x_out.sem, 1)

            def spill_step(sp, i, q):
                lag = 2 if q % 2 else 3
                at_i, j = i + (q // 2 - lag) // NX, (q // 2 - lag) % NX
                if isinstance(at_i, int) and not 0 <= NX * at_i + j < NSPILL:
                    return
                (spill_store if q % 2 else spill_stored)(sp, at_i, j)

            @block.gpsimd
            def _(g):
                with g.Fori(0, NSPILL // NX) as i:
                    for j in range(NX):
                        spill_gather(g, i, j)
                for j in range(NSPILL % NX):
                    spill_gather(g, NSPILL // NX, j)

            @block.sync
            def _(sp):
                x_out.start(sp)
                for q in range(NQ):
                    load_rows(sp, 0, q)
                    spill_step(sp, 0, q)
                with sp.Fori(1, ITER) as i:
                    for q in range(NQ):
                        load_rows(sp, i, q)
                        spill_step(sp, i, q)
                for q in range(2 * (NSPILL - ITER * NX + 3)):
                    if q * HG < SREST:
                        load_rows(sp, ITER, q)
                    spill_step(sp, ITER, q)

            def product(pe, i, k):
                q = k // HG
                if k % HG == 0:
                    pe.wait_ge(e_land[q % 2], (i * (NQ // 2) + q // 2 + 1) * (16 * PARTS))
                if k % 2 == 0:
                    pe.wait_ge(e_relu.sem, e_relu.at(i * (EG // 2) + k // 2 - 2))
                pe.matmul(bank[k % 4][0:C, :], w36[:, :], ek[:, q % 2, k % HG, :],
                          start=True, stop=True).then_inc(e_mm.sem, 1)

            @block.tensor
            def _(pe):
                e_mm.start(pe)
                with pe.Fori(0, ITER) as i:
                    for k in range(EG):
                        product(pe, i, k)
                for k in range(SREST):
                    product(pe, ITER, k)
                pe.wait_ge(e_v, 6)
                pe.matmul(bank[7][:, 0:C], trep[0:C, :], w3[:, :], start=True, stop=False)
                pe.matmul(bank[7][:, 0:C], ones[0:1, :], bm_row[:, :], start=False, stop=True).then_inc(cst_mm, 1)

            def relu_pair(act, i, k, n):
                act.wait_ge(e_mm.sem, e_mm.at(i * EG + k + n - 1))
                act.wait_ge(e_stat.sem, e_stat.at(i * EG + k - 3))
                act.activation(er[:, (k // 2) % 2, 0:n * ES], psum[0:C, (k % 4) * ES:(k % 4 + n) * ES], ACT.Relu,
                               bias=par[:, B_EDGE:B_EDGE + 1]).then_inc(e_relu.sem, 1)

            @block.scalar
            def _(act):
                e_relu.start(act)
                with act.Fori(0, ITER) as i:
                    for k in range(0, EG, 2):
                        if k % SPILL == 0:
                            spill_indices(act, i, k // SPILL)
                        relu_pair(act, i, k, 2)
                for k in range(0, max(SREST, (NSPILL - NX * ITER) * SPILL), 2):
                    n = NX * ITER + k // SPILL
                    if k % SPILL == 0 and n < NSPILL:
                        spill_indices(act, n // NX, n % NX)
                    if k < SREST:
                        relu_pair(act, ITER, k, min(2, SREST - k))
                act.wait_ge(e_v, 1)
                act.activation(aff[:, TMP0:TMP0 + 1], agg2[:, 1:2], ACT.Sqrt, bias=eps[0:C, :]).then_inc(e_std, 1)

            def stats(dve, i, k, cols):
                if k % 2 == 0:
                    dve.wait_ge(e_relu.sem, e_relu.at(i * (EG // 2) + k // 2))
                dve.bn_stats(estat[:, i * EG + k, :],
                             er[:, (k // 2) % 2, (k % 2) * ES:(k % 2) * ES + cols]).then_inc(e_stat.sem, 1)

            @block.vector
            def _(dve):
                e_stat.start(dve)
                with dve.Fori(0, ITER) as i:
                    for k in range(EG):
                        stats(dve, i, k, ES)
                for k in range(SREST):
                    stats(dve, ITER, k, min(ES, E - (ITER * EG + k) * ES))
                dve.wait_ge(e_stat.sem, e_stat.at(SV - 1))
                dve.bn_aggr(agg2[:, 0:2], sT[0:C, 0:SV * 6]).then_inc(e_v, 1)
                dve.wait_ge(e_std, 1)
                n = [1]

                def link(ins):
                    n[0] += 1
                    ins.then_inc(e_v, 1)
                    dve.wait_ge(e_v, n[0])
                def col(c):
                    return aff[:, c:c + 1]
                link(dve.reciprocal(col(TMP1), col(TMP0)))
                link(dve.tensor_tensor(col(S_E), col(TMP1), par[:, G_EDGE:G_EDGE + 1], ALU.mult))
                link(dve.tensor_tensor(col(TMP2), agg2[:, 0:1], col(S_E), ALU.mult))
                link(dve.tensor_tensor(col(T_E), par[:, T_EDGE:T_EDGE + 1], col(TMP2), ALU.subtract))
                link(dve.tensor_scalar(trep[0:C, :], ones[0:C, :], col(T_E), None, ALU.mult))
                for b in range(2):
                    link(dve.tensor_scalar(rhs[0:C, b, :], w3[:, :], col(S_E), None, ALU.mult))
                dve.wait_ge(cst_mm, 1)
                link(dve.tensor_copy(cstb[:, :], bank[7][:, 0:C]))


        HP = 2
        g_land = [sem(f"g_land{k}") for k in range(4)]
        r_land = [sem(f"r_land{k}") for k in range(2)]
        d_land = [sem(f"d_land{k}") for k in range(2)]
        msgs = Turns(S, SPILL)
        wraw = x_flat[:, 6 * ES:6 * ES + 2 * C].rearrange("p (b c) -> p b c", b=2)
        x_load = sem("x_load")
        w_ok = signal("w_ok", 2)
        w_land = [sem(f"w_land{k}") for k in range(2)]
        idx_ok = signal("idx_ok", 0)
        r_mm = signal("r_mm", 4)
        r_ok = signal("r_ok", 2)
        ohT_ok = signal("ohT_ok", 4)
        oh_ok = signal("oh_ok", 0)
        m_mm = signal("m_mm", 2)
        m_pre = signal("m_pre", 4)
        m_ok = signal("m_ok", 2)
        m_sq = signal("m_sq", 2)
        m_acc = signal("m_acc", 2)
        s_mm = signal("s_mm", 4)
        s_add = signal("s_add", 2)

        def ps_r(k):
            return bank[k % 2][0:C, :]

        def ps_m(k):
            return bank[2 + k % 2][:, 0:SUP * C].rearrange("p (t c) -> p t c", t=SUP)

        def ps_s(k):
            return bank[4 + k % 2][0:C + 1, 0:W]

        def copy_indices(act, i, k):
            if msgs.absent(i, k) or k == SPILL - 1:
                return
            act.wait_ge(m_pre.sem, m_pre.at(SPILL * i + k - 4))
            act.activation(idxb[:, k % 4, :], src_i[:, bass.ds((SPILL * i + k) * SUP, SUP)], ACT.Copy).then_inc(idx_ok.sem, 1)

        def gather(g, i, k):
            if msgs.absent(i, k) or k == SPILL - 1:
                return
            g.wait_ge(idx_ok.sem, idx_ok.at((SPILL - 1) * i + k))
            g.wait_ge(m_pre.sem, m_pre.at(SPILL * i + k - 4))
            g.sem_inc(pool_turn, 1)
            for t in range(SUP):
                g.indirect_dma_start(gbuf[:, k % 4, t, :], None, a_tab[:, :],
                                     bass.IndirectOffsetOnAxis(ap=idxb[:, k % 4, t:t + 1], axis=0)).then_inc(g_land[k % 4], 16)

        def load_spilled(sp, i, k):
            if msgs.absent(i, k) or k != SPILL - 1:
                return
            sp.wait_ge(m_pre.sem, m_pre.at(SPILL * i + k - 4))
            sp.sem_inc(sp_turn, 1)
            sp.dma_start(gbuf[:, k % 4, :, :].rearrange("p t c -> p (t c)"), spilled[i]).then_inc(x_load, 16)

        def load_pair(sp, i, k):
            if msgs.absent(i, k):
                return
            if k % HP:
                return
            b = (k // HP) % 2
            e0 = (SPILL * i + k) * ES
            sp.wait_ge(r_mm.sem, r_mm.at(SPILL * i + k + 1 - 4))
            sp.sem_inc(sp_turn, 1)
            for j in range(PARTS):
                r = j * PARTS * KE
                sp.dma_start(rk[r:r + PARTS * KE, b, :, :].rearrange("p s e -> p (s e)"),
                             attr_rows[:, bass.ds(e0, HP * ES)]).then_inc(r_land[b], 16)
            sp.wait_ge(ohT_ok.sem, ohT_ok.at(SPILL * i + k + 1 - 4))
            sp.sem_inc(sp_turn, 1)
            sp.dma_start(dstbc[C:P, b, :, :].rearrange("p s e -> p (s e)"),
                         a["dst_row"][:, bass.ds(e0, HP * ES)].partition_broadcast(W)).then_inc(d_land[b], 16)

        def load_window(sp, i, k):
            if msgs.absent(i, k):
                return
            base = sp.value_load(base_i[:, bass.ds(SPILL * i + k, 1)], min_val=0, max_val=N - 1)
            sp.wait_ge(w_ok.sem, w_ok.at(SPILL * i + k - 2))
            sp.sem_inc(sp_turn, 1)
            sp.dma_start(wraw[C:P, k % 2, :], b_tab[bass.ds(base, W), :]).then_inc(w_land[k % 2], 16)

        def window_rows(dve, i, k):
            if msgs.absent(i, k):
                return
            dve.wait_ge(w_land[k % 2], i * (16 * SPILL // 2) + 16 * (k // 2) + 16)
            dve.wait_ge(m_mm.sem, m_mm.at(SPILL * i + k - 2))
            dve.tensor_tensor(rhs[C:P, k % 2, :], wraw[C:P, k % 2, :], cstb[C:P, :], ALU.add).then_inc(w_ok.sem, 1)

        def edge_product(pe, i, k):
            if msgs.absent(i, k):
                return
            if k % HP == 0:
                pe.wait_ge(r_land[(k // HP) % 2], (i * 2 + k // 4 + 1) * (16 * PARTS))
            pe.wait_ge(r_ok.sem, r_ok.at(SPILL * i + k - 2))
            pe.matmul(ps_r(k), w36[:, :], rk[:, (k // HP) % 2, k % HP, :], start=True, stop=True).then_inc(r_mm.sem, 1)

        def edge_relu(act, i, k):
            if msgs.absent(i, k):
                return
            act.wait_ge(r_mm.sem, r_mm.at(SPILL * i + k))
            act.wait_ge(m_mm.sem, m_mm.at(SPILL * i + k - 2))
            act.activation(lhs[0:C, k % 2, :], ps_r(k), ACT.Relu, bias=par[:, B_EDGE:B_EDGE + 1]).then_inc(r_ok.sem, 1)

        def onehot_T(dve, i, k):
            if msgs.absent(i, k):
                return
            if k % HP == 0:
                dve.wait_ge(d_land[(k // HP) % 2], (i * 2 + k // 4 + 1) * 16)
            dve.wait_ge(m_mm.sem, m_mm.at(SPILL * i + k - 2))
            dve.tensor_scalar(lhs[C:P, k % 2, :], dstbc[C:P, (k // HP) % 2, k % HP, :], winid[C:P, bass.ds(SPILL * i + k, 1)],
                              None, ALU.is_equal).then_inc(ohT_ok.sem, 1)

        def onehot(dve, i, k):
            if msgs.absent(i, k):
                return
            dve.wait_ge(s_mm.sem, s_mm.at(SPILL * i + k - 4))
            dve.tensor_tensor(oh[:, k % 4, :, :], iota_w[:, :].unsqueeze(1).to_broadcast([P, SUP, W]),
                              dstrel[:, bass.ds(SPILL * i + k, 1), :].rearrange("p s t -> p (s t)").unsqueeze(2).to_broadcast([P, SUP, W]),
                              ALU.is_equal).then_inc(oh_ok.sem, 1)

        def message_product(pe, i, k):
            if msgs.absent(i, k):
                return
            pe.wait_ge(r_ok.sem, r_ok.at(SPILL * i + k))
            pe.wait_ge(ohT_ok.sem, ohT_ok.at(SPILL * i + k))
            pe.wait_ge(w_ok.sem, w_ok.at(SPILL * i + k))
            pe.wait_ge(m_pre.sem, m_pre.at(SPILL * i + k - 2))
            for t in range(SUP):
                ins = pe.matmul(ps_m(k)[:, t, :], lhs[:, k % 2, t * TILE:(t + 1) * TILE], rhs[:, k % 2, :],
                                start=True, stop=True)
            ins.then_inc(m_mm.sem, 1)

        def add_gathered(dve, i, k):
            if msgs.absent(i, k):
                return
            dve.wait_ge(m_mm.sem, m_mm.at(SPILL * i + k))
            if k == SPILL - 1:
                dve.wait_ge(x_load, i * 16 + 16)
            elif k == 3:
                dve.wait_ge(g_land[k], i * (16 * SUP) + 16 * SUP)
            else:
                dve.wait_ge(g_land[k % 4], (i * 2 + k // 4 + 1) * (16 * SUP))
            dve.wait_ge(m_ok.sem, m_ok.at(SPILL * i + k - 2))
            dve.tensor_tensor(pre[:, k % 2, :, :], ps_m(k), gbuf[:, k % 4, :, :], ALU.add).then_inc(m_pre.sem, 1)

        def message_relu(act, i, k):
            if msgs.absent(i, k):
                return
            act.wait_ge(m_pre.sem, m_pre.at(SPILL * i + k))
            act.wait_ge(s_mm.sem, s_mm.at(SPILL * i + k - 2))
            act.wait_ge(m_sq.sem, m_sq.at(SPILL * i + k - 2))
            act.activation(msg[:, k % 2, :, 0:C], pre[:, k % 2, :, :], ACT.Relu).then_inc(m_ok.sem, 1)

        def square(act, i, k):
            if msgs.absent(i, k):
                return
            act.wait_ge(m_ok.sem, m_ok.at(SPILL * i + k))
            act.wait_ge(m_acc.sem, m_acc.at(SPILL * i + k - 2))
            act.activation(sq[:, k % 2, :, :], msg[:, k % 2, :, 0:C], ACT.Square).then_inc(m_sq.sem, 1)

        def accumulate(dve, i, k):
            if msgs.absent(i, k):
                return
            dve.wait_ge(m_sq.sem, m_sq.at(SPILL * i + k))
            dve.wait_ge(m_acc.sem, m_acc.at(SPILL * i + k - 1))
            dve.tensor_tensor(acc[:, :, :], acc[:, :, :], sq[:, k % 2, :, :], ALU.add).then_inc(m_acc.sem, 1)

        def sum_edges(pe, i, k):
            if msgs.absent(i, k):
                return
            pe.wait_ge(m_ok.sem, m_ok.at(SPILL * i + k))
            pe.wait_ge(oh_ok.sem, oh_ok.at(SPILL * i + k))
            pe.wait_ge(s_add.sem, s_add.at(SPILL * i + k - 2))
            for t in range(SUP):
                ins = pe.matmul(ps_s(k), msg[:, k % 2, t, :], oh[:, k % 4, t, :], start=(t == 0), stop=(t == SUP - 1))
            ins.then_inc(s_mm.sem, 1)

        def add_window(dve, i, k):
            if msgs.absent(i, k):
                return
            base = dve.value_load(base_i[:, bass.ds(SPILL * i + k, 1)], min_val=0, max_val=N - 1)
            dve.wait_ge(s_mm.sem, s_mm.at(SPILL * i + k))
            dve.wait_ge(s_add.sem, s_add.at(SPILL * i + k - 1))
            cols = sT[0:C + 1, bass.ds(base, W)]
            dve.tensor_tensor(cols, cols, ps_s(k), ALU.add).then_inc(s_add.sem, 1)


        y = gbuf[:, :, :, :].rearrange("p k t c -> p (k t c)")
        y_drow = y[:, 0:P].bitcast(I32)
        y_eq = y[:, P:2 * P]
        y_low = y[:, 2 * P:3 * P]
        y_both = y[:, 3 * P:4 * P]
        y_ga = y[:, 4 * P:4 * P + C]
        y_gb = y[:, 4 * P + C:4 * P + 2 * C]
        y_gs = y[:, 4 * P + 2 * C:4 * P + 3 * C + 1]
        YS = 4 * P + 3 * C + 1
        y_is, y_id, y_iw = (y[:, YS + j:YS + j + 1].bitcast(I32) for j in range(3))
        y_dst, y_rank, y_trash, y_w = (y[:, YS + j:YS + j + 1] for j in range(3, 7))
        y_msg = msg[:, 0, 0, :]

        def general_pass(tag, messages):
            table = a_tab if messages else t_tab
            y_zero = sem("y_zero" + tag)
            y_init = sem("y_init" + tag)
            y_load = sem("y_load" + tag)
            y_gath = sem("y_gath" + tag)
            y_scat = sem("y_scat" + tag)
            y_v = sem("y_v" + tag)
            y_pe = sem("y_pe" + tag)
            y_act = sem("y_act" + tag)
            z_load = sem("z_load" + tag)
            z_tr = sem("z_tr" + tag)
            z_copy = sem("z_copy" + tag)
            nload = 3 + (PARTS if messages else 0)
            ngath = 3 if messages else 2
            VSTEPS = 12 if messages else 9
            PSTEPS = 3 if messages else 1
            ASTEPS = 3
            ninit = 5

            with nc.Block() as block:
                @block.sync
                def _(sp):
                    sp.wait_ge(y_init, ninit)
                    sp.dma_start(s_tab.rearrange("(t p) f -> p t f", p=P),
                                 sT[:, 0:(NT + 1) * (C + 1)].rearrange("p (t f) -> p t f", f=C + 1)).then_inc(y_zero, 16)
                    sp.wait_ge(y_zero, 16)
                    with sp.Fori(0, T) as t:
                        sp.dma_start(y_is, a["src"][:, bass.ds(t, 1)]).then_inc(y_load, 16)
                        sp.dma_start(y_id, a["dst"][:, bass.ds(t, 1)]).then_inc(y_load, 16)
                        sp.dma_start(y_drow, a["dst_row"][:, bass.ds(t * TILE, TILE)].partition_broadcast(P)).then_inc(y_load, 16)
                        if messages:
                            for j in range(PARTS):
                                r = j * PARTS * KE
                                sp.dma_start(rk[r:r + PARTS * KE, 0, 0, 0:TILE],
                                             attr_rows[:, bass.ds(t * TILE, TILE)]).then_inc(y_load, 16)
                        sp.wait_ge(y_scat, t * 16 + 16)
                        sp.sem_inc(sp_turn, 1)
                    with sp.Fori(0, NT) as t:
                        sp.dma_start(y_gs, s_tab[bass.ds(t * P, P), :]).then_inc(z_load, 16)
                        sp.wait_ge(z_copy, t + 1)
                        sp.sem_inc(sp_turn, 1)

                @block.gpsimd
                def _(g):
                    g.memset(y_low, 1.0).then_inc(y_init, 1)
                    g.memset(sT[:, 0:(NT + 1) * (C + 1)], 0.0).then_inc(y_init, 1)
                    g.wait_ge(y_init, 2)
                    g.affine_select(out=y_low, in_=y_low, compare_op=ALU.is_gt, fill=0.0, base=0,
                                    pattern=[[-1, P]], channel_multiplier=1).then_inc(y_init, 1)
                    g.iota(y_trash, [[0, 1]], base=NP, channel_multiplier=1,
                           allow_small_or_imprecise_dtypes=True).then_inc(y_init, 1)
                    g.memset(acc[:, :, :], 0.0).then_inc(y_init, 1)
                    with g.Fori(0, T) as t:
                        g.wait_ge(y_load, t * (16 * nload) + 16 * nload)
                        g.sem_inc(pool_turn, 1)

                        def gather_rows(to, tab, idx):
                            g.indirect_dma_start(to, None, tab[:, :], bass.IndirectOffsetOnAxis(ap=idx, axis=0)).then_inc(y_gath, 16)
                        gather_rows(y_ga, table, y_is)
                        if messages:
                            gather_rows(y_gb, b_tab, y_id)
                        gather_rows(y_gs, s_tab, y_id)
                        g.wait_ge(y_v, t * VSTEPS + VSTEPS)
                        g.sem_inc(pool_turn, 1)
                        g.indirect_dma_start(s_tab[:, :], bass.IndirectOffsetOnAxis(ap=y_iw, axis=0), y_gs, None).then_inc(y_scat, 16)

                @block.vector
                def _(dve):
                    dve.wait_ge(y_init, ninit)
                    with dve.Fori(0, T) as t:
                        n = [0]

                        def link(ins):
                            n[0] += 1
                            ins.then_inc(y_v, 1)
                            dve.wait_ge(y_v, t * VSTEPS + n[0])
                        dve.wait_ge(y_load, t * (16 * nload) + 16 * nload)
                        link(dve.tensor_copy(y_dst, y_id))
                        link(dve.tensor_scalar(y_eq, y_drow, y_dst, None, ALU.is_equal))
                        link(dve.tensor_tensor(y_both, y_eq, y_low, ALU.mult))
                        link(dve.tensor_reduce(y_rank, y_both, AX, ALU.max))
                        link(dve.tensor_tensor(y_w, y_trash, y_dst, ALU.subtract))
                        link(dve.tensor_tensor(y_w, y_w, y_rank, ALU.mult))
                        link(dve.tensor_tensor(y_iw, y_w, y_dst, ALU.add))
                        dve.wait_ge(y_gath, t * (16 * ngath) + 16 * ngath)
                        if messages:
                            dve.wait_ge(y_pe, t * PSTEPS + 2)
                            link(dve.tensor_tensor(pre[:, 0, 0, :], bank[1][:, 0:C], y_ga, ALU.add))
                            link(dve.tensor_tensor(pre[:, 0, 0, :], pre[:, 0, 0, :], y_gb, ALU.add))
                            link(dve.tensor_tensor(pre[:, 0, 0, :], pre[:, 0, 0, :], cstb[:, :], ALU.add))
                            dve.wait_ge(y_act, t * ASTEPS + 3)
                            link(dve.tensor_tensor(acc[:, 0, :], acc[:, 0, :], sq[:, 0, 0, :], ALU.add))
                        else:
                            link(dve.tensor_copy(y_msg[:, 0:C], y_ga))
                        dve.wait_ge(y_pe, t * PSTEPS + PSTEPS)
                        link(dve.tensor_tensor(y_gs, bank[2][:, 0:C + 1], y_gs, ALU.add))

                @block.tensor
                def _(pe):
                    with pe.Fori(0, T) as t:
                        if messages:
                            pe.wait_ge(y_load, t * (16 * nload) + 16 * nload)
                            pe.matmul(bank[0][0:C, 0:TILE], w36[:, :], rk[:, 0, 0, 0:TILE], start=True, stop=True).then_inc(y_pe, 1)
                            pe.wait_ge(y_act, t * ASTEPS + 1)
                            pe.matmul(bank[1][:, 0:C], lhs[0:C, 0, 0:TILE], rhs[0:C, 0, :], start=True, stop=True).then_inc(y_pe, 1)
                            pe.wait_ge(y_act, t * ASTEPS + 2)
                        else:
                            pe.wait_ge(y_v, t * VSTEPS + 8)
                        pe.matmul(bank[2][:, 0:C + 1], y_eq, y_msg, start=True, stop=True).then_inc(y_pe, 1)
                    with pe.Fori(0, NT) as t:
                        pe.wait_ge(z_load, t * 16 + 16)
                        pe.transpose(bank[0][0:C + 1, 0:P], y_gs, ident[:, :]).then_inc(z_tr, 1)

                @block.scalar
                def _(act):
                    if messages:
                        with act.Fori(0, T) as t:
                            act.wait_ge(y_pe, t * PSTEPS + 1)
                            act.activation(lhs[0:C, 0, 0:TILE], bank[0][0:C, 0:TILE], ACT.Relu,
                                           bias=par[:, B_EDGE:B_EDGE + 1]).then_inc(y_act, 1)
                            act.wait_ge(y_v, t * VSTEPS + 10)
                            act.activation(y_msg[:, 0:C], pre[:, 0, 0, :], ACT.Relu).then_inc(y_act, 1)
                            act.wait_ge(y_act, t * ASTEPS + 2)
                            act.activation(sq[:, 0, 0, :], y_msg[:, 0:C], ACT.Square).then_inc(y_act, 1)
                    with act.Fori(0, NT) as t:
                        act.wait_ge(z_tr, t + 1)
                        act.activation(sT[0:C + 1, bass.ds(t * P, P)], bank[0][0:C + 1, 0:P], ACT.Copy).then_inc(z_copy, 1)

        windowed = nc.values_load(flag_i[:, :], min_val=0, max_val=1)
        m0 = sem("m0")
        with nc.If(windowed):
            with nc.Block() as block:
                @block.gpsimd
                def _(g):
                    def step(i, k):
                        gather(g, i, k)
                    msgs.run(g, step, 0)

                @block.sync
                def _(sp):
                    def step(i, k):
                        load_pair(sp, i, k)
                        load_window(sp, i, k)
                        load_spilled(sp, i, k)
                    msgs.run(sp, step, 0)

                @block.tensor
                def _(pe):
                    for x in (r_mm, m_mm, s_mm):
                        x.start(pe)
                    def step(i, k):
                        edge_product(pe, i, k)
                        message_product(pe, *msgs.earlier(i, k, 1))
                        sum_edges(pe, *msgs.earlier(i, k, 2))
                    msgs.run(pe, step, 2)

                @block.scalar
                def _(act):
                    for x in (r_ok, m_ok, m_sq):
                        x.start(act)
                    def step(i, k):
                        copy_indices(act, i, k)
                        edge_relu(act, *msgs.earlier(i, k, 2))
                        message_relu(act, *msgs.earlier(i, k, 3))
                        square(act, *msgs.earlier(i, k, 3))
                    msgs.run(act, step, 3)

                @block.vector
                def _(dve):
                    dve.memset(sT[:, 0:NP], 0.0).then_inc(m0, 1)
                    dve.memset(acc[:, :, :], 0.0).then_inc(m0, 1)
                    dve.wait_ge(m0, 2)
                    for x in (ohT_ok, w_ok, m_pre, m_acc, s_add):
                        x.start(dve)
                    def step(i, k):
                        onehot_T(dve, i, k)
                        window_rows(dve, i, k)
                        onehot(dve, i, k)
                        add_gathered(dve, *msgs.earlier(i, k, 1))
                        accumulate(dve, *msgs.earlier(i, k, 2))
                        add_window(dve, *msgs.earlier(i, k, 2))
                    msgs.run(dve, step, 2)
        with nc.Else():
            general_pass("_m", True)

        h2_all = nf[:, 0:NT * C].rearrange("p (t c) -> p t c", c=C)
        sq_all = sT[:, 0:NT * C].rearrange("p (t c) -> p t c", c=C)
        v_sb = lhs[0:C + 1, 0, :]
        v1_sb = lhs[0:C + 1, 1, :]
        tm_l = trep[0:C, 0:C + 1]
        mix = cstb[0:C + 1, :]
        m_row = bank[6][0:C + 1, 0:C]
        ps_x = bank[0][:, 0:CT * C].rearrange("p (k f) -> p k f", k=CT)
        ps_c = bank[1][:, 0:CT].unsqueeze(2)
        PADS = EP - E
        l_x2 = sem("l_x2")
        q_mm = sem("q_mm")
        q_v = sem("q_v")
        q_std = sem("q_std")
        q_row = sem("q_row")
        q_lhs = sem("q_lhs")
        p_v1 = signal("p_v1", 0)
        p_v = signal("p_v", 1)
        p_mm = signal("p_mm", 1)
        p_x1 = signal("p_x1", 1)
        p_row = sem("p_row")
        o_cnt = sem("o_cnt")
        p_c = sem("p_c")
        p_sq = sem("p_sq")
        p_var = sem("p_var")
        p_std = sem("p_std")
        p_h2 = sem("p_h2")
        p_xh = sem("p_xh")
        p_t2 = sem("p_t2")
        p_sum = sem("p_sum")
        o_t = sem("o_t")
        l_w5 = sem("l_w5")
        wc_mm = sem("wc_mm")
        wc_ok = sem("wc_ok")
        s_zero = sem("s_zero")
        t_rows = t_tab.rearrange("(t p) f -> p t f", p=P)

        with nc.Block() as block:
            @block.sync
            def _(sp):
                sp.dma_start(x_all[:, :, :], a["x"]).then_inc(l_x2, 16)
                sp.wait_ge(q_lhs, 3)
                sp.dma_start(cnt_row[:, :], sT[C:C + 1, 0:NP]).then_inc(o_cnt, 16)
                sp.wait_ge(p_t2, 1)
                sp.dma_start(t_rows, h2_all).then_inc(o_t, 16)
                sp.wait_ge(o_t, 16)
                sp.dma_start(t_tab[N:N + 1, :], zrow[:, :]).then_inc(o_t, 16)
                sp.wait_ge(o_t, 32)

            @block.vector
            def _(dve):
                n = [0]

                def link(ins):
                    n[0] += 1
                    ins.then_inc(q_v, 1)
                    dve.wait_ge(q_v, n[0])

                def col(c):
                    return aff[:, c:c + 1]
                link(dve.tensor_reduce(col(TMP0), sT[0:C, 0:N], AX, ALU.add))
                link(dve.tensor_scalar(col(TMP0), col(TMP0), 1.0 / E, None, ALU.mult))
                link(dve.tensor_tensor(col(TMP1), col(TMP0), col(TMP0), ALU.mult))
                dve.wait_ge(q_mm, 1)
                link(dve.scalar_tensor_tensor(col(TMP2), bank[7][0:C, 0:1], 1.0 / E, col(TMP1), ALU.mult, ALU.subtract))
                dve.tensor_scalar(col(TMP2), col(TMP2), 0.0, None, ALU.max).then_inc(q_row, 1)
                dve.wait_ge(q_std, 1)
                link(dve.reciprocal(col(TMP1), col(TMP3)))
                link(dve.memset(smc[:, :], 1.0))
                link(dve.tensor_tensor(smc[0:C, :], col(TMP1), par[:, G_MSG:G_MSG + 1], ALU.mult))
                link(dve.tensor_tensor(col(TMP2), col(TMP0), smc[0:C, :], ALU.mult))
                link(dve.memset(tm_l, 0.0))
                dve.tensor_tensor(tm_l[:, C:C + 1], par[:, T_MSG:T_MSG + 1], col(TMP2), ALU.subtract).then_inc(q_lhs, 1)
                link(dve.tensor_copy(mix[:, :], ident[0:C + 1, 0:C]))
                dve.wait_ge(q_lhs, 2)
                link(dve.tensor_copy(mix[C:C + 1, :], m_row[C:C + 1, :]))
                last = sT[C:C + 1, N - 1:N]
                link(dve.tensor_scalar(last, last, -float(PADS), None, ALU.add))
                dve.memset(v1_sb[C:C + 1, :], 0.0).then_inc(q_lhs, 1)
                dve.wait_ge(q_lhs, 3)
                dve.wait_ge(l_x2, 16)
                p_v.start(dve)
                p_x1.start(dve)
                with dve.Fori(0, NCH) as c:
                    dve.wait_ge(p_v1.sem, p_v1.at(c))
                    dve.wait_ge(p_mm.sem, p_mm.at(c - 1))
                    dve.scalar_tensor_tensor(v_sb, sT[0:C + 1, bass.ds(c * CH, CH)], smc[:, :], v1_sb,
                                             ALU.mult, ALU.add).then_inc(p_v.sem, 1)
                    dve.wait_ge(p_mm.sem, p_mm.at(c))
                    xs = x_all[:, bass.ds(c * CT, CT), :]
                    dve.tensor_tensor(xs, xs, ps_x, ALU.add)
                    dve.tensor_copy(dinv[:, bass.ds(c * CT, CT)], bank[1][:, 0:CT]).then_inc(p_x1.sem, 1)
                dve.wait_ge(p_x1.sem, p_x1.at(NCH - 1))
                dve.tensor_reduce(mean[:, :], x_all[:, :, :], AX, ALU.add).then_inc(p_sum, 1)
                dve.wait_ge(p_sum, 1)
                dve.tensor_scalar(mean[:, :], mean[:, :], 1.0 / C, None, ALU.mult).then_inc(p_sum, 1)
                dve.wait_ge(p_sum, 2)
                dve.tensor_tensor(h2_all, x_all[:, :, :], mean[:, :].unsqueeze(2).to_broadcast([P, NT, C]),
                                  ALU.subtract).then_inc(p_c, 1)
                dve.wait_ge(p_row, 1)
                dve.reciprocal(dinv[:, :], dinv[:, :]).then_inc(p_sum, 1)
                dve.wait_ge(p_sq, 1)
                dve.tensor_reduce(rstd[:, :], sq_all, AX, ALU.add).then_inc(p_var, 1)
                dve.wait_ge(p_std, 1)
                dve.reciprocal(rstd[:, :], rstd[:, :]).then_inc(p_sum, 1)
                dve.wait_ge(p_sum, 4)
                dve.wait_ge(p_c, 1)
                dve.scalar_tensor_tensor(h2_all, h2_all, 0.0, rstd[:, :].unsqueeze(2).to_broadcast([P, NT, C]),
                                         ALU.max, ALU.mult).then_inc(p_h2, 1)
                dve.wait_ge(p_h2, 1)
                dve.tensor_tensor(x_all[:, :, :], x_all[:, :, :], h2_all, ALU.add).then_inc(p_xh, 1)
                dve.wait_ge(p_xh, 1)
                dve.tensor_tensor(h2_all, h2_all, dinv[:, :].unsqueeze(2).to_broadcast([P, NT, C]),
                                  ALU.mult).then_inc(p_t2, 1)

            @block.tensor
            def _(pe):
                for t in range(SUP):
                    ins = pe.matmul(bank[7][0:C, 0:1], acc[:, t, :], ones[:, 0:1], start=(t == 0), stop=(t == SUP - 1))
                ins.then_inc(q_mm, 1)
                pe.wait_ge(q_lhs, 1)
                pe.matmul(m_row, tm_l, ident[0:C, 0:C], start=True, stop=True).then_inc(q_lhs, 1)
                pe.wait_ge(l_w5, 16 * 5)
                for j in range(3):
                    ins = pe.matmul(bank[5][0:C, 0:H], wgT[:, j, :], w1[:, j, :], start=(j == 0), stop=(j == 2))
                ins.then_inc(wc_mm, 1)
                p_mm.start(pe)
                with pe.Fori(0, NCH) as c:
                    pe.wait_ge(p_v.sem, p_v.at(c))
                    pe.wait_ge(p_x1.sem, p_x1.at(c - 1))
                    for k in range(CT):
                        pe.matmul(ps_x[:, k, :], v_sb[:, k * P:(k + 1) * P], mix[:, :], start=True, stop=True)
                        ins = pe.matmul(ps_c[:, k, :], v_sb[:, k * P:(k + 1) * P], ident[0:C + 1, C:C + 1], start=True, stop=True)
                    ins.then_inc(p_mm.sem, 1)

            @block.scalar
            def _(act):
                act.wait_ge(q_row, 1)
                act.activation(aff[:, TMP3:TMP3 + 1], aff[:, TMP2:TMP2 + 1], ACT.Sqrt, bias=eps[0:C, :]).then_inc(q_std, 1)
                act.wait_ge(wc_mm, 1)
                act.activation(wc[:, :], bank[5][0:C, 0:H], ACT.Copy).then_inc(wc_ok, 1)
                with act.Fori(0, NCH) as c:
                    act.wait_ge(p_v.sem, p_v.at(c - 1))
                    act.activation(v1_sb[0:C, :], nf[0:C, bass.ds(c * CH, CH)], ACT.Identity,
                                   bias=aff[:, T_N:T_N + 1], scale=aff[:, S_N:S_N + 1]).then_inc(p_v1.sem, 1)
                act.wait_ge(p_x1.sem, p_x1.at(NCH - 1))
                act.activation(dinv[:, :], dinv[:, :], ACT.Sqrt, bias=ones[:, 0:1]).then_inc(p_row, 1)
                act.wait_ge(p_c, 1)
                act.wait_ge(o_cnt, 16)
                act.activation(sq_all, h2_all, ACT.Square).then_inc(p_sq, 1)
                act.wait_ge(p_var, 1)
                act.activation(rstd[:, :], rstd[:, :], ACT.Sqrt, bias=eps[:, :], scale=1.0 / C).then_inc(p_std, 1)

            @block.gpsimd
            def _(g):
                g.dma_start(wgT[:, :, :], a["W_gcn_T"].rearrange("(j p) c -> p j c", p=C)).then_inc(l_w5, 16)
                g.dma_start(w1[:, :, :], a["W1"].rearrange("(j p) h -> p j h", p=C)).then_inc(l_w5, 16)
                g.dma_start(w2[0:H, :], a["W2"]).then_inc(l_w5, 16)
                g.dma_start(w2[H:H + 1, :], a["b2"]).then_inc(l_w5, 16)
                g.dma_start(b1c[:, :], a["b1"].rearrange("a h -> h a")).then_inc(l_w5, 16)
                g.wait_ge(l_w5, 16 * 5)
                g.wait_ge(p_var, 1)
                g.memset(sT[:, 0:NP], 0.0).then_inc(s_zero, 1)

        sums = Turns(S, 4)
        c_land = [sem(f"c_land{k}") for k in range(4)]
        c_idx = signal("c_idx", 0)
        c_oh = signal("c_oh", 0)
        c_mm = signal("c_mm", 4)
        c_add = signal("c_add", 2)

        def gcn_indices(act, i, k):
            if sums.absent(i, k):
                return
            act.wait_ge(c_mm.sem, c_mm.at(4 * i + k - 4))
            act.activation(idxb[:, k, :], src_i[:, bass.ds(16 * i + 4 * k, SUP)], ACT.Copy).then_inc(c_idx.sem, 1)

        def gcn_gather(g, i, k):
            if sums.absent(i, k):
                return
            g.wait_ge(c_idx.sem, c_idx.at(4 * i + k))
            g.wait_ge(c_mm.sem, c_mm.at(4 * i + k - 4))
            g.sem_inc(pool_turn, 1)
            for t in range(SUP):
                g.indirect_dma_start(gbuf[:, k, t, :], None, t_tab[:, :],
                                     bass.IndirectOffsetOnAxis(ap=idxb[:, k, t:t + 1], axis=0)).then_inc(c_land[k], 16)

        def gcn_onehot(dve, i, k):
            if sums.absent(i, k):
                return
            dve.wait_ge(c_mm.sem, c_mm.at(4 * i + k - 4))
            dve.tensor_tensor(oh[:, k, :, :], iota_w[:, :].unsqueeze(1).to_broadcast([P, SUP, W]),
                              dstrel[:, bass.ds(4 * i + k, 1), :].rearrange("p s t -> p (s t)").unsqueeze(2).to_broadcast([P, SUP, W]),
                              ALU.is_equal).then_inc(c_oh.sem, 1)

        def gcn_sum(pe, i, k):
            if sums.absent(i, k):
                return
            pe.wait_ge(c_land[k], i * (16 * SUP) + 16 * SUP)
            pe.wait_ge(c_oh.sem, c_oh.at(4 * i + k))
            pe.wait_ge(c_add.sem, c_add.at(4 * i + k - 2))
            for t in range(SUP):
                ins = pe.matmul(ps_s(k)[0:C, :], gbuf[:, k, t, :], oh[:, k, t, :], start=(t == 0), stop=(t == SUP - 1))
            ins.then_inc(c_mm.sem, 1)

        def gcn_add(dve, i, k):
            if sums.absent(i, k):
                return
            base = dve.value_load(base_i[:, bass.ds(4 * i + k, 1)], min_val=0, max_val=N - 1)
            dve.wait_ge(c_mm.sem, c_mm.at(4 * i + k))
            dve.wait_ge(c_add.sem, c_add.at(4 * i + k - 1))
            cols = sT[0:C, bass.ds(base, W)]
            dve.tensor_tensor(cols, cols, ps_s(k)[0:C, :], ALU.add).then_inc(c_add.sem, 1)

        with nc.If(windowed):
            with nc.Block() as block:
                @block.gpsimd
                def _(g):
                    def step(i, k):
                        gcn_gather(g, i, k)
                    sums.run(g, step, 0)

                @block.scalar
                def _(act):
                    def step(i, k):
                        gcn_indices(act, i, k)
                    sums.run(act, step, 0)

                @block.tensor
                def _(pe):
                    c_mm.start(pe)
                    def step(i, k):
                        gcn_sum(pe, i, k)
                    sums.run(pe, step, 0)

                @block.vector
                def _(dve):
                    c_add.start(dve)
                    def step(i, k):
                        gcn_onehot(dve, i, k)
                        gcn_add(dve, *sums.earlier(i, k, 1))
                    sums.run(dve, step, 1)
        with nc.Else():
            general_pass("_g", False)

        t2_sb = pre[:, 0, :, :]
        u_sb = lhs[0:C, 0, :]
        g_flat = gbuf[0:H, :, :, :].rearrange("p k t c -> p (k t c)")
        cnt_sb = g_flat[:, 0:CH]
        z1_sb = g_flat[:, CH:2 * CH]
        z_sb = lhs[0:H + 1, 1, :]
        o_sb = pre[:, 1, :, :]
        ps_o = bank[2][:, 0:CT * C].rearrange("p (k f) -> p k f", k=CT)
        f_cnt = sem("f_cnt")
        f_t2 = signal("f_t2", 0)
        f_tr = signal("f_tr", 1)
        f_u = signal("f_u", 1)
        f_z = signal("f_z", 1)
        f_sd = signal("f_sd", 0)
        f_di = signal("f_di", 0)
        f_z1 = signal("f_z1", 1)
        f_zr = signal("f_zr", 1)
        f_o = signal("f_o", 1)
        f_out = signal("f_out", 1)
        f_st = signal("f_st", 1)
        f_one = sem("f_one")
        o_out = sem("o_out")

        with nc.Block() as block:
            @block.sync
            def _(sp):
                f_st.start(sp)
                with sp.Fori(0, NCH) as c:
                    sp.wait_ge(f_z1.sem, f_z1.at(c - 1))
                    sp.sem_inc(sp_turn, 1)
                    sp.dma_start(cnt_sb, cnt_row[:, bass.ds(c * CH, CH)].partition_broadcast(H)).then_inc(f_cnt, 16)
                    sp.wait_ge(f_out.sem, f_out.at(c))
                    sp.sem_inc(sp_turn, 1)
                    sp.dma_start(out[:, bass.ds(c * CT, CT), :], o_sb).then_inc(o_out, 16)
                    sp.wait_ge(o_out, c * 16 + 16)
                    sp.sem_inc(f_st.sem, 1)

            @block.scalar
            def _(act):
                f_zr.start(act)
                with act.Fori(0, NCH) as c:
                    act.wait_ge(f_tr.sem, f_tr.at(c - 1))
                    act.activation(t2_sb, h2_all[:, bass.ds(c * CT, CT), :], ACT.Copy).then_inc(f_t2.sem, 1)
                    act.wait_ge(f_cnt, c * 16 + 16)
                    act.activation(cnt_sb, cnt_sb, ACT.Sqrt, bias=ones[0:H, 0:1]).then_inc(f_sd.sem, 1)
                    act.wait_ge(f_z1.sem, f_z1.at(c))
                    act.wait_ge(f_o.sem, f_o.at(c - 1))
                    act.activation(z_sb[0:H, :], z1_sb, ACT.Relu, bias=b1c[:, :]).then_inc(f_zr.sem, 1)

            @block.tensor
            def _(pe):
                f_tr.start(pe)
                f_z.start(pe)
                f_o.start(pe)
                pe.wait_ge(f_one, 1)
                with pe.Fori(0, NCH) as c:
                    pe.wait_ge(f_t2.sem, f_t2.at(c))
                    pe.wait_ge(f_u.sem, f_u.at(c - 1))
                    for k in range(CT):
                        ins = pe.transpose(bank[0][0:C, k * P:(k + 1) * P], t2_sb[:, k, :], ident[:, :])
                    ins.then_inc(f_tr.sem, 1)
                    pe.wait_ge(f_u.sem, f_u.at(c))
                    pe.wait_ge(f_z1.sem, f_z1.at(c - 1))
                    pe.matmul(bank[1][0:H, :], wc[:, :], u_sb, start=True, stop=True).then_inc(f_z.sem, 1)
                    pe.wait_ge(f_zr.sem, f_zr.at(c))
                    pe.wait_ge(f_out.sem, f_out.at(c - 1))
                    for k in range(CT):
                        ins = pe.matmul(ps_o[:, k, :], z_sb[:, k * P:(k + 1) * P], w2[:, :], start=True, stop=True)
                    ins.then_inc(f_o.sem, 1)

            @block.vector
            def _(dve):
                f_u.start(dve)
                f_z1.start(dve)
                f_out.start(dve)
                dve.memset(z_sb[H:H + 1, :], 1.0).then_inc(f_one, 1)
                with dve.Fori(0, NCH) as c:
                    dve.wait_ge(f_tr.sem, f_tr.at(c))
                    dve.wait_ge(f_z.sem, f_z.at(c - 1))
                    dve.tensor_tensor(u_sb, bank[0][0:C, :], sT[0:C, bass.ds(c * CH, CH)], ALU.add).then_inc(f_u.sem, 1)
                    dve.wait_ge(f_sd.sem, f_sd.at(c))
                    dve.reciprocal(cnt_sb, cnt_sb).then_inc(f_di.sem, 1)
                    dve.wait_ge(f_di.sem, f_di.at(c))
                    dve.wait_ge(f_z.sem, f_z.at(c))
                    dve.wait_ge(f_zr.sem, f_zr.at(c - 1))
                    dve.tensor_tensor(z1_sb, bank[1][0:H, :], cnt_sb, ALU.mult).then_inc(f_z1.sem, 1)
                    dve.wait_ge(f_o.sem, f_o.at(c))
                    dve.wait_ge(f_st.sem, f_st.at(c - 1))
                    dve.tensor_tensor(o_sb, ps_o, x_all[:, bass.ds(c * CT, CT), :], ALU.add).then_inc(f_out.sem, 1)

def lay_out(inputs):
    import numpy as np
    x = np.asarray(inputs["x"])
    src, dst = np.asarray(inputs["src"]), np.asarray(inputs["dst"])
    attr = np.asarray(inputs["edge_attr_4"])
    n, e = x.shape[0], src.shape[0]
    d = Dims(n, e)

    def nodes(v):
        pad = np.zeros((d.NP, v.shape[1]), v.dtype)
        pad[:n] = v
        return np.ascontiguousarray(pad.reshape(d.NT, P, -1).transpose(1, 0, 2))

    def edges(v, fill):
        pad = np.full(d.EP, fill, v.dtype)
        pad[:e] = v
        return pad

    attr_t = np.zeros((KE, d.EP), attr.dtype)
    attr_t[:, :e] = attr.T
    dst_p = edges(dst, n - 1)
    arrays = {
        "x": nodes(x),
        "src": np.ascontiguousarray(edges(src, n).reshape(d.T, P).T),
        "dst": np.ascontiguousarray(dst_p.reshape(d.T, P).T),
        "dst_row": dst_p.reshape(1, d.EP),
        "attr": attr_t,
    }
    for name, v in inputs.items():
        if name[:3] in ("L0_", "L1_"):
            v = np.asarray(v)
            arrays[name[7:]] = np.ascontiguousarray(v if v.ndim == 2 else v.reshape(1, -1))
    arrays["W_gcn_T"] = np.ascontiguousarray(arrays.pop("W_gcn").T)
    return d, arrays


def build(nc, d, arrays):
    a = {k: nc.dram_tensor(k, v.shape, mybir.dt.from_np(v.dtype), kind="ExternalInput").ap() for k, v in arrays.items()}
    out = nc.dram_tensor("out_0_dram", (P, d.NT, C), FP32, kind="ExternalOutput").ap()
    gnn_kernel(nc, d, a, out)


def unpack(o, n):
    import numpy as np
    return np.ascontiguousarray(np.asarray(o).transpose(1, 0, 2).reshape(-1, C)[:n])


def kernel(**inputs):
    import concourse.bacc as bacc
    from concourse.bass_utils import run_bass_kernel_spmd
    d, arrays = lay_out(inputs)
    nc = bacc.Bacc("TRN2", target_bir_lowering=False, num_devices=1)
    build(nc, d, arrays)
    r = run_bass_kernel_spmd(nc, [arrays], core_ids=[0])
    return unpack(r.results[0]["out_0_dram"], d.N)
```

```python
import concourse.bass as bass
from concourse import mybir
from contextlib import ExitStack

FP32 = mybir.dt.float32
BF16 = mybir.dt.bfloat16
I32 = mybir.dt.int32
ALU = mybir.AluOpType
ACT = mybir.ActivationFunctionType
AX = mybir.AxisListType.X
RMAX = bass.bass_isa.ReduceOp.max
RADD = bass.bass_isa.ReduceOp.add

C = 96
KE = 4
H = 32
P = 128
TILE = 128
SUP = 4
ES = TILE * SUP
W = P - C
CH = 512
CT = CH // P
PARTS = 3
KR = PARTS * PARTS * KE
EPS = 1e-5
SPILL = 6
NEG = -1e30


class Dims:

    def __init__(self, n, e):
        self.N, self.E = n, e
        self.NCH = -(-(n + W) // CH)
        self.NP = self.NCH * CH
        self.NT = self.NP // P
        self.SV = -(-e // ES)
        self.S = -(-self.SV // (2 * SPILL)) * 2 * SPILL
        self.EP = self.S * ES
        self.T = self.S * SUP


class Signal:

    def __init__(self, handle, ahead):
        self.sem, self.ahead = handle, ahead

    def start(self, engine):
        engine.sem_inc(self.sem, self.ahead)

    def at(self, item):
        return item + (1 + self.ahead)


class Turns:

    def __init__(self, count, unroll, plain=None):
        self.count, self.unroll = count, unroll
        self.loops = (count if plain is None else plain) // unroll

    def earlier(self, i, k, n):
        return i + (k - n) // self.unroll, (k - n) % self.unroll

    def absent(self, i, k):
        return isinstance(i, int) and not 0 <= self.unroll * i + k < self.count

    def run(self, engine, step, lag):
        first = max(1, -(-lag // self.unroll))
        for k in range(first * self.unroll):
            step(k // self.unroll, k % self.unroll)
        with engine.Fori(first, self.loops) as i:
            for k in range(self.unroll):
                step(i, k)
        for k in range(self.count - self.loops * self.unroll + lag):
            step(self.loops + k // self.unroll, k % self.unroll)


def gnn_kernel(nc, d, a, out):
    N, E, NP, NT, NCH, SV, S, EP, T = d.N, d.E, d.NP, d.NT, d.NCH, d.SV, d.S, d.EP, d.T
    ctx = ExitStack()
    with ctx:
        ctx.enter_context(nc.allow_non_contiguous_dma(reason="short rows of node tables and parameters"))

        def sb(name, shape, dt=FP32):
            return ctx.enter_context(nc.sbuf_tensor(name, shape, dt))

        def sem(name):
            return ctx.enter_context(nc.semaphore(name))

        def signal(name, ahead):
            return Signal(ctx.enter_context(nc.semaphore(name)), ahead)

        turn = sem("turn")

        def dram(name, shape, dt=FP32):
            return nc.dram_tensor(name, shape, dt, kind="Internal").ap()

        attr_parts = dram("attr_parts", (PARTS, KE, EP), BF16)
        w_parts = dram("w_parts", (PARTS, KE, C), BF16)
        a_tab = dram("a_tab", (NP, C))
        b_tab = dram("b_tab", (NP, C))
        t_tab = dram("t_tab", (NP, C))
        NSPILL = SV // SPILL
        spilled = dram("spilled", (NSPILL, P, SUP * C))
        s_tab = dram("s_tab", (NP + P, C + 1))

        x_all = sb("x_all", [P, NT, C])
        sT = sb("sT", [P, max(NP, (NT + 1) * (C + 1), 8 * KE * EP // P // 8, 6 * S)])
        nf = sb("nf", [P, max(NP, T + NT * C)])
        src_i = sb("src_i", [P, T], I32)
        dstrel = sb("dstrel", [P, S, SUP])
        winid = sb("winid", [P, S])
        base_i = sb("base_i", [1, S], I32)
        ident = sb("ident", [P, P])
        iota_w = sb("iota_w", [P, W])
        pcol = sb("pcol", [P, 1])
        ones = sb("ones", [P, P])
        flag_f = sb("flag_f", [P, 4])
        flag_i = sb("flag_i", [1, 1], I32)
        negrow = sb("negrow", [1, C])
        zrow = sb("zrow", [1, C])
        w36 = sb("w36", [KR, C], BF16)
        wnode = sb("wnode", [C, C])
        wab = sb("wab", [C, 2 * C])
        w3 = sb("w3", [C, C])
        bm_row = sb("bm_row", [1, C])
        par = sb("par", [C, 8])
        B_NODE, G_NODE, T_NODE, B_EDGE, G_EDGE, T_EDGE, G_MSG, T_MSG = range(8)
        eps = sb("eps", [P, 1])
        cstb = sb("cstb", [P, C])
        aff = sb("aff", [C, 16])
        S_E, T_E, S_N, T_N, S_M, T_M, TMP0, TMP1, TMP2, TMP3 = range(10)
        rstd = sb("rstd", [P, NT])
        mean = sb("mean", [P, NT])
        nstat = sb("nstat", [C, NCH, 6])
        agg2 = sb("agg2", [C, 4])
        sdeg = sb("sdeg", [P, NT])
        dinv = sb("dinv", [P, NT])
        smc = sb("smc", [C + 1, 1])
        wgT = sb("wgT", [C, 3, C])
        w1 = sb("w1", [C, 3, H])
        w2 = sb("w2", [H + 1, C])
        wc = sb("wc", [C + 1, H + 1])
        trep = sb("trep", [C, P])
        gbuf = sb("gbuf", [P, 4, SUP, C])
        idxb = sb("idxb", [P, 4, SUP], I32)
        lhs = sb("lhs", [P, 2, ES])
        rhs = sb("rhs", [P, 2, C])
        pre = sb("pre", [P, 2, SUP, C])
        msg = sb("msg", [P, 2, SUP, C + 1])
        sq = sb("sq", [P, 2, SUP, C])
        acc = sb("acc", [P, SUP, C])
        oh = sb("oh", [P, 4, SUP, W])
        psum = ctx.enter_context(nc.psum_tensor("psum", [P, 8 * 512], FP32))
        bank = [psum[:, i * 512:(i + 1) * 512] for i in range(8)]

        x_flat = x_all[:, :, :].rearrange("p t c -> p (t c)")
        rk = x_flat[0:KR, 0:2 * ES].bitcast(BF16).rearrange("p (b s e) -> p b s e", b=2, e=ES)
        dstbc = x_flat[:, 2 * ES:6 * ES].bitcast(I32).rearrange("p (b s e) -> p b s e", b=2, e=ES)
        dst_i = nf[:, 0:T].bitcast(I32)
        sum_sq = nf[:, T:T + NT * C].rearrange("p (t c) -> p t c", c=C)
        NPC = 8
        AC = KE * EP // P // NPC
        araw = sT[:, 0:2 * AC].rearrange("p (b f) -> p b f", b=2)
        ares = sT[:, 2 * AC:4 * AC].rearrange("p (b f) -> p b f", b=2)
        part0 = sT[:, 4 * AC:4 * AC + 3 * AC // 2].bitcast(BF16).rearrange("p (b f) -> p b f", b=3)
        part12 = sT[:, 4 * AC + 3 * AC // 2:4 * AC + 7 * AC // 2].bitcast(BF16).rearrange("p (i b f) -> p i b f", i=2, b=2)
        attr_in = a["attr"].rearrange("k e -> (k e)").rearrange("(p q f) -> q p f", p=P, q=NPC)
        attr_out = [attr_parts[j].rearrange("k e -> (k e)").rearrange("(p q f) -> q p f", p=P, q=NPC)
                    for j in range(PARTS)]

        l_par = sem("l_par")
        l_dst = sem("l_dst")
        l_src = sem("l_src")
        l_x = [sem("l_x0"), sem("l_x1")]
        l_attr = [sem("l_attr0"), sem("l_attr1")]
        l_we = sem("l_we")
        o_wp = sem("o_wp")
        l_w36 = sem("l_w36")
        o_sp = [sem("o_sp0"), sem("o_sp1"), sem("o_sp2")]
        split_0 = sem("split_0")
        split_1 = sem("split_1")
        split_2 = sem("split_2")
        rest_1 = sem("rest_1")
        rest_2 = sem("rest_2")
        c_pool = sem("c_pool")
        v = sem("v")
        base_f_ok = sem("base_f_ok")
        base_mm = sem("base_mm")
        viol_ok = sem("viol_ok")
        viol_all = sem("viol_all")
        centred = sem("centred")
        squared = sem("squared")
        var_ok = sem("var_ok")
        std_ok = sem("std_ok")
        we_ok = sem("we_ok")

        base_f = lhs[0:1, :, :].rearrange("p a b -> p (a b)")[:, 0:S]
        we_f = trep[0:KE, 0:C]
        we_r = cstb[0:KE, 0:C]
        we_p = acc[0:KE, 0:2, :].rearrange("p a b -> p (a b)").bitcast(BF16)[:, 0:PARTS * C].rearrange("p (i c) -> p i c", i=PARTS)
        SH = S // 2
        NH = NT // 2

        with nc.Block() as block:
            @block.sync
            def _(sp):
                sp.dma_start(dst_i[:, :], a["dst"]).then_inc(l_dst, 16)
                sp.dma_start(we_f, a["W_edge"]).then_inc(l_we, 16)
                for h in range(2):
                    sp.dma_start(x_all[:, h * NH:(h + 1) * NH, :], a["x"][:, h * NH:(h + 1) * NH, :]).then_inc(l_x[h], 16)
                for i in range(2):
                    sp.dma_start(araw[:, i, :], attr_in[i]).then_inc(l_attr[i], 16)
                sp.dma_start(src_i[:, :], a["src"]).then_inc(l_src, 16)
                sp.dma_start(wnode[:, :], a["W_node"]).then_inc(l_par, 16)
                sp.dma_start(wab[:, 0:C], a["W_msg"][0:C, :]).then_inc(l_par, 16)
                sp.dma_start(wab[:, C:2 * C], a["W_msg"][C:2 * C, :]).then_inc(l_par, 16)
                sp.dma_start(w3[:, :], a["W_msg"][2 * C:3 * C, :]).then_inc(l_par, 16)
                sp.dma_start(bm_row[:, :], a["b_msg"]).then_inc(l_par, 16)
                for j, name in enumerate(("b_node", "g_node", "beta_node", "b_edge", "g_edge", "beta_edge", "g_msg", "beta_msg")):
                    sp.dma_start(par[:, j:j + 1], a[name].rearrange("a c -> c a")).then_inc(l_par, 16)
                sp.wait_ge(we_ok, 3)
                sp.dma_start(w_parts.rearrange("i k c -> k i c"), we_p).then_inc(o_wp, 16)
                sp.wait_ge(o_wp, 16)
                for j in range(PARTS):
                    for i in range(PARTS):
                        r = (j * PARTS + i) * KE
                        sp.dma_start(w36[r:r + KE, :], w_parts[j]).then_inc(l_w36, 16)
                for i in range(NPC):
                    if i + 2 < NPC:
                        sp.wait_ge(rest_1, i + 1)
                        sp.dma_start(araw[:, i % 2, :], attr_in[i + 2]).then_inc(l_attr[i % 2], 16)
                    sp.wait_ge(split_2, i + 1)
                    for j, part in enumerate((part0[:, i % 3, :], part12[:, 0, i % 2, :], part12[:, 1, i % 2, :])):
                        sp.dma_start(attr_out[j][i], part).then_inc(o_sp[i % 3], 16)
                for b in range(3):
                    sp.wait_ge(o_sp[b], 16 * PARTS * len(range(b, NPC, 3)))
                sp.wait_ge(l_w36, 16 * PARTS * PARTS)
                sp.wait_ge(l_par, 16 * 13)
                sp.wait_ge(l_src, 16)

            @block.scalar
            def _(act):
                def stored(i):
                    if i >= 0:
                        act.wait_ge(o_sp[i % 3], 16 * PARTS * (i // 3 + 1))

                def split0(i):
                    act.wait_ge(l_attr[i % 2], 16 * (i // 2 + 1))
                    stored(i - 3)
                    act.activation(part0[:, i % 3, :], araw[:, i % 2, :], ACT.Copy).then_inc(split_0, 1)
                split0(0)
                split0(1)
                for i in range(NPC):
                    act.wait_ge(rest_1, i + 1)
                    stored(i - 2)
                    act.activation(part12[:, 0, i % 2, :], ares[:, i % 2, :], ACT.Copy).then_inc(split_1, 1)
                    if i + 2 < NPC:
                        split0(i + 2)
                    act.wait_ge(rest_2, i + 1)
                    act.activation(part12[:, 1, i % 2, :], ares[:, i % 2, :], ACT.Copy).then_inc(split_2, 1)
                    if i in (2, 3):
                        h = i - 2
                        act.wait_ge(centred, h + 1)
                        act.activation(sum_sq[:, h * NH:(h + 1) * NH, :], x_all[:, h * NH:(h + 1) * NH, :],
                                       ACT.Square).then_inc(squared, 1)
                act.wait_ge(var_ok, 2)
                act.activation(rstd[:, :], rstd[:, :], ACT.Sqrt, bias=eps[:, :], scale=1.0 / C).then_inc(std_ok, 1)

            @block.gpsimd
            def _(g):
                g.memset(ident[:, :], 0.0).then_inc(c_pool, 1)
                g.memset(ones[:, :], 1.0).then_inc(c_pool, 1)
                g.wait_ge(c_pool, 2)
                g.affine_select(out=ident[:, :], in_=ident[:, :], compare_op=ALU.not_equal, fill=1.0,
                                base=0, pattern=[[-1, P]], channel_multiplier=1).then_inc(c_pool, 1)
                g.iota(iota_w[:, :], [[1, W]], base=0, channel_multiplier=0,
                       allow_small_or_imprecise_dtypes=True).then_inc(c_pool, 1)
                g.iota(pcol[:, :], [[0, 1]], base=-C, channel_multiplier=1,
                       allow_small_or_imprecise_dtypes=True).then_inc(c_pool, 1)
                g.memset(negrow[:, :], NEG).then_inc(c_pool, 1)
                g.memset(zrow[:, :], 0.0).then_inc(c_pool, 1)
                g.memset(eps[:, :], EPS).then_inc(c_pool, 1)
                g.memset(msg[:, :, :, C:C + 1], 1.0).then_inc(c_pool, 1)
                g.memset(acc[:, 2:SUP, :], 0.0).then_inc(c_pool, 1)
                def rest1(i):
                    g.wait_ge(split_0, i + 1)
                    if i >= 2:
                        g.wait_ge(split_2, i - 1)
                    g.tensor_tensor(ares[:, i % 2, :], araw[:, i % 2, :], part0[:, i % 3, :], ALU.subtract).then_inc(rest_1, 1)
                rest1(0)
                for i in range(NPC):
                    if i + 1 < NPC:
                        rest1(i + 1)
                    g.wait_ge(split_1, i + 1)
                    g.tensor_tensor(ares[:, i % 2, :], ares[:, i % 2, :], part12[:, 0, i % 2, :], ALU.subtract).then_inc(rest_2, 1)
                g.wait_ge(viol_ok, 2)
                g.partition_all_reduce(flag_f[:, 2:4], flag_f[:, 0:2], P, RMAX).then_inc(viol_all, 1)

            @block.tensor
            def _(pe):
                pe.wait_ge(c_pool, 10)
                pe.wait_ge(base_f_ok, 1)
                for h in range(2):
                    pe.matmul(bank[h][:, 0:SH], ones[0:1, :], base_f[:, h * SH:(h + 1) * SH],
                              start=True, stop=True).then_inc(base_mm, 1)

            @block.vector
            def _(dve):
                steps = [0]

                def link(ins):
                    steps[0] += 1
                    ins.then_inc(v, 1)
                    dve.wait_ge(v, steps[0])

                dve.wait_ge(l_we, 16)
                dve.wait_ge(c_pool, 10)
                dve.tensor_copy(we_p[:, 0, :], we_f).then_inc(we_ok, 1)
                dve.wait_ge(we_ok, 1)
                link(dve.tensor_tensor(we_r, we_f, we_p[:, 0, :], ALU.subtract))
                dve.tensor_copy(we_p[:, 1, :], we_r).then_inc(we_ok, 1)
                dve.wait_ge(we_ok, 2)
                link(dve.tensor_tensor(we_r, we_r, we_p[:, 1, :], ALU.subtract))
                dve.tensor_copy(we_p[:, 2, :], we_r).then_inc(we_ok, 1)
                for h in range(2):
                    t = slice(h * NH, (h + 1) * NH)
                    dve.wait_ge(l_x[h], 16)
                    link(dve.tensor_reduce(mean[:, t], x_all[:, t, :], AX, ALU.add))
                    link(dve.tensor_scalar(mean[:, t], mean[:, t], 1.0 / C, None, ALU.mult))
                    dve.tensor_tensor(x_all[:, t, :], x_all[:, t, :], mean[:, t].unsqueeze(2).to_broadcast([P, NH, C]),
                                      ALU.subtract).then_inc(centred, 1)
                dve.wait_ge(l_dst, 16)
                dst3 = dst_i.rearrange("p (s t) -> p s t", t=SUP)
                dve.tensor_copy(base_f, dst3[0:1, :, 0]).then_inc(base_f_ok, 1)
                link(dve.tensor_copy(base_i[:, :], dst3[0:1, :, 0]))
                for h in range(2):
                    dve.wait_ge(base_mm, h + 1)
                    s = slice(h * SH, (h + 1) * SH)
                    link(dve.tensor_scalar(winid[:, s], bank[h][:, 0:SH], pcol[:, :], None, ALU.add))
                    link(dve.tensor_tensor(dstrel[:, s, :], dst3[:, s, :],
                                           bank[h][:, 0:SH].unsqueeze(2).to_broadcast([P, SH, SUP]), ALU.subtract))
                dflat = dstrel[:, :, :].rearrange("p s t -> p (s t)")
                dve.tensor_reduce(flag_f[:, 0:1], dflat, AX, ALU.max).then_inc(viol_ok, 1)
                dve.tensor_reduce(flag_f[:, 1:2], dflat, AX, ALU.min, negate=True).then_inc(viol_ok, 1)
                for h in range(2):
                    t = slice(h * NH, (h + 1) * NH)
                    dve.wait_ge(squared, h + 1)
                    dve.tensor_reduce(rstd[:, t], sum_sq[:, t, :], AX, ALU.add).then_inc(var_ok, 1)
                dve.wait_ge(std_ok, 1)
                dve.reciprocal(rstd[:, :], rstd[:, :]).then_inc(v, 1)
                steps[0] += 1
                dve.wait_ge(viol_all, 1)
                link(dve.tensor_scalar(flag_f[:, 2:3], flag_f[:, 2:3], float(W - 1), None, ALU.is_le))
                link(dve.tensor_scalar(flag_f[:, 3:4], flag_f[:, 3:4], 0.0, None, ALU.is_le))
                link(dve.tensor_tensor(flag_f[:, 0:1], flag_f[:, 2:3], flag_f[:, 3:4], ALU.mult))
                link(dve.tensor_copy(flag_i[:, :], flag_f[0:1, 0:1]))

        nodes = Turns(NCH, 2, N // CH)
        h_sb = pre
        abuf = sq
        bbuf = gbuf[:, 0:2, :, :]

        def ps_chunk(b):
            return bank[b][:, 0:CT * C].rearrange("p (k f) -> p k f", k=CT)
        n_h = signal("n_h", 0)
        n_tr = signal("n_tr", 2)
        n_hT = signal("n_hT", 2)
        n_mlp = signal("n_mlp", 0)
        n_nf = signal("n_nf", 2)
        n_ab = signal("n_ab", 2)
        n_a = signal("n_a", 2)
        n_b = signal("n_b", 2)
        n_out = signal("n_out", 2)
        n_stat = sem("n_stat")
        o_ab = [sem("o_ab0"), sem("o_ab1")]
        o_pad = sem("o_pad")
        n_v = sem("n_v")
        n_std = sem("n_std")
        NSTAT = -(-N // CH)
        a_rows = a_tab.rearrange("(c k p) f -> c p k f", k=CT, p=P)
        b_rows = b_tab.rearrange("(c k p) f -> c p k f", k=CT, p=P)

        def node_h(dve, i, k):
            if nodes.absent(i, k):
                return
            c = 2 * i + k
            dve.wait_ge(n_tr.sem, n_tr.at(c - 2))
            dve.scalar_tensor_tensor(h_sb[:, k, :, :], x_all[:, bass.ds(c * CT, CT), :], 0.0,
                                     rstd[:, bass.ds(c * CT, CT)].unsqueeze(2).to_broadcast([P, CT, C]),
                                     ALU.max, ALU.mult).then_inc(n_h.sem, 1)

        def node_transpose(pe, i, k):
            if nodes.absent(i, k):
                return
            c = 2 * i + k
            pe.wait_ge(n_h.sem, n_h.at(c))
            pe.wait_ge(n_hT.sem, n_hT.at(c - 2))
            for t in range(CT):
                ins = pe.transpose(bank[k][0:C, t * P:(t + 1) * P], h_sb[:, k, t, :], ident[:, :])
            ins.then_inc(n_tr.sem, 1)

        def node_copy(act, i, k):
            if nodes.absent(i, k):
                return
            c = 2 * i + k
            act.wait_ge(n_tr.sem, n_tr.at(c))
            act.wait_ge(n_ab.sem, n_ab.at(c - 2))
            act.activation(lhs[0:C, k, :], bank[k][0:C, :], ACT.Copy).then_inc(n_hT.sem, 1)

        def node_products(pe, i, k):
            if nodes.absent(i, k):
                return
            c = 2 * i + k
            pe.wait_ge(n_hT.sem, n_hT.at(c))
            pe.wait_ge(n_nf.sem, n_nf.at(c - 2))
            pe.matmul(bank[2 + k][0:C, :], wnode[:, :], lhs[0:C, k, :], start=True, stop=True).then_inc(n_mlp.sem, 1)
            pe.wait_ge(n_a.sem, n_a.at(c - 2))
            pe.wait_ge(n_b.sem, n_b.at(c - 2))
            for t in range(CT):
                rows = lhs[0:C, k, t * P:(t + 1) * P]
                pe.matmul(ps_chunk(4 + k)[:, t, :], rows, wab[:, 0:C], start=True, stop=True)
                ins = pe.matmul(ps_chunk(6 + k)[:, t, :], rows, wab[:, C:2 * C], start=True, stop=True)
            ins.then_inc(n_ab.sem, 1)

        def node_relu(act, i, k):
            if nodes.absent(i, k):
                return
            c = 2 * i + k
            act.wait_ge(n_mlp.sem, n_mlp.at(c))
            act.activation(nf[0:C, bass.ds(c * CH, CH)], bank[2 + k][0:C, :], ACT.Relu,
                           bias=par[:, B_NODE:B_NODE + 1]).then_inc(n_nf.sem, 1)

        def node_src_rows(act, i, k):
            if nodes.absent(i, k):
                return
            c = 2 * i + k
            act.wait_ge(n_ab.sem, n_ab.at(c))
            act.wait_ge(n_out.sem, n_out.at(c - 2))
            act.activation(abuf[:, k, :, :], ps_chunk(4 + k), ACT.Copy).then_inc(n_a.sem, 1)

        def node_dst_rows(dve, i, k):
            if nodes.absent(i, k):
                return
            c = 2 * i + k
            dve.wait_ge(n_ab.sem, n_ab.at(c))
            dve.wait_ge(n_out.sem, n_out.at(c - 2))
            dve.tensor_copy(bbuf[:, k, :, :], ps_chunk(6 + k)).then_inc(n_b.sem, 1)

        def node_stats(dve, i, k):
            if nodes.absent(i, k):
                return
            c = 2 * i + k
            cols = min(CH, N - c * CH) if isinstance(i, int) else CH
            if cols > 0:
                dve.wait_ge(n_nf.sem, n_nf.at(c))
                dve.bn_stats(nstat[:, c, :], nf[0:C, bass.ds(c * CH, cols)]).then_inc(n_stat, 1)

        def node_store(sp, i, k):
            if nodes.absent(i, k):
                return
            c = 2 * i + k
            sp.wait_ge(n_a.sem, n_a.at(c))
            sp.wait_ge(n_b.sem, n_b.at(c))
            sp.sem_inc(turn, 1)
            sp.dma_start(a_rows[c], abuf[:, k, :, :]).then_inc(o_ab[k], 16)
            sp.dma_start(b_rows[c], bbuf[:, k, :, :]).then_inc(o_ab[k], 16)

        def node_stored(sp, i, k):
            if nodes.absent(i, k):
                return
            sp.wait_ge(o_ab[k], i * 32 + 32)
            sp.sem_inc(n_out.sem, 1)

        with nc.Block() as block:
            @block.vector
            def _(dve):
                n_b.start(dve)

                def step(i, k):
                    node_h(dve, i, k)
                    node_dst_rows(dve, *nodes.earlier(i, k, 2))
                    node_stats(dve, *nodes.earlier(i, k, 2))
                nodes.run(dve, step, 2)
                dve.wait_ge(n_stat, NSTAT)
                dve.bn_aggr(agg2[:, 2:4], nstat[:, 0:NSTAT, :].rearrange("p c k -> p (c k)")).then_inc(n_v, 1)
                n = [1]

                def link(ins):
                    n[0] += 1
                    ins.then_inc(n_v, 1)
                    dve.wait_ge(n_v, n[0])

                def col(c):
                    return aff[:, c:c + 1]
                dve.wait_ge(n_std, 1)
                link(dve.reciprocal(col(TMP1), col(TMP0)))
                link(dve.tensor_tensor(col(S_N), col(TMP1), par[:, G_NODE:G_NODE + 1], ALU.mult))
                link(dve.tensor_tensor(col(TMP2), agg2[:, 2:3], col(S_N), ALU.mult))
                link(dve.tensor_tensor(col(T_N), par[:, T_NODE:T_NODE + 1], col(TMP2), ALU.subtract))

            @block.tensor
            def _(pe):
                n_tr.start(pe)
                n_ab.start(pe)

                def step(i, k):
                    node_transpose(pe, i, k)
                    node_products(pe, *nodes.earlier(i, k, 1))
                nodes.run(pe, step, 1)

            @block.scalar
            def _(act):
                n_hT.start(act)
                n_nf.start(act)
                n_a.start(act)

                def step(i, k):
                    node_copy(act, i, k)
                    node_relu(act, *nodes.earlier(i, k, 1))
                    node_src_rows(act, *nodes.earlier(i, k, 1))
                nodes.run(act, step, 1)
                act.wait_ge(n_v, 1)
                act.activation(aff[:, TMP0:TMP0 + 1], agg2[:, 3:4], ACT.Sqrt, bias=eps[0:C, :]).then_inc(n_std, 1)

            @block.sync
            def _(sp):
                n_out.start(sp)

                def step(i, k):
                    node_store(sp, i, k)
                    node_stored(sp, *nodes.earlier(i, k, 1))
                nodes.run(sp, step, 1)
                sp.dma_start(a_tab[N:N + 1, :], negrow[:, :]).then_inc(o_pad, 16)
                sp.wait_ge(o_pad, 16)

        HG = SPILL // 2
        EG = 4 * SPILL
        NQ = EG // HG
        NB = 4
        NX = EG // SPILL
        ek = x_flat[0:KR, 0:NB * HG * ES // 2].bitcast(BF16).rearrange("p (b s e) -> p b s e", b=NB, e=ES)
        er = x_flat[0:C, NB * HG * ES // 2:NB * HG * ES // 2 + 4 * ES].rearrange("p (b e) -> p b e", b=2)
        estat = sT[0:C, 0:S * 6].rearrange("p (s k) -> p s k", k=6)
        attr_rows = attr_parts.rearrange("i k e -> (i k) e")
        ITER = (SV - 1) // EG
        e_land = [sem(f"e_land{b}") for b in range(NB)]
        e_mm = signal("e_mm", NB * HG)
        e_relu = signal("e_relu", 2)
        e_stat = signal("e_stat", 4)
        x_idx = signal("x_idx", 0)
        x_land = [sem(f"x_land{j}") for j in range(NX)]
        x_st = [sem("x_st0"), sem("x_st1")]
        x_out = signal("x_out", NX)
        e_v = sem("e_v")
        e_std = sem("e_std")
        cst_mm = sem("cst_mm")
        SREST = SV - ITER * EG

        with nc.Block() as block:
            def load_rows(sp, i, q):
                b = q % NB
                sp.wait_ge(e_mm.sem, e_mm.at(i * EG + (q + 1 - NB) * HG - 1))
                sp.sem_inc(turn, 1)
                for j in range(PARTS):
                    r = j * PARTS * KE
                    sp.dma_start(ek[r:r + PARTS * KE, b, :, :].rearrange("p s e -> p (s e)"),
                                 attr_rows[:, bass.ds((i * EG + q * HG) * ES, HG * ES)]).then_inc(e_land[b], 16)

            def spill_indices(act, i, j):
                n = NX * i + j
                act.wait_ge(x_out.sem, x_out.at(n - NX))
                act.activation(idxb[:, j, :], src_i[:, bass.ds(n * (SPILL * SUP) + (SPILL - 1) * SUP, SUP)],
                               ACT.Copy).then_inc(x_idx.sem, 1)

            def spill_gather(g, i, j):
                n = NX * i + j
                g.wait_ge(x_idx.sem, x_idx.at(n))
                g.wait_ge(x_out.sem, x_out.at(n - NX))
                g.sem_inc(turn, 1)
                for t in range(SUP):
                    g.indirect_dma_start(gbuf[:, j, t, :], None, a_tab[:, :],
                                         bass.IndirectOffsetOnAxis(ap=idxb[:, j, t:t + 1], axis=0)).then_inc(x_land[j], 16)

            def spill_store(sp, i, j):
                sp.wait_ge(x_land[j], i * (16 * SUP) + 16 * SUP)
                sp.sem_inc(turn, 1)
                sp.dma_start(spilled[NX * i + j], gbuf[:, j, :, :].rearrange("p t c -> p (t c)")).then_inc(x_st[j % 2], 16)

            def spill_stored(sp, i, j):
                sp.wait_ge(x_st[j % 2], (i * (NX // 2) + j // 2 + 1) * 16)
                sp.sem_inc(x_out.sem, 1)

            def spill_step(sp, i, q):
                lag = 2 if q % 2 else 3
                at_i, j = i + (q // 2 - lag) // NX, (q // 2 - lag) % NX
                if isinstance(at_i, int) and not 0 <= NX * at_i + j < NSPILL:
                    return
                (spill_store if q % 2 else spill_stored)(sp, at_i, j)

            @block.gpsimd
            def _(g):
                with g.Fori(0, NSPILL // NX) as i:
                    for j in range(NX):
                        spill_gather(g, i, j)
                for j in range(NSPILL % NX):
                    spill_gather(g, NSPILL // NX, j)

            @block.sync
            def _(sp):
                x_out.start(sp)
                for q in range(NQ):
                    load_rows(sp, 0, q)
                    spill_step(sp, 0, q)
                with sp.Fori(1, ITER) as i:
                    for q in range(NQ):
                        load_rows(sp, i, q)
                        spill_step(sp, i, q)
                for q in range(max(NQ, 2 * (NSPILL - ITER * NX + 3))):
                    if q * HG < SREST:
                        load_rows(sp, ITER, q)
                    spill_step(sp, ITER, q)

            def product(pe, i, k):
                q = k // HG
                if k % HG == 0:
                    pe.wait_ge(e_land[q % NB], (i * (NQ // NB) + q // NB + 1) * (16 * PARTS))
                if k % 2 == 0:
                    pe.wait_ge(e_relu.sem, e_relu.at(i * (EG // 2) + k // 2 - 2))
                pe.matmul(bank[k % 4][0:C, :], w36[:, :], ek[:, q % NB, k % HG, :],
                          start=True, stop=True).then_inc(e_mm.sem, 1)

            @block.tensor
            def _(pe):
                e_mm.start(pe)
                with pe.Fori(0, ITER) as i:
                    for k in range(EG):
                        product(pe, i, k)
                for k in range(SREST):
                    product(pe, ITER, k)
                pe.wait_ge(e_v, 6)
                pe.matmul(bank[7][:, 0:C], trep[0:C, :], w3[:, :], start=True, stop=False)
                pe.matmul(bank[7][:, 0:C], ones[0:1, :], bm_row[:, :], start=False, stop=True).then_inc(cst_mm, 1)

            def relu_pair(act, i, k, n):
                act.wait_ge(e_mm.sem, e_mm.at(i * EG + k + n - 1))
                act.wait_ge(e_stat.sem, e_stat.at(i * EG + k - 3))
                act.activation(er[:, (k // 2) % 2, 0:n * ES], psum[0:C, (k % 4) * ES:(k % 4 + n) * ES], ACT.Relu,
                               bias=par[:, B_EDGE:B_EDGE + 1]).then_inc(e_relu.sem, 1)

            @block.scalar
            def _(act):
                e_relu.start(act)
                with act.Fori(0, ITER) as i:
                    for k in range(0, EG, 2):
                        if k % SPILL == 0:
                            spill_indices(act, i, k // SPILL)
                        relu_pair(act, i, k, 2)
                for k in range(0, max(SREST, (NSPILL - NX * ITER) * SPILL), 2):
                    n = NX * ITER + k // SPILL
                    if k % SPILL == 0 and n < NSPILL:
                        spill_indices(act, n // NX, n % NX)
                    if k < SREST:
                        relu_pair(act, ITER, k, min(2, SREST - k))
                act.wait_ge(e_v, 1)
                act.activation(aff[:, TMP0:TMP0 + 1], agg2[:, 1:2], ACT.Sqrt, bias=eps[0:C, :]).then_inc(e_std, 1)

            def stats(dve, i, k, cols):
                if k % 2 == 0:
                    dve.wait_ge(e_relu.sem, e_relu.at(i * (EG // 2) + k // 2))
                dve.bn_stats(estat[:, i * EG + k, :],
                             er[:, (k // 2) % 2, (k % 2) * ES:(k % 2) * ES + cols]).then_inc(e_stat.sem, 1)

            @block.vector
            def _(dve):
                e_stat.start(dve)
                with dve.Fori(0, ITER) as i:
                    for k in range(EG):
                        stats(dve, i, k, ES)
                for k in range(SREST):
                    stats(dve, ITER, k, min(ES, E - (ITER * EG + k) * ES))
                dve.wait_ge(e_stat.sem, e_stat.at(SV - 1))
                dve.bn_aggr(agg2[:, 0:2], sT[0:C, 0:SV * 6]).then_inc(e_v, 1)
                dve.wait_ge(e_std, 1)
                n = [1]

                def link(ins):
                    n[0] += 1
                    ins.then_inc(e_v, 1)
                    dve.wait_ge(e_v, n[0])
                def col(c):
                    return aff[:, c:c + 1]
                link(dve.reciprocal(col(TMP1), col(TMP0)))
                link(dve.tensor_tensor(col(S_E), col(TMP1), par[:, G_EDGE:G_EDGE + 1], ALU.mult))
                link(dve.tensor_tensor(col(TMP2), agg2[:, 0:1], col(S_E), ALU.mult))
                link(dve.tensor_tensor(col(T_E), par[:, T_EDGE:T_EDGE + 1], col(TMP2), ALU.subtract))
                link(dve.tensor_scalar(trep[0:C, :], ones[0:C, :], col(T_E), None, ALU.mult))
                for b in range(2):
                    link(dve.tensor_scalar(rhs[0:C, b, :], w3[:, :], col(S_E), None, ALU.mult))
                dve.wait_ge(cst_mm, 1)
                link(dve.tensor_copy(cstb[:, :], bank[7][:, 0:C]))


        HP = 2
        g_land = [sem(f"g_land{k}") for k in range(4)]
        r_land = [sem(f"r_land{k}") for k in range(2)]
        d_land = [sem(f"d_land{k}") for k in range(2)]
        MT = 2 * SPILL
        msgs = Turns(SV, MT)
        wraw = x_flat[:, 6 * ES:6 * ES + 2 * C].rearrange("p (b c) -> p b c", b=2)
        x_load = sem("x_load")
        w_ok = signal("w_ok", 2)
        w_land = [sem(f"w_land{k}") for k in range(2)]
        idx_ok = signal("idx_ok", 0)
        r_mm = signal("r_mm", 4)
        r_ok = signal("r_ok", 2)
        ohT_ok = signal("ohT_ok", 4)
        oh_ok = signal("oh_ok", 0)
        m_mm = signal("m_mm", 2)
        m_pre = signal("m_pre", 4)
        m_ok = signal("m_ok", 2)
        m_sq = signal("m_sq", 2)
        m_acc = signal("m_acc", 2)
        s_mm = signal("s_mm", 4)
        s_add = signal("s_add", 2)
        def was_spilled(k):
            return k % SPILL == SPILL - 1

        def gathers(k):
            return sum(not was_spilled(q) for q in range(k % 4, k + 1, 4))

        def gathered(i, k):
            return i * (16 * SUP * gathers(MT - 4 + k % 4)) + 16 * SUP * gathers(k)


        def ps_r(k):
            return bank[k % 2][0:C, :]

        def ps_m(k):
            return bank[2 + k % 2][:, 0:SUP * C].rearrange("p (t c) -> p t c", t=SUP)

        def ps_s(k):
            return bank[4 + k % 2][0:C + 1, 0:W]

        def copy_indices(act, i, k):
            if msgs.absent(i, k) or was_spilled(k):
                return
            act.wait_ge(m_pre.sem, m_pre.at(MT * i + k - 4))
            act.activation(idxb[:, k % 4, :], src_i[:, bass.ds((MT * i + k) * SUP, SUP)], ACT.Copy).then_inc(idx_ok.sem, 1)

        def gather(g, i, k):
            if msgs.absent(i, k) or was_spilled(k):
                return
            g.wait_ge(idx_ok.sem, idx_ok.at((MT - MT // SPILL) * i + k - k // SPILL))
            g.wait_ge(m_pre.sem, m_pre.at(MT * i + k - 4))
            g.sem_inc(turn, 1)
            for t in range(SUP):
                g.indirect_dma_start(gbuf[:, k % 4, t, :], None, a_tab[:, :],
                                     bass.IndirectOffsetOnAxis(ap=idxb[:, k % 4, t:t + 1], axis=0)).then_inc(g_land[k % 4], 16)

        def load_spilled(sp, i, k):
            if msgs.absent(i, k) or not was_spilled(k):
                return
            sp.wait_ge(m_pre.sem, m_pre.at(MT * i + k - 4))
            sp.sem_inc(turn, 1)
            sp.dma_start(gbuf[:, k % 4, :, :].rearrange("p t c -> p (t c)"), spilled[i * (MT // SPILL) + k // SPILL]).then_inc(x_load, 16)

        def load_pair(sp, i, k):
            if msgs.absent(i, k):
                return
            if k % HP:
                return
            b = (k // HP) % 2
            e0 = (MT * i + k) * ES
            sp.wait_ge(r_mm.sem, r_mm.at(MT * i + k + 1 - 4))
            sp.sem_inc(turn, 1)
            for j in range(PARTS):
                r = j * PARTS * KE
                sp.dma_start(rk[r:r + PARTS * KE, b, :, :].rearrange("p s e -> p (s e)"),
                             attr_rows[:, bass.ds(e0, HP * ES)]).then_inc(r_land[b], 16)
            sp.wait_ge(ohT_ok.sem, ohT_ok.at(MT * i + k + 1 - 4))
            sp.sem_inc(turn, 1)
            sp.dma_start(dstbc[C:P, b, :, :].rearrange("p s e -> p (s e)"),
                         a["dst_row"][:, bass.ds(e0, HP * ES)].partition_broadcast(W)).then_inc(d_land[b], 16)

        def load_window(sp, i, k):
            if msgs.absent(i, k):
                return
            base = sp.value_load(base_i[:, bass.ds(MT * i + k, 1)], min_val=0, max_val=N - 1)
            sp.wait_ge(w_ok.sem, w_ok.at(MT * i + k - 2))
            sp.sem_inc(turn, 1)
            sp.dma_start(wraw[C:P, k % 2, :], b_tab[bass.ds(base, W), :]).then_inc(w_land[k % 2], 16)

        def window_rows(dve, i, k):
            if msgs.absent(i, k):
                return
            dve.wait_ge(w_land[k % 2], i * (16 * MT // 2) + 16 * (k // 2) + 16)
            dve.wait_ge(m_mm.sem, m_mm.at(MT * i + k - 2))
            dve.tensor_tensor(rhs[C:P, k % 2, :], wraw[C:P, k % 2, :], cstb[C:P, :], ALU.add).then_inc(w_ok.sem, 1)

        def edge_product(pe, i, k):
            if msgs.absent(i, k):
                return
            if k % HP == 0:
                pe.wait_ge(r_land[(k // HP) % 2], (i * (MT // 4) + k // 4 + 1) * (16 * PARTS))
            pe.wait_ge(r_ok.sem, r_ok.at(MT * i + k - 2))
            pe.matmul(ps_r(k), w36[:, :], rk[:, (k // HP) % 2, k % HP, :], start=True, stop=True).then_inc(r_mm.sem, 1)

        def edge_relu(act, i, k):
            if msgs.absent(i, k):
                return
            act.wait_ge(r_mm.sem, r_mm.at(MT * i + k))
            act.wait_ge(m_mm.sem, m_mm.at(MT * i + k - 2))
            act.activation(lhs[0:C, k % 2, :], ps_r(k), ACT.Relu, bias=par[:, B_EDGE:B_EDGE + 1]).then_inc(r_ok.sem, 1)

        def onehot_T(dve, i, k):
            if msgs.absent(i, k):
                return
            if k % HP == 0:
                dve.wait_ge(d_land[(k // HP) % 2], (i * (MT // 4) + k // 4 + 1) * 16)
            dve.wait_ge(m_mm.sem, m_mm.at(MT * i + k - 2))
            dve.tensor_scalar(lhs[C:P, k % 2, :], dstbc[C:P, (k // HP) % 2, k % HP, :], winid[C:P, bass.ds(MT * i + k, 1)],
                              None, ALU.is_equal).then_inc(ohT_ok.sem, 1)

        def onehot(dve, i, k):
            if msgs.absent(i, k):
                return
            dve.wait_ge(s_mm.sem, s_mm.at(MT * i + k - 4))
            dve.tensor_tensor(oh[:, k % 4, :, :], iota_w[:, :].unsqueeze(1).to_broadcast([P, SUP, W]),
                              dstrel[:, bass.ds(MT * i + k, 1), :].rearrange("p s t -> p (s t)").unsqueeze(2).to_broadcast([P, SUP, W]),
                              ALU.is_equal).then_inc(oh_ok.sem, 1)

        def message_product(pe, i, k):
            if msgs.absent(i, k):
                return
            pe.wait_ge(r_ok.sem, r_ok.at(MT * i + k))
            pe.wait_ge(ohT_ok.sem, ohT_ok.at(MT * i + k))
            pe.wait_ge(w_ok.sem, w_ok.at(MT * i + k))
            pe.wait_ge(m_pre.sem, m_pre.at(MT * i + k - 2))
            for t in range(SUP):
                ins = pe.matmul(ps_m(k)[:, t, :], lhs[:, k % 2, t * TILE:(t + 1) * TILE], rhs[:, k % 2, :],
                                start=True, stop=True)
            ins.then_inc(m_mm.sem, 1)

        def add_gathered(dve, i, k):
            if msgs.absent(i, k):
                return
            dve.wait_ge(m_mm.sem, m_mm.at(MT * i + k))
            if was_spilled(k):
                dve.wait_ge(x_load, i * (16 * (MT // SPILL)) + 16 * (k // SPILL + 1))
            else:
                dve.wait_ge(g_land[k % 4], gathered(i, k))
            dve.wait_ge(m_ok.sem, m_ok.at(MT * i + k - 2))
            dve.tensor_tensor(pre[:, k % 2, :, :], ps_m(k), gbuf[:, k % 4, :, :], ALU.add).then_inc(m_pre.sem, 1)

        def message_relu(act, i, k):
            if msgs.absent(i, k):
                return
            act.wait_ge(m_pre.sem, m_pre.at(MT * i + k))
            act.wait_ge(s_mm.sem, s_mm.at(MT * i + k - 2))
            act.wait_ge(m_sq.sem, m_sq.at(MT * i + k - 2))
            act.activation(msg[:, k % 2, :, 0:C], pre[:, k % 2, :, :], ACT.Relu).then_inc(m_ok.sem, 1)

        def square(act, i, k):
            if msgs.absent(i, k):
                return
            act.wait_ge(m_ok.sem, m_ok.at(MT * i + k))
            act.wait_ge(m_acc.sem, m_acc.at(MT * i + k - 2))
            act.activation(sq[:, k % 2, :, :], msg[:, k % 2, :, 0:C], ACT.Square).then_inc(m_sq.sem, 1)

        def accumulate(dve, i, k):
            if msgs.absent(i, k):
                return
            dve.wait_ge(m_sq.sem, m_sq.at(MT * i + k))
            dve.wait_ge(m_acc.sem, m_acc.at(MT * i + k - 1))
            dve.tensor_tensor(acc[:, :, :], acc[:, :, :], sq[:, k % 2, :, :], ALU.add).then_inc(m_acc.sem, 1)

        def sum_edges(pe, i, k):
            if msgs.absent(i, k):
                return
            pe.wait_ge(m_ok.sem, m_ok.at(MT * i + k))
            pe.wait_ge(oh_ok.sem, oh_ok.at(MT * i + k))
            pe.wait_ge(s_add.sem, s_add.at(MT * i + k - 2))
            for t in range(SUP):
                ins = pe.matmul(ps_s(k), msg[:, k % 2, t, :], oh[:, k % 4, t, :], start=(t == 0), stop=(t == SUP - 1))
            ins.then_inc(s_mm.sem, 1)

        def add_window(dve, i, k):
            if msgs.absent(i, k):
                return
            base = dve.value_load(base_i[:, bass.ds(MT * i + k, 1)], min_val=0, max_val=N - 1)
            dve.wait_ge(s_mm.sem, s_mm.at(MT * i + k))
            dve.wait_ge(s_add.sem, s_add.at(MT * i + k - 1))
            cols = sT[0:C + 1, bass.ds(base, W)]
            dve.tensor_tensor(cols, cols, ps_s(k), ALU.add).then_inc(s_add.sem, 1)


        y = gbuf[:, :, :, :].rearrange("p k t c -> p (k t c)")
        y_drow = y[:, 0:P].bitcast(I32)
        y_eq = y[:, P:2 * P]
        y_low = y[:, 2 * P:3 * P]
        y_both = y[:, 3 * P:4 * P]
        y_ga = y[:, 4 * P:4 * P + C]
        y_gb = y[:, 4 * P + C:4 * P + 2 * C]
        y_gs = y[:, 4 * P + 2 * C:4 * P + 3 * C + 1]
        YS = 4 * P + 3 * C + 1
        y_is, y_id, y_iw = (y[:, YS + j:YS + j + 1].bitcast(I32) for j in range(3))
        y_dst, y_rank, y_trash, y_w = (y[:, YS + j:YS + j + 1] for j in range(3, 7))
        y_msg = msg[:, 0, 0, :]

        def general_pass(tag, messages):
            table = a_tab if messages else t_tab
            y_zero = sem("y_zero" + tag)
            y_init = sem("y_init" + tag)
            y_load = sem("y_load" + tag)
            y_gath = sem("y_gath" + tag)
            y_scat = sem("y_scat" + tag)
            y_v = sem("y_v" + tag)
            y_pe = sem("y_pe" + tag)
            y_act = sem("y_act" + tag)
            z_load = sem("z_load" + tag)
            z_tr = sem("z_tr" + tag)
            z_copy = sem("z_copy" + tag)
            nload = 3 + (PARTS if messages else 0)
            ngath = 3 if messages else 2
            VSTEPS = 12 if messages else 9
            PSTEPS = 3 if messages else 1
            ASTEPS = 3
            ninit = 5

            with nc.Block() as block:
                @block.sync
                def _(sp):
                    sp.wait_ge(y_init, ninit)
                    sp.dma_start(s_tab.rearrange("(t p) f -> p t f", p=P),
                                 sT[:, 0:(NT + 1) * (C + 1)].rearrange("p (t f) -> p t f", f=C + 1)).then_inc(y_zero, 16)
                    sp.wait_ge(y_zero, 16)
                    with sp.Fori(0, SV * SUP) as t:
                        sp.dma_start(y_is, a["src"][:, bass.ds(t, 1)]).then_inc(y_load, 16)
                        sp.dma_start(y_id, a["dst"][:, bass.ds(t, 1)]).then_inc(y_load, 16)
                        sp.dma_start(y_drow, a["dst_row"][:, bass.ds(t * TILE, TILE)].partition_broadcast(P)).then_inc(y_load, 16)
                        if messages:
                            for j in range(PARTS):
                                r = j * PARTS * KE
                                sp.dma_start(rk[r:r + PARTS * KE, 0, 0, 0:TILE],
                                             attr_rows[:, bass.ds(t * TILE, TILE)]).then_inc(y_load, 16)
                        sp.wait_ge(y_scat, t * 16 + 16)
                        sp.sem_inc(turn, 1)
                    with sp.Fori(0, NT) as t:
                        sp.dma_start(y_gs, s_tab[bass.ds(t * P, P), :]).then_inc(z_load, 16)
                        sp.wait_ge(z_copy, t + 1)
                        sp.sem_inc(turn, 1)

                @block.gpsimd
                def _(g):
                    g.memset(y_low, 1.0).then_inc(y_init, 1)
                    g.memset(sT[:, 0:(NT + 1) * (C + 1)], 0.0).then_inc(y_init, 1)
                    g.wait_ge(y_init, 2)
                    g.affine_select(out=y_low, in_=y_low, compare_op=ALU.is_gt, fill=0.0, base=0,
                                    pattern=[[-1, P]], channel_multiplier=1).then_inc(y_init, 1)
                    g.iota(y_trash, [[0, 1]], base=NP, channel_multiplier=1,
                           allow_small_or_imprecise_dtypes=True).then_inc(y_init, 1)
                    g.memset(acc[:, :, :], 0.0).then_inc(y_init, 1)
                    with g.Fori(0, SV * SUP) as t:
                        g.wait_ge(y_load, t * (16 * nload) + 16 * nload)
                        g.sem_inc(turn, 1)

                        def gather_rows(to, tab, idx):
                            g.indirect_dma_start(to, None, tab[:, :], bass.IndirectOffsetOnAxis(ap=idx, axis=0)).then_inc(y_gath, 16)
                        gather_rows(y_ga, table, y_is)
                        if messages:
                            gather_rows(y_gb, b_tab, y_id)
                        gather_rows(y_gs, s_tab, y_id)
                        g.wait_ge(y_v, t * VSTEPS + VSTEPS)
                        g.sem_inc(turn, 1)
                        g.indirect_dma_start(s_tab[:, :], bass.IndirectOffsetOnAxis(ap=y_iw, axis=0), y_gs, None).then_inc(y_scat, 16)

                @block.vector
                def _(dve):
                    if not messages:
                        second_layer_residual(dve)
                    dve.wait_ge(y_init, ninit)
                    with dve.Fori(0, SV * SUP) as t:
                        n = [0]

                        def link(ins):
                            n[0] += 1
                            ins.then_inc(y_v, 1)
                            dve.wait_ge(y_v, t * VSTEPS + n[0])
                        dve.wait_ge(y_load, t * (16 * nload) + 16 * nload)
                        link(dve.tensor_copy(y_dst, y_id))
                        link(dve.tensor_scalar(y_eq, y_drow, y_dst, None, ALU.is_equal))
                        link(dve.tensor_tensor(y_both, y_eq, y_low, ALU.mult))
                        link(dve.tensor_reduce(y_rank, y_both, AX, ALU.max))
                        link(dve.tensor_tensor(y_w, y_trash, y_dst, ALU.subtract))
                        link(dve.tensor_tensor(y_w, y_w, y_rank, ALU.mult))
                        link(dve.tensor_tensor(y_iw, y_w, y_dst, ALU.add))
                        dve.wait_ge(y_gath, t * (16 * ngath) + 16 * ngath)
                        if messages:
                            dve.wait_ge(y_pe, t * PSTEPS + 2)
                            link(dve.tensor_tensor(pre[:, 0, 0, :], bank[1][:, 0:C], y_ga, ALU.add))
                            link(dve.tensor_tensor(pre[:, 0, 0, :], pre[:, 0, 0, :], y_gb, ALU.add))
                            link(dve.tensor_tensor(pre[:, 0, 0, :], pre[:, 0, 0, :], cstb[:, :], ALU.add))
                            dve.wait_ge(y_act, t * ASTEPS + 3)
                            link(dve.tensor_tensor(acc[:, 0, :], acc[:, 0, :], sq[:, 0, 0, :], ALU.add))
                        else:
                            link(dve.tensor_copy(y_msg[:, 0:C], y_ga))
                        dve.wait_ge(y_pe, t * PSTEPS + PSTEPS)
                        link(dve.tensor_tensor(y_gs, bank[2][:, 0:C + 1], y_gs, ALU.add))

                @block.tensor
                def _(pe):
                    with pe.Fori(0, SV * SUP) as t:
                        if messages:
                            pe.wait_ge(y_load, t * (16 * nload) + 16 * nload)
                            pe.matmul(bank[0][0:C, 0:TILE], w36[:, :], rk[:, 0, 0, 0:TILE], start=True, stop=True).then_inc(y_pe, 1)
                            pe.wait_ge(y_act, t * ASTEPS + 1)
                            pe.matmul(bank[1][:, 0:C], lhs[0:C, 0, 0:TILE], rhs[0:C, 0, :], start=True, stop=True).then_inc(y_pe, 1)
                            pe.wait_ge(y_act, t * ASTEPS + 2)
                        else:
                            pe.wait_ge(y_v, t * VSTEPS + 8)
                        pe.matmul(bank[2][:, 0:C + 1], y_eq, y_msg, start=True, stop=True).then_inc(y_pe, 1)
                    with pe.Fori(0, NT) as t:
                        pe.wait_ge(z_load, t * 16 + 16)
                        pe.transpose(bank[0][0:C + 1, 0:P], y_gs, ident[:, :]).then_inc(z_tr, 1)

                @block.scalar
                def _(act):
                    if messages:
                        with act.Fori(0, SV * SUP) as t:
                            act.wait_ge(y_pe, t * PSTEPS + 1)
                            act.activation(lhs[0:C, 0, 0:TILE], bank[0][0:C, 0:TILE], ACT.Relu,
                                           bias=par[:, B_EDGE:B_EDGE + 1]).then_inc(y_act, 1)
                            act.wait_ge(y_v, t * VSTEPS + 10)
                            act.activation(y_msg[:, 0:C], pre[:, 0, 0, :], ACT.Relu).then_inc(y_act, 1)
                            act.wait_ge(y_act, t * ASTEPS + 2)
                            act.activation(sq[:, 0, 0, :], y_msg[:, 0:C], ACT.Square).then_inc(y_act, 1)
                    rows = C + 1 if messages else C
                    with act.Fori(0, NT) as t:
                        act.wait_ge(z_tr, t + 1)
                        act.activation(sT[0:rows, bass.ds(t * P, P)], bank[0][0:rows, 0:P], ACT.Copy).then_inc(z_copy, 1)

        windowed = nc.values_load(flag_i[:, :], min_val=0, max_val=1)
        m0 = sem("m0")
        with nc.If(windowed):
            with nc.Block() as block:
                @block.gpsimd
                def _(g):
                    def step(i, k):
                        gather(g, i, k)
                    msgs.run(g, step, 0)

                @block.sync
                def _(sp):
                    def step(i, k):
                        load_pair(sp, i, k)
                        load_window(sp, i, k)
                        load_spilled(sp, i, k)
                    msgs.run(sp, step, 0)

                @block.tensor
                def _(pe):
                    for x in (r_mm, m_mm, s_mm):
                        x.start(pe)
                    def step(i, k):
                        edge_product(pe, i, k)
                        message_product(pe, *msgs.earlier(i, k, 1))
                        sum_edges(pe, *msgs.earlier(i, k, 2))
                    msgs.run(pe, step, 2)

                @block.scalar
                def _(act):
                    for x in (r_ok, m_ok, m_sq):
                        x.start(act)
                    def step(i, k):
                        copy_indices(act, i, k)
                        edge_relu(act, *msgs.earlier(i, k, 2))
                        message_relu(act, *msgs.earlier(i, k, 3))
                        square(act, *msgs.earlier(i, k, 3))
                    msgs.run(act, step, 3)

                @block.vector
                def _(dve):
                    dve.memset(sT[:, 0:NP], 0.0).then_inc(m0, 1)
                    dve.memset(acc[:, :, :], 0.0).then_inc(m0, 1)
                    dve.wait_ge(m0, 2)
                    for x in (ohT_ok, w_ok, m_pre, m_acc, s_add):
                        x.start(dve)
                    def step(i, k):
                        onehot_T(dve, i, k)
                        window_rows(dve, i, k)
                        onehot(dve, i, k)
                        add_gathered(dve, *msgs.earlier(i, k, 1))
                        accumulate(dve, *msgs.earlier(i, k, 2))
                        add_window(dve, *msgs.earlier(i, k, 2))
                    msgs.run(dve, step, 2)
        with nc.Else():
            general_pass("_m", True)

        h2_all = nf[:, 0:NT * C].rearrange("p (t c) -> p t c", c=C)
        v1_sb = gbuf[0:C + 1, :, :, :].rearrange("p k t c -> p (k t c)")[:, 0:2 * CH].rearrange("p (b n) -> p b n", b=2)
        t2_sb = pre
        tm_l = trep[0:C, 0:C + 1]
        mix = cstb[0:C + 1, :]
        m_row = bank[6][0:C + 1, 0:C]
        PADS = SV * ES - E
        l_x2 = sem("l_x2")
        q_mm = sem("q_mm")
        q_v = sem("q_v")
        q_std = sem("q_std")
        q_row = sem("q_row")
        q_lhs = sem("q_lhs")
        layer = Turns(NCH, 2)
        p_v1 = signal("p_v1", 0)
        p_v = signal("p_v", 0)
        p_mm = signal("p_mm", 2)
        p_x1 = signal("p_x1", 2)
        p_deg = signal("p_deg", 2)
        p_mean = sem("p_mean")
        p_c = signal("p_c", 0)
        p_sq = signal("p_sq", 0)
        p_var = signal("p_var", 2)
        p_std = signal("p_std", 0)
        p_rec = signal("p_rec", 0)
        p_h2 = signal("p_h2", 0)
        p_t2 = signal("p_t2", 0)
        p_out = signal("p_out", 2)
        o_t = [sem("o_t0"), sem("o_t1")]
        o_zero = sem("o_zero")
        l_w5 = sem("l_w5")
        wc_mm = sem("wc_mm")
        t_rows = t_tab.rearrange("(c k p) f -> c p k f", k=CT, p=P)

        def cols(c):
            return bass.ds(c * CT, CT)

        def layer_v1(act, i, k):
            if layer.absent(i, k):
                return
            c = 2 * i + k
            if not (isinstance(c, int) and c < 2):
                act.wait_ge(p_v.sem, p_v.at(c - 2))
            act.activation(v1_sb[0:C, k, :], nf[0:C, bass.ds(c * CH, CH)], ACT.Identity,
                           bias=aff[:, T_N:T_N + 1], scale=aff[:, S_N:S_N + 1]).then_inc(p_v1.sem, 1)

        def layer_v(dve, i, k):
            if layer.absent(i, k):
                return
            c = 2 * i + k
            dve.wait_ge(p_v1.sem, p_v1.at(c))
            dve.wait_ge(p_mm.sem, p_mm.at(c - 2))
            dve.scalar_tensor_tensor(lhs[0:C + 1, k, :], sT[0:C + 1, bass.ds(c * CH, CH)], smc[:, :], v1_sb[:, k, :],
                                     ALU.mult, ALU.add).then_inc(p_v.sem, 1)

        def layer_product(pe, i, k):
            if layer.absent(i, k):
                return
            c = 2 * i + k
            pe.wait_ge(p_v.sem, p_v.at(c))
            pe.wait_ge(p_x1.sem, p_x1.at(c - 2))
            pe.wait_ge(p_deg.sem, p_deg.at(c - 2))
            for t in range(CT):
                v_t = lhs[0:C + 1, k, t * P:(t + 1) * P]
                pe.matmul(ps_chunk(k)[:, t, :], v_t, mix[:, :], start=True, stop=True)
                ins = pe.matmul(bank[2 + k][:, t:t + 1], v_t, ident[0:C + 1, C:C + 1], start=True, stop=True)
            ins.then_inc(p_mm.sem, 1)

        def layer_mean(dve, i, k):
            if layer.absent(i, k):
                return
            c = 2 * i + k
            xs = x_all[:, cols(c), :]
            dve.wait_ge(p_mm.sem, p_mm.at(c))
            dve.tensor_tensor(xs, xs, ps_chunk(k), ALU.add).then_inc(p_x1.sem, 1)
            dve.wait_ge(p_x1.sem, p_x1.at(c))
            dve.tensor_reduce(mean[:, cols(c)], xs, AX, ALU.add).then_inc(p_mean, 1)
            dve.wait_ge(p_mean, c * 2 + 1)
            dve.tensor_scalar(mean[:, cols(c)], mean[:, cols(c)], 1.0 / C, None, ALU.mult).then_inc(p_mean, 1)

        def layer_degree(act, i, k):
            if layer.absent(i, k):
                return
            c = 2 * i + k
            act.wait_ge(p_mm.sem, p_mm.at(c))
            act.activation(sdeg[:, cols(c)], bank[2 + k][:, 0:CT], ACT.Sqrt, bias=ones[:, 0:1]).then_inc(p_deg.sem, 1)
            act.activation(sT[:, bass.ds(c * CH, CH)].rearrange("p (k n) -> p k n", k=CT),
                           ones[:, :].unsqueeze(1).to_broadcast([P, CT, P]), ACT.Copy, scale=0.0)

        def layer_centre(g, i, k):
            if layer.absent(i, k):
                return
            c = 2 * i + k
            g.wait_ge(p_mean, c * 2 + 2)
            g.tensor_tensor(h2_all[:, cols(c), :], x_all[:, cols(c), :],
                            mean[:, cols(c)].unsqueeze(2).to_broadcast([P, CT, C]), ALU.subtract).then_inc(p_c.sem, 1)

        def layer_square(act, i, k):
            if layer.absent(i, k):
                return
            c = 2 * i + k
            act.wait_ge(p_c.sem, p_c.at(c))
            act.wait_ge(p_var.sem, p_var.at(c - 2))
            act.activation(sq[:, k, :, :], h2_all[:, cols(c), :], ACT.Square).then_inc(p_sq.sem, 1)

        def layer_variance(dve, i, k):
            if layer.absent(i, k):
                return
            c = 2 * i + k
            dve.wait_ge(p_sq.sem, p_sq.at(c))
            dve.tensor_reduce(rstd[:, cols(c)], sq[:, k, :, :], AX, ALU.add).then_inc(p_var.sem, 1)

        def layer_std(act, i, k):
            if layer.absent(i, k):
                return
            c = 2 * i + k
            act.wait_ge(p_var.sem, p_var.at(c))
            act.activation(rstd[:, cols(c)], rstd[:, cols(c)], ACT.Sqrt, bias=eps[:, :], scale=1.0 / C).then_inc(p_std.sem, 1)

        def layer_h2(dve, i, k):
            if layer.absent(i, k):
                return
            c = 2 * i + k
            dve.wait_ge(p_deg.sem, p_deg.at(c))
            dve.wait_ge(p_std.sem, p_std.at(c))
            dve.sem_inc(turn, 1)
            dve.reciprocal(dinv[:, cols(c)], sdeg[:, cols(c)])
            dve.reciprocal(rstd[:, cols(c)], rstd[:, cols(c)]).then_inc(p_rec.sem, 1)
            dve.wait_ge(p_rec.sem, p_rec.at(c))
            dve.scalar_tensor_tensor(h2_all[:, cols(c), :], h2_all[:, cols(c), :], 0.0,
                                     rstd[:, cols(c)].unsqueeze(2).to_broadcast([P, CT, C]),
                                     ALU.max, ALU.mult).then_inc(p_h2.sem, 1)

        def scaled_h2(g, c, to):
            return g.tensor_tensor(to, h2_all[:, cols(c), :],
                                   dinv[:, cols(c)].unsqueeze(2).to_broadcast([P, CT, C]), ALU.mult)

        def layer_rows(g, i, k):
            if layer.absent(i, k):
                return
            c = 2 * i + k
            g.wait_ge(p_h2.sem, p_h2.at(c))
            g.wait_ge(p_out.sem, p_out.at(c - 2))
            scaled_h2(g, c, t2_sb[:, k, :, :]).then_inc(p_t2.sem, 1)

        def layer_store(sp, i, k):
            if layer.absent(i, k):
                return
            c = 2 * i + k
            sp.wait_ge(p_t2.sem, p_t2.at(c))
            sp.sem_inc(turn, 1)
            sp.dma_start(t_rows[c], t2_sb[:, k, :, :]).then_inc(o_t[k], 16)

        def layer_stored(sp, i, k):
            if layer.absent(i, k):
                return
            sp.wait_ge(o_t[k], i * 16 + 16)
            sp.sem_inc(p_out.sem, 1)

        def second_layer_residual(dve):
            dve.tensor_tensor(x_all[:, :, :], x_all[:, :, :], h2_all, ALU.add)

        with nc.Block() as block:
            @block.sync
            def _(sp):
                sp.dma_start(x_all[:, :, :], a["x"]).then_inc(l_x2, 16)
                p_out.start(sp)

                def step(i, k):
                    layer_store(sp, i, k)
                    layer_stored(sp, *layer.earlier(i, k, 1))
                layer.run(sp, step, 1)
                sp.dma_start(t_tab[N:N + 1, :], zrow[:, :]).then_inc(o_zero, 16)
                sp.wait_ge(o_zero, 16)

            @block.vector
            def _(dve):
                n = [0]

                def link(ins):
                    n[0] += 1
                    ins.then_inc(q_v, 1)
                    dve.wait_ge(q_v, n[0])

                def col(c):
                    return aff[:, c:c + 1]
                link(dve.tensor_reduce(col(TMP0), sT[0:C, 0:N], AX, ALU.add))
                link(dve.tensor_scalar(col(TMP0), col(TMP0), 1.0 / E, None, ALU.mult))
                link(dve.tensor_tensor(col(TMP1), col(TMP0), col(TMP0), ALU.mult))
                dve.wait_ge(q_mm, 1)
                link(dve.scalar_tensor_tensor(col(TMP2), bank[7][0:C, 0:1], 1.0 / E, col(TMP1), ALU.mult, ALU.subtract))
                dve.tensor_scalar(col(TMP2), col(TMP2), 0.0, None, ALU.max).then_inc(q_row, 1)
                dve.wait_ge(q_std, 1)
                link(dve.reciprocal(col(TMP1), col(TMP3)))
                link(dve.memset(smc[:, :], 1.0))
                link(dve.tensor_tensor(smc[0:C, :], col(TMP1), par[:, G_MSG:G_MSG + 1], ALU.mult))
                link(dve.tensor_tensor(col(TMP2), col(TMP0), smc[0:C, :], ALU.mult))
                link(dve.memset(tm_l, 0.0))
                dve.tensor_tensor(tm_l[:, C:C + 1], par[:, T_MSG:T_MSG + 1], col(TMP2), ALU.subtract).then_inc(q_lhs, 1)
                link(dve.tensor_copy(mix[:, :], ident[0:C + 1, 0:C]))
                dve.wait_ge(q_lhs, 2)
                link(dve.tensor_copy(mix[C:C + 1, :], m_row[C:C + 1, :]))
                last = sT[C:C + 1, N - 1:N]
                link(dve.tensor_scalar(last, last, -float(PADS), None, ALU.add))
                dve.memset(v1_sb[C:C + 1, :, :], 0.0).then_inc(q_lhs, 1)
                dve.wait_ge(q_lhs, 3)
                dve.wait_ge(l_x2, 16)
                for x in (p_x1, p_var):
                    x.start(dve)

                def step(i, k):
                    layer_v(dve, i, k)
                    layer_mean(dve, *layer.earlier(i, k, 1))
                    layer_variance(dve, *layer.earlier(i, k, 2))
                    layer_h2(dve, *layer.earlier(i, k, 3))
                layer.run(dve, step, 3)

            @block.tensor
            def _(pe):
                for t in range(SUP):
                    ins = pe.matmul(bank[7][0:C, 0:1], acc[:, t, :], ones[:, 0:1], start=(t == 0), stop=(t == SUP - 1))
                ins.then_inc(q_mm, 1)
                pe.wait_ge(q_lhs, 1)
                pe.matmul(m_row, tm_l, ident[0:C, 0:C], start=True, stop=True).then_inc(q_lhs, 1)
                pe.wait_ge(l_w5, 16 * 5)
                for j in range(3):
                    ins = pe.matmul(bank[5][0:C, 0:H], wgT[:, j, :], w1[:, j, :], start=(j == 0), stop=(j == 2))
                ins.then_inc(wc_mm, 1)
                p_mm.start(pe)

                def step(i, k):
                    layer_product(pe, i, k)
                layer.run(pe, step, 0)

            @block.scalar
            def _(act):
                act.wait_ge(q_row, 1)
                act.activation(aff[:, TMP3:TMP3 + 1], aff[:, TMP2:TMP2 + 1], ACT.Sqrt, bias=eps[0:C, :]).then_inc(q_std, 1)
                act.wait_ge(wc_mm, 1)
                act.activation(wc[0:C, 0:H], bank[5][0:C, 0:H], ACT.Copy)
                act.activation(wc[:, H:H + 1], ident[0:C + 1, C:C + 1], ACT.Copy)
                p_deg.start(act)

                def step(i, k):
                    layer_v1(act, i, k)
                    layer_degree(act, *layer.earlier(i, k, 1))
                    layer_std(act, *layer.earlier(i, k, 2))
                    layer_square(act, *layer.earlier(i, k, 1))
                layer.run(act, step, 2)

            @block.gpsimd
            def _(g):
                g.dma_start(wgT[:, :, :], a["W_gcn_T"].rearrange("(j p) c -> p j c", p=C)).then_inc(l_w5, 16)
                g.dma_start(w1[:, :, :], a["W1"].rearrange("(j p) h -> p j h", p=C)).then_inc(l_w5, 16)
                g.dma_start(w2[0:H, :], a["W2"]).then_inc(l_w5, 16)
                g.dma_start(w2[H:H + 1, :], a["b2"]).then_inc(l_w5, 16)
                g.dma_start(wc[C:C + 1, 0:H], a["b1"]).then_inc(l_w5, 16)
                g.wait_ge(l_w5, 16 * 5)

                def step(i, k):
                    layer_centre(g, i, k)
                    layer_rows(g, *layer.earlier(i, k, 2))
                layer.run(g, step, 2)

        sums = Turns(SV, 4)
        c_land = [sem(f"c_land{k}") for k in range(4)]
        c_idx = signal("c_idx", 0)
        c_oh = signal("c_oh", 0)
        c_mm = signal("c_mm", 4)
        c_add = signal("c_add", 2)

        def gcn_indices(act, i, k):
            if sums.absent(i, k):
                return
            act.wait_ge(c_mm.sem, c_mm.at(4 * i + k - 4))
            act.activation(idxb[:, k, :], src_i[:, bass.ds(16 * i + 4 * k, SUP)], ACT.Copy).then_inc(c_idx.sem, 1)

        def gcn_gather(g, i, k):
            if sums.absent(i, k):
                return
            g.wait_ge(c_idx.sem, c_idx.at(4 * i + k))
            g.wait_ge(c_mm.sem, c_mm.at(4 * i + k - 4))
            g.sem_inc(turn, 1)
            for t in range(SUP):
                g.indirect_dma_start(gbuf[:, k, t, :], None, t_tab[:, :],
                                     bass.IndirectOffsetOnAxis(ap=idxb[:, k, t:t + 1], axis=0)).then_inc(c_land[k], 16)

        def gcn_onehot(dve, i, k):
            if sums.absent(i, k):
                return
            dve.wait_ge(c_mm.sem, c_mm.at(4 * i + k - 4))
            dve.tensor_tensor(oh[:, k, :, :], iota_w[:, :].unsqueeze(1).to_broadcast([P, SUP, W]),
                              dstrel[:, bass.ds(4 * i + k, 1), :].rearrange("p s t -> p (s t)").unsqueeze(2).to_broadcast([P, SUP, W]),
                              ALU.is_equal).then_inc(c_oh.sem, 1)

        def gcn_sum(pe, i, k):
            if sums.absent(i, k):
                return
            pe.wait_ge(c_land[k], i * (16 * SUP) + 16 * SUP)
            pe.wait_ge(c_oh.sem, c_oh.at(4 * i + k))
            pe.wait_ge(c_add.sem, c_add.at(4 * i + k - 2))
            for t in range(SUP):
                ins = pe.matmul(ps_s(k)[0:C, :], gbuf[:, k, t, :], oh[:, k, t, :], start=(t == 0), stop=(t == SUP - 1))
            ins.then_inc(c_mm.sem, 1)

        def gcn_add(dve, i, k):
            if sums.absent(i, k):
                return
            base = dve.value_load(base_i[:, bass.ds(4 * i + k, 1)], min_val=0, max_val=N - 1)
            dve.wait_ge(c_mm.sem, c_mm.at(4 * i + k))
            dve.wait_ge(c_add.sem, c_add.at(4 * i + k - 1))
            cols = sT[0:C, bass.ds(base, W)]
            dve.tensor_tensor(cols, cols, ps_s(k)[0:C, :], ALU.add).then_inc(c_add.sem, 1)

        with nc.If(windowed):
            with nc.Block() as block:
                @block.gpsimd
                def _(g):
                    def step(i, k):
                        gcn_gather(g, i, k)
                    sums.run(g, step, 0)

                @block.scalar
                def _(act):
                    def step(i, k):
                        gcn_indices(act, i, k)
                    sums.run(act, step, 0)

                @block.tensor
                def _(pe):
                    c_mm.start(pe)
                    def step(i, k):
                        gcn_sum(pe, i, k)
                    sums.run(pe, step, 0)

                @block.vector
                def _(dve):
                    second_layer_residual(dve)
                    c_add.start(dve)

                    def step(i, k):
                        gcn_onehot(dve, i, k)
                        gcn_add(dve, *sums.earlier(i, k, 1))
                    sums.run(dve, step, 1)
        with nc.Else():
            general_pass("_g", False)

        u_rows = msg
        z_sb = gbuf[0:H + 1, :, :, :].rearrange("p k t c -> p (k t c)")[:, 0:2 * CH].rearrange("p (b n) -> p b n", b=2)
        o_sb = sq
        final = Turns(NCH, 2)
        f_t2 = signal("f_t2", 0)
        f_tr = signal("f_tr", 2)
        f_u = signal("f_u", 2)
        f_z = signal("f_z", 2)
        f_zr = signal("f_zr", 2)
        f_o = signal("f_o", 2)
        f_out = signal("f_out", 2)
        f_st = signal("f_st", 2)
        o_out = [sem("o_out0"), sem("o_out1")]

        def final_rows(g, i, k):
            if final.absent(i, k):
                return
            c = 2 * i + k
            g.wait_ge(f_tr.sem, f_tr.at(c - 2))
            scaled_h2(g, c, u_rows[:, k, :, 0:C])
            g.tensor_copy(u_rows[:, k, :, C:C + 1], sdeg[:, cols(c)].unsqueeze(2)).then_inc(f_t2.sem, 1)

        def final_transpose(pe, i, k):
            if final.absent(i, k):
                return
            c = 2 * i + k
            pe.wait_ge(f_t2.sem, f_t2.at(c))
            pe.wait_ge(f_u.sem, f_u.at(c - 2))
            for t in range(CT):
                ins = pe.transpose(bank[k][0:C + 1, t * P:(t + 1) * P], u_rows[:, k, t, :], ident[:, :])
            ins.then_inc(f_tr.sem, 1)

        def final_sums(dve, i, k):
            if final.absent(i, k):
                return
            c = 2 * i + k
            dve.wait_ge(f_tr.sem, f_tr.at(c))
            dve.wait_ge(f_z.sem, f_z.at(c - 2))
            dve.tensor_tensor(lhs[0:C + 1, k, :], bank[k][0:C + 1, :], sT[0:C + 1, bass.ds(c * CH, CH)],
                              ALU.add).then_inc(f_u.sem, 1)

        def final_hidden(pe, i, k):
            if final.absent(i, k):
                return
            c = 2 * i + k
            pe.wait_ge(f_u.sem, f_u.at(c))
            pe.wait_ge(f_zr.sem, f_zr.at(c - 2))
            pe.matmul(bank[2 + k][0:H + 1, :], wc[:, :], lhs[0:C + 1, k, :], start=True, stop=True).then_inc(f_z.sem, 1)

        def final_relu(act, i, k):
            if final.absent(i, k):
                return
            c = 2 * i + k
            act.wait_ge(f_z.sem, f_z.at(c))
            act.wait_ge(f_o.sem, f_o.at(c - 2))
            act.activation(z_sb[:, k, :], bank[2 + k][0:H + 1, :], ACT.Relu).then_inc(f_zr.sem, 1)

        def final_product(pe, i, k):
            if final.absent(i, k):
                return
            c = 2 * i + k
            pe.wait_ge(f_zr.sem, f_zr.at(c))
            pe.wait_ge(f_out.sem, f_out.at(c - 2))
            for t in range(CT):
                ins = pe.matmul(ps_chunk(4 + k)[:, t, :], z_sb[:, k, t * P:(t + 1) * P], w2[:, :], start=True, stop=True)
            ins.then_inc(f_o.sem, 1)

        def final_output(dve, i, k):
            if final.absent(i, k):
                return
            c = 2 * i + k
            dve.wait_ge(f_o.sem, f_o.at(c))
            dve.wait_ge(f_st.sem, f_st.at(c - 2))
            for t in range(CT):
                ins = dve.scalar_tensor_tensor(o_sb[:, k, t, :], ps_chunk(4 + k)[:, t, :], dinv[:, bass.ds(c * CT + t, 1)],
                                               x_all[:, bass.ds(c * CT + t, 1), :].rearrange("p t c -> p (t c)"),
                                               ALU.mult, ALU.add)
            ins.then_inc(f_out.sem, 1)

        def final_store(sp, i, k):
            if final.absent(i, k):
                return
            c = 2 * i + k
            sp.wait_ge(f_out.sem, f_out.at(c))
            sp.sem_inc(turn, 1)
            sp.dma_start(out[:, cols(c), :], o_sb[:, k, :, :]).then_inc(o_out[k], 16)

        def final_stored(sp, i, k):
            if final.absent(i, k):
                return
            sp.wait_ge(o_out[k], i * 16 + 16)
            sp.sem_inc(f_st.sem, 1)

        with nc.Block() as block:
            @block.gpsimd
            def _(g):
                def step(i, k):
                    final_rows(g, i, k)
                final.run(g, step, 0)

            @block.tensor
            def _(pe):
                for x in (f_tr, f_z, f_o):
                    x.start(pe)

                def step(i, k):
                    final_transpose(pe, i, k)
                    final_hidden(pe, *final.earlier(i, k, 1))
                    final_product(pe, *final.earlier(i, k, 2))
                final.run(pe, step, 2)

            @block.scalar
            def _(act):
                f_zr.start(act)

                def step(i, k):
                    final_relu(act, i, k)
                final.run(act, step, 0)

            @block.vector
            def _(dve):
                for x in (f_u, f_out):
                    x.start(dve)

                def step(i, k):
                    final_sums(dve, i, k)
                    final_output(dve, *final.earlier(i, k, 2))
                final.run(dve, step, 2)

            @block.sync
            def _(sp):
                f_st.start(sp)

                def step(i, k):
                    final_store(sp, i, k)
                    final_stored(sp, *final.earlier(i, k, 1))
                final.run(sp, step, 1)


def lay_out(inputs):
    import numpy as np
    x = np.asarray(inputs["x"])
    src, dst = np.asarray(inputs["src"]), np.asarray(inputs["dst"])
    attr = np.asarray(inputs["edge_attr_4"])
    n, e = x.shape[0], src.shape[0]
    d = Dims(n, e)

    def nodes(v):
        pad = np.zeros((d.NP, v.shape[1]), v.dtype)
        pad[:n] = v
        return np.ascontiguousarray(pad.reshape(d.NT, P, -1).transpose(1, 0, 2))

    def edges(v, fill):
        pad = np.full(d.EP, fill, v.dtype)
        pad[:e] = v
        return pad

    attr_t = np.zeros((KE, d.EP), attr.dtype)
    attr_t[:, :e] = attr.T
    dst_p = edges(dst, n - 1)
    arrays = {
        "x": nodes(x),
        "src": np.ascontiguousarray(edges(src, n).reshape(d.T, P).T),
        "dst": np.ascontiguousarray(dst_p.reshape(d.T, P).T),
        "dst_row": dst_p.reshape(1, d.EP),
        "attr": attr_t,
    }
    for name, v in inputs.items():
        if name[:3] in ("L0_", "L1_"):
            v = np.asarray(v)
            arrays[name[7:]] = np.ascontiguousarray(v if v.ndim == 2 else v.reshape(1, -1))
    arrays["W_gcn_T"] = np.ascontiguousarray(arrays.pop("W_gcn").T)
    return d, arrays


def build(nc, d, arrays):
    a = {k: nc.dram_tensor(k, v.shape, mybir.dt.from_np(v.dtype), kind="ExternalInput").ap() for k, v in arrays.items()}
    out = nc.dram_tensor("out_0_dram", (P, d.NT, C), FP32, kind="ExternalOutput").ap()
    gnn_kernel(nc, d, a, out)


def unpack(o, n):
    import numpy as np
    return np.ascontiguousarray(np.asarray(o).transpose(1, 0, 2).reshape(-1, C)[:n])


def kernel(**inputs):
    import concourse.bacc as bacc
    from concourse.bass_utils import run_bass_kernel_spmd
    d, arrays = lay_out(inputs)
    nc = bacc.Bacc("TRN2", target_bir_lowering=False, num_devices=1)
    build(nc, d, arrays)
    r = run_bass_kernel_spmd(nc, [arrays], core_ids=[0])
    return unpack(r.results[0]["out_0_dram"], d.N)
```
